# Optimizing a Trainium2 kernel written in Bass

```python
import numpy as np
import jax
import jax.numpy as jnp

def _softmax(x, axis=-1):
    return jax.nn.softmax(x, axis=axis)

def _gelu(x):
    return jax.nn.gelu(x, approximate=True)

def _silu(x):
    return jax.nn.silu(x)

def _sigmoid(x):
    return jax.nn.sigmoid(x)

def _layernorm(x, axis=-1, eps=1e-05):
    m = jnp.mean(x, axis=axis, keepdims=True)
    v = jnp.var(x, axis=axis, keepdims=True)
    return (x - m) / jnp.sqrt(v + eps)

def _scatter_add(tgt, idx, src, axis=0):
    return tgt.at[idx].add(src)

def _segment_sum(src, seg, n):
    return jax.ops.segment_sum(src, seg, n)
kernel_name = 'mk_adaln_d1_jaxref_r8_1e1e9a'

def setup_inputs(seed: int=0):
    np.random.seed(seed)
    _w = jnp.asarray

    def _L0_attn_setup():
        import jax, jax.numpy as jnp
        import numpy as np
        NUM_HEADS = 16

        def _heads(t, B, N, H, hd):
            return t.reshape(B, N, H, hd).transpose(0, 2, 1, 3)
        key = jax.random.key(seed)
        ks = jax.random.split(key, 9)
        B, N, D = (2, 256, 128)
        w = 0.02
        return {'x': jax.random.normal(ks[0], (B, N, D), dtype=jnp.float32), 'wq': jax.random.normal(ks[1], (D, D), dtype=jnp.float32) * w, 'bq': jax.random.normal(ks[2], (D,), dtype=jnp.float32) * w, 'wk': jax.random.normal(ks[3], (D, D), dtype=jnp.float32) * w, 'bk': jax.random.normal(ks[4], (D,), dtype=jnp.float32) * w, 'wv': jax.random.normal(ks[5], (D, D), dtype=jnp.float32) * w, 'bv': jax.random.normal(ks[6], (D,), dtype=jnp.float32) * w, 'wo': jax.random.normal(ks[7], (D, D), dtype=jnp.float32) * w, 'bo': jax.random.normal(ks[8], (D,), dtype=jnp.float32) * w}
    _L0_attn_in = _L0_attn_setup()

    def _L0_ffn_setup():
        import jax, jax.numpy as jnp
        import numpy as np
        DIM = 128
        DEPTH = 6
        HEADS = 16
        DIM_HEAD = 64
        WINDOW = 32
        INNER = HEADS * DIM_HEAD
        DIM_INNER = int(DIM * 4 * 2 / 3)
        QK_SCALE = 8.0

        def shift_tokens(t):
            a, s = jnp.split(t, 2, -1)
            s = jnp.pad(s, ((0, 0), (1, 0), (0, 0)))[:, :-1]
            return jnp.concatenate([a, s], -1)

        def l2norm(t):
            return t / jnp.maximum(jnp.linalg.norm(t, axis=-1, keepdims=True), 1e-12)

        def rotate_half(x):
            x1, x2 = jnp.split(x, 2, -1)
            return jnp.concatenate([-x2, x1], -1)

        def rotary_tables(n):
            half = jnp.arange(0, DIM_HEAD, 2, dtype=jnp.float32)
            inv_freq = 1.0 / 10000.0 ** (half / DIM_HEAD)
            t = jnp.arange(n, dtype=jnp.float32)
            freqs = t[:, None] * inv_freq[None, :]
            freqs = jnp.concatenate([freqs, freqs], -1)
            base_scale = (half + 0.4 * DIM_HEAD) / (1.4 * DIM_HEAD)
            power = (t - n // 2) / (WINDOW // 2)
            scale = base_scale[None, :] ** power[:, None]
            scale = jnp.concatenate([scale, scale], -1)
            return (freqs, scale)

        def local_attention(q, k, v):
            b, h, n, d = q.shape
            w = WINDOW
            nw = n // w
            bq = q.reshape(b, h, nw, w, d)
            bk = k.reshape(b, h, nw, w, d)
            bv = v.reshape(b, h, nw, w, d)

            def look(t):
                p = jnp.pad(t, ((0, 0), (0, 0), (1, 0), (0, 0), (0, 0)))
                return jnp.concatenate([p[:, :, :nw], p[:, :, 1:]], axis=3)
            bk2, bv2 = (look(bk), look(bv))
            seq = jnp.arange(n).reshape(nw, w)
            seq_p = jnp.pad(seq, ((1, 0), (0, 0)), constant_values=-1)
            jt = jnp.concatenate([seq_p[:nw], seq_p[1:]], axis=1)
            it = seq[:, :, None]
            jb = jt[:, None, :]
            mask = (it < jb) | (it > jb + w) | (jb == -1)
            sim = jnp.einsum('bhwie,bhwje->bhwij', bq, bk2) * QK_SCALE
            sim = jnp.where(mask, -jnp.finfo(sim.dtype).max, sim)
            attn = jax.nn.softmax(sim, -1)
            out = jnp.einsum('bhwij,bhwje->bhwie', attn, bv2)
            return out.reshape(b, h, n, d)

        def attn_layer(x, Wqkv, qs, ksc, Wo):
            b, n, _ = x.shape
            qkv = x @ Wqkv
            q, k, v = jnp.split(qkv, 3, -1)
            sh = lambda t: t.reshape(b, n, HEADS, DIM_HEAD).transpose(0, 2, 1, 3)
            q, k, v = (sh(q), sh(k), sh(v))
            q = l2norm(q) * qs
            k = l2norm(k) * ksc
            freqs, scale = rotary_tables(n)
            cos, sin = (jnp.cos(freqs), jnp.sin(freqs))
            q = q * cos * scale + rotate_half(q) * sin * scale
            inv = 1.0 / scale
            k = k * cos * inv + rotate_half(k) * sin * inv
            out = local_attention(q, k, v)
            out = out.transpose(0, 2, 1, 3).reshape(b, n, INNER)
            return out @ Wo

        def ffn_layer(x, g, bln, W1, b1, W2, b2):
            mu = x.mean(-1, keepdims=True)
            var = ((x - mu) ** 2).mean(-1, keepdims=True)
            xn = (x - mu) / jnp.sqrt(var + 1e-05) * g + bln
            hg = xn @ W1 + b1
            a, gate = jnp.split(hg, 2, -1)
            return a * jax.nn.gelu(gate, approximate=False) @ W2 + b2
        key = jax.random.key(seed)
        ks = jax.random.split(key, 8)
        B, N = (2, 256)
        init = lambda k, shape: jax.random.normal(k, shape, jnp.float32) * 0.02
        return {'x': jax.random.normal(ks[0], (B, N, DIM), jnp.float32), 'Wqkv': init(ks[1], (DEPTH, DIM, 3 * INNER)), 'q_scale': jnp.ones((DEPTH, DIM_HEAD), jnp.float32), 'k_scale': jnp.ones((DEPTH, DIM_HEAD), jnp.float32), 'Wo': init(ks[2], (DEPTH, INNER, DIM)), 'ln_g': jnp.ones((DEPTH, DIM), jnp.float32), 'ln_b': jnp.zeros((DEPTH, DIM), jnp.float32), 'W1': init(ks[3], (DEPTH, DIM, 2 * DIM_INNER)), 'b1': jnp.zeros((DEPTH, 2 * DIM_INNER), jnp.float32), 'W2': init(ks[4], (DEPTH, DIM_INNER, DIM)), 'b2': jnp.zeros((DEPTH, DIM), jnp.float32)}
    _L0_ffn_in = _L0_ffn_setup()
    _L0_c = _w((lambda *s: np.random.randn(*s).astype(np.float32) * 0.05)(8, 128))
    _L0_wmod = _w((lambda *s: np.random.randn(*s).astype(np.float32) * 0.05)(128, 6 * 128) * 128 ** (-0.5))
    _d = {'L0_attn_x': _L0_attn_in['x'], 'L0_attn_wq': _L0_attn_in['wq'], 'L0_attn_bq': _L0_attn_in['bq'], 'L0_attn_wk': _L0_attn_in['wk'], 'L0_attn_bk': _L0_attn_in['bk'], 'L0_attn_wv': _L0_attn_in['wv'], 'L0_attn_bv': _L0_attn_in['bv'], 'L0_attn_wo': _L0_attn_in['wo'], 'L0_attn_bo': _L0_attn_in['bo'], 'L0_ffn_Wqkv': _L0_ffn_in['Wqkv'], 'L0_ffn_q_scale': _L0_ffn_in['q_scale'], 'L0_ffn_k_scale': _L0_ffn_in['k_scale'], 'L0_ffn_Wo': _L0_ffn_in['Wo'], 'L0_ffn_ln_g': _L0_ffn_in['ln_g'], 'L0_ffn_ln_b': _L0_ffn_in['ln_b'], 'L0_ffn_W1': _L0_ffn_in['W1'], 'L0_ffn_b1': _L0_ffn_in['b1'], 'L0_ffn_W2': _L0_ffn_in['W2'], 'L0_ffn_b2': _L0_ffn_in['b2'], 'L0_c': _L0_c, 'L0_wmod': _L0_wmod}
    _x0 = _d['L0_attn_x']
    _d['L0_attn_x'] = jax.random.normal(jax.random.fold_in(jax.random.key(seed), 1), (8, 256, 128), dtype=_x0.dtype)
    del _x0
    return _d

def reference(L0_attn_x, L0_attn_wq, L0_attn_bq, L0_attn_wk, L0_attn_bk, L0_attn_wv, L0_attn_bv, L0_attn_wo, L0_attn_bo, L0_ffn_Wqkv, L0_ffn_q_scale, L0_ffn_k_scale, L0_ffn_Wo, L0_ffn_ln_g, L0_ffn_ln_b, L0_ffn_W1, L0_ffn_b1, L0_ffn_W2, L0_ffn_b2, L0_c, L0_wmod):

    def _L0_attn_ref(x, wq, bq, wk, bk, wv, bv, wo, bo):
        import jax, jax.numpy as jnp
        import numpy as np
        NUM_HEADS = 16

        def _heads(t, B, N, H, hd):
            return t.reshape(B, N, H, hd).transpose(0, 2, 1, 3)
        B, N, D = x.shape
        H = NUM_HEADS
        hd = D // H
        q = _heads(x @ wq.T + bq, B, N, H, hd)
        k = _heads(x @ wk.T + bk, B, N, H, hd)
        v = _heads(x @ wv.T + bv, B, N, H, hd)
        q2 = jnp.sum(q * q, axis=-1)
        k2 = jnp.sum(k * k, axis=-1)
        qk = jnp.einsum('bhid,bhjd->bhij', q, k)
        d2 = jnp.maximum(q2[..., :, None] + k2[..., None, :] - 2.0 * qk, 1e-12)
        attn = jax.nn.softmax(-jnp.sqrt(d2), axis=-1)
        out = jnp.einsum('bhij,bhjd->bhid', attn, v)
        out = out.transpose(0, 2, 1, 3).reshape(B, N, D)
        return out @ wo.T + bo

    def _L0_ffn_ref(x, Wqkv, q_scale, k_scale, Wo, ln_g, ln_b, W1, b1, W2, b2):
        import jax, jax.numpy as jnp
        import numpy as np
        DIM = 128
        DEPTH = 6
        HEADS = 16
        DIM_HEAD = 64
        WINDOW = 32
        INNER = HEADS * DIM_HEAD
        DIM_INNER = int(DIM * 4 * 2 / 3)
        QK_SCALE = 8.0

        def shift_tokens(t):
            a, s = jnp.split(t, 2, -1)
            s = jnp.pad(s, ((0, 0), (1, 0), (0, 0)))[:, :-1]
            return jnp.concatenate([a, s], -1)

        def l2norm(t):
            return t / jnp.maximum(jnp.linalg.norm(t, axis=-1, keepdims=True), 1e-12)

        def rotate_half(x):
            x1, x2 = jnp.split(x, 2, -1)
            return jnp.concatenate([-x2, x1], -1)

        def rotary_tables(n):
            half = jnp.arange(0, DIM_HEAD, 2, dtype=jnp.float32)
            inv_freq = 1.0 / 10000.0 ** (half / DIM_HEAD)
            t = jnp.arange(n, dtype=jnp.float32)
            freqs = t[:, None] * inv_freq[None, :]
            freqs = jnp.concatenate([freqs, freqs], -1)
            base_scale = (half + 0.4 * DIM_HEAD) / (1.4 * DIM_HEAD)
            power = (t - n // 2) / (WINDOW // 2)
            scale = base_scale[None, :] ** power[:, None]
            scale = jnp.concatenate([scale, scale], -1)
            return (freqs, scale)

        def local_attention(q, k, v):
            b, h, n, d = q.shape
            w = WINDOW
            nw = n // w
            bq = q.reshape(b, h, nw, w, d)
            bk = k.reshape(b, h, nw, w, d)
            bv = v.reshape(b, h, nw, w, d)

            def look(t):
                p = jnp.pad(t, ((0, 0), (0, 0), (1, 0), (0, 0), (0, 0)))
                return jnp.concatenate([p[:, :, :nw], p[:, :, 1:]], axis=3)
            bk2, bv2 = (look(bk), look(bv))
            seq = jnp.arange(n).reshape(nw, w)
            seq_p = jnp.pad(seq, ((1, 0), (0, 0)), constant_values=-1)
            jt = jnp.concatenate([seq_p[:nw], seq_p[1:]], axis=1)
            it = seq[:, :, None]
            jb = jt[:, None, :]
            mask = (it < jb) | (it > jb + w) | (jb == -1)
            sim = jnp.einsum('bhwie,bhwje->bhwij', bq, bk2) * QK_SCALE
            sim = jnp.where(mask, -jnp.finfo(sim.dtype).max, sim)
            attn = jax.nn.softmax(sim, -1)
            out = jnp.einsum('bhwij,bhwje->bhwie', attn, bv2)
            return out.reshape(b, h, n, d)

        def attn_layer(x, Wqkv, qs, ksc, Wo):
            b, n, _ = x.shape
            qkv = x @ Wqkv
            q, k, v = jnp.split(qkv, 3, -1)
            sh = lambda t: t.reshape(b, n, HEADS, DIM_HEAD).transpose(0, 2, 1, 3)
            q, k, v = (sh(q), sh(k), sh(v))
            q = l2norm(q) * qs
            k = l2norm(k) * ksc
            freqs, scale = rotary_tables(n)
            cos, sin = (jnp.cos(freqs), jnp.sin(freqs))
            q = q * cos * scale + rotate_half(q) * sin * scale
            inv = 1.0 / scale
            k = k * cos * inv + rotate_half(k) * sin * inv
            out = local_attention(q, k, v)
            out = out.transpose(0, 2, 1, 3).reshape(b, n, INNER)
            return out @ Wo

        def ffn_layer(x, g, bln, W1, b1, W2, b2):
            mu = x.mean(-1, keepdims=True)
            var = ((x - mu) ** 2).mean(-1, keepdims=True)
            xn = (x - mu) / jnp.sqrt(var + 1e-05) * g + bln
            hg = xn @ W1 + b1
            a, gate = jnp.split(hg, 2, -1)
            return a * jax.nn.gelu(gate, approximate=False) @ W2 + b2
        for i in range(DEPTH):
            x = attn_layer(shift_tokens(x), Wqkv[i], q_scale[i], k_scale[i], Wo[i]) + x
            x = ffn_layer(shift_tokens(x), ln_g[i], ln_b[i], W1[i], b1[i], W2[i], b2[i]) + x
        return x
    x = L0_attn_x
    mod = (_silu(L0_c) @ L0_wmod).reshape(L0_c.shape[0], 6, 1, -1)
    sa, ca, ga, sb, cb, gb = (mod[:, 0], mod[:, 1], mod[:, 2], mod[:, 3], mod[:, 4], mod[:, 5])
    ga = (2 * (ga >= 0) - 1) * jnp.maximum(jnp.abs(ga), 0.25)
    gb = (2 * (gb >= 0) - 1) * jnp.maximum(jnp.abs(gb), 0.25)
    h = _layernorm(x, axis=-1) * (1 + ca) + sa
    x = x + ga * _L0_attn_ref(h, L0_attn_wq, L0_attn_bq, L0_attn_wk, L0_attn_bk, L0_attn_wv, L0_attn_bv, L0_attn_wo, L0_attn_bo)
    h = _layernorm(x, axis=-1) * (1 + cb) + sb
    x = x + gb * _L0_ffn_ref(h, L0_ffn_Wqkv, L0_ffn_q_scale, L0_ffn_k_scale, L0_ffn_Wo, L0_ffn_ln_g, L0_ffn_ln_b, L0_ffn_W1, L0_ffn_b1, L0_ffn_W2, L0_ffn_b2)
    return x

_drawn_inputs = setup_inputs


def setup_inputs(seed=0):
    import zlib

    import numpy as np

    out = dict(_drawn_inputs(seed))
    spreads = {'L0_ffn_q_scale': (1.0, 0.6),
     'L0_ffn_k_scale': (1.0, 0.6),
     'L0_ffn_ln_g': (1.0, 0.6),
     'L0_ffn_ln_b': (0.0, 0.8),
     'L0_ffn_b1': (0.0, 0.8),
     'L0_ffn_b2': (0.0, 0.65)}
    factors = {'L0_attn_wq': 8.0,
     'L0_attn_bq': 8.0,
     'L0_attn_wk': 8.0,
     'L0_attn_bk': 8.0,
     'L0_attn_wv': 8.0,
     'L0_attn_bv': 8.0,
     'L0_attn_wo': 8.0,
     'L0_attn_bo': 8.0,
     'L0_ffn_W1': 7.415,
     'L0_ffn_W2': 7.279}
    for name, (base, spread) in spreads.items():
        noise = np.random.default_rng([zlib.crc32(name.encode()), seed]).standard_normal(out[name].shape)
        drawn = base * np.exp(spread * noise) if base else spread * noise
        out[name] = jnp.asarray(drawn.astype(out[name].dtype))
    for name, factor in factors.items():
        out[name] = (out[name] * factor).astype(out[name].dtype)
    return out
```

```python
import concourse.bass as bass
from concourse import mybir
from contextlib import ExitStack

BATCH, TOKENS, DIM = 8, 256, 128
COLS = BATCH * TOKENS
TILES = TOKENS // 128
HEADS = 16
LAYERS = 6
DH = 64
PAIRS = HEADS // 2
WINDOW = 32
WINDOWS = TOKENS // WINDOW
INNER = HEADS * DH
FF = int(DIM * 4 * 2 / 3)
FFC = 3
FFP = [128, 128, FF - 256]
WA = 6 * INNER + 4
WF = 2 * FF + FFC * DIM + 2 * FFC + 3
QK_SCALE = 8.0
LN_EPS = 1e-5


def adaln_kernel(nc, xT, cT, wmod, w_att1, v_att1, w_att, w_ffn, c_f32, c_bf16, out):
    f32 = mybir.dt.float32
    bf16 = mybir.dt.bfloat16
    ALU = mybir.AluOpType
    ACT = mybir.ActivationFunctionType
    X = mybir.AxisListType.X
    ds = bass.ds

    ctx = ExitStack()
    with ctx:
        def sb(name, shape, dt=f32):
            return ctx.enter_context(nc.sbuf_tensor(name, shape, dt))

        def sem(name):
            return ctx.enter_context(nc.semaphore(name))

        consts = sb("consts", [128, c_f32.shape[1]])
        at = [0]

        def const(n):
            at[0] += n
            return consts[:, at[0] - n:at[0]]

        ident = const(128)
        mean_w = const(128)
        q2_w = const(128)
        k2_w = const(128)
        head_sel = const(4)
        one8 = const(1)
        one9 = const(1)
        eps_col = const(1)
        ones_w = const(128)
        slide = const(64)
        k_sel = const(PAIRS * 128).rearrange("p (c n) -> p c n", c=PAIRS)
        rot = const(4 * TOKENS).rearrange("p (a t) -> p a t", a=4)
        cb = sb("cb", [128, 128 + 2 * 2 * WINDOW], bf16)
        ident_b = cb[:, 0:128]
        mask_b = [cb[:, 128 + 64 * t:192 + 64 * t] for t in range(TILES)]

        wa = sb("wa", [128, WA])
        wq, wq_r, wk, wk_r = [wa[:, INNER * j:INNER * (j + 1)].rearrange("p (c n) -> p c n", c=PAIRS)
                              for j in range(4)]
        wv = wa[:, 4 * INNER:5 * INNER].rearrange("p (v n) -> p v n", v=2)
        wo = wa[:, 5 * INNER:6 * INNER].rearrange("p (c n) -> p c n", c=PAIRS)
        qk_vec = wa[:, 6 * INNER:WA]
        wf = sb("wf", [128, WF])
        w1 = wf[:, 0:2 * FF]
        w2 = wf[:, 2 * FF:2 * FF + FFC * DIM].rearrange("p (c n) -> p c n", c=FFC)
        o = 2 * FF + FFC * DIM
        b1a, b1g = wf[:, o:o + FFC], wf[:, o + FFC:o + 2 * FFC]
        b2, ln_g, ln_b = [wf[:, o + 2 * FFC + j:o + 2 * FFC + j + 1] for j in range(3)]

        xo = sb("xo", [128, COLS])
        xi = sb("xi", [128, COLS])

        cs = sb("cs", [128, 4 * BATCH])
        wm = sb("wm", [128, 6 * DIM])
        mod = sb("mod", [128, 6, BATCH])
        mod_t = sb("mod_t", [128, 3, BATCH])

        arena_cols = 37000
        arena = sb("arena", [128, arena_cols])

        class Carve:
            def __init__(self):
                self.at = 0

            def __call__(self, *shape):
                n = 1
                for k in shape:
                    n *= k
                v = arena[:, self.at:self.at + n]
                self.at += n
                assert self.at <= arena_cols, self.at
                names = "abcd"[:len(shape)]
                if len(shape) > 1:
                    v = v.rearrange("p (" + " ".join(names) + ") -> p " + " ".join(names),
                                    **dict(zip(names[1:], shape[1:])))
                return v

        c0 = Carve()
        ln_c = c0(COLS)
        ln_q = c0(COLS)
        ln_s = c0(COLS)
        ln_sd, ln_rs = c0(16), c0(16)
        after_ln = c0.at

        c1 = Carve()
        pt1 = c1(8, TILES, TOKENS)
        c1.at = after_ln
        h1 = ln_s
        w1a = c1(3, 512)
        wo1 = c1(4, 128)
        bv1 = c1(512)
        vec1 = c1(9)
        dist = [c1(HEADS, TILES, TOKENS) for _ in range(2)]
        dmin = [c1(HEADS * TILES) for _ in range(2)]
        dmin_r = [c1(HEADS * TILES) for _ in range(2)]
        rsum1 = c1(HEADS * TILES)
        rinv1 = c1(4, 4, TILES)
        rinv_w = c1(TILES, 128)
        qk1 = [c1(2, TOKENS) for _ in range(2)]
        sq1 = [c1(2, TOKENS) for _ in range(2)]
        qa1 = [c1(TOKENS) for _ in range(2)]
        ka1 = c1(TOKENS)
        km1 = [c1(4, TOKENS) for _ in range(2)]
        v1 = [c1(TILES, 512) for _ in range(2)]
        hs1 = [c1(TOKENS) for _ in range(2)]
        osb1 = [c1(TOKENS) for _ in range(2)]
        on1 = c1(4, TOKENS)
        tmp1 = c1(TOKENS)

        c2 = Carve()
        c2.at = 0
        qk_tab = c2(4, TOKENS)
        PAD = WINDOW + TOKENS
        xs = [c2(PAD) for _ in range(2)]
        t_cos = [c2(2, TOKENS) for _ in range(2)]
        t_sin = [c2(2, TOKENS) for _ in range(2)]
        ln_at = c2.at
        sq = c2(2 * PAIRS, TOKENS)
        k0 = c2(PAIRS, TOKENS)
        nrm, nrm_c, rinv = c2(TOKENS), c2(TOKENS), c2(TOKENS)
        rq = [c2(TILES, 2, PAIRS) for _ in range(2)]
        qr = [c2(PAIRS, TOKENS) for _ in range(2)]
        kr = [c2(PAIRS, PAD) for _ in range(2)]
        vw_at = c2.at
        vw = [c2(WINDOWS, 512) for _ in range(2)]
        pr = [c2(HEADS, 2 * WINDOW) for _ in range(TILES)]
        mx, rs, rsi = [[c2(HEADS) for _ in range(TILES)] for _ in range(3)]
        pt = [c2(PAIRS, 128) for _ in range(TILES)]
        ow = [c2(PAIRS, 128) for _ in range(TILES)]
        ot = c2(PAIRS, TOKENS)
        c3 = Carve()
        c3.at = vw_at
        gl = [c3(512) for _ in range(FFC)]
        hh = [c3(512) for _ in range(FFC)]

        c4 = Carve()
        c4.at = ln_at
        f_c, f_q, f_s = c4(COLS), c4(COLS), c4(COLS)
        f_sd, f_rs = c4(16), c4(16)

        PS = [ctx.enter_context(nc.psum_tensor(f"ps{i}", [128, 512], f32)) for i in range(8)]
        pb, sbk, tb, ob = PS[0:2], PS[2:4], PS[4:6], PS[6:8]
        wb = PS[0:2] + PS[6:8]
        VB = (0, 1, 2, 3, 1, 2, 1, 2)

        S = {}

        def sems(*names):
            for n in names:
                S[n] = sem(n)

        sems("in_x", "in_mod", "in_const", "in_w1", "wa_in", "wf_in", "stored")
        sems("silu_e", "silu_done", "mod_mm", "mod_step", "mod_done")
        sems("mean_mm", "cent", "cent_sq", "var_mm", "sd_done", "rstd_done", "rstd_mm", "normed", "affine", "h_in")
        sems("a_qk", "a_qksb", "a_sq", "a_n2", "a_qa", "a_ka", "a_km", "a_sc", "a_cl", "a_sqrt", "a_vmm", "a_vs",
             "b_exp", "b_ri", "b_rw", "b_t", "b_pd", "b_pa", "b_pv", "b_r", "b_o", "b_on", "b_y", "b_tmp", "b_x")
        sems("pads", "tab", "xs_in", "qk_mm", "t_done", "sq_done", "add_done", "nrm_mm", "nrm_sd", "nrm_max", "rinv_done",
             "rq_mm", "rq_done", "kb_mm", "k_done", "v_mm", "v_done",
             "s_mm", "sc_done", "mx_done", "sub_done", "exp_done", "rs_sum", "rs_done", "tr_mm", "tr_out",
             "pv_mm", "o_done", "y_mm", "x_done")
        sems("fs_in", "h_mm", "gl_done", "hh_done", "y2_mm", "xf_done")

        block = ctx.enter_context(nc.Block())

        def batch(t, b):
            return t[:, ds(b * TOKENS, TOKENS)]

        def rep(ap, dim, n):
            ap = ap.unsqueeze(dim)
            shape = list(ap.shape)
            shape[dim] = n
            return ap.broadcast_to(shape)

        class Bank:

            def enter(self, last):
                self.last = last

            def take(self, pe, name, value):
                if self.last:
                    pe.wait_ge(S[self.last[0]], self.last[1])
                self.last = (name, value)

        def ln_pe(pe, k, src, ready, bc, bq, brs):
            ready(pe)
            for n in range(4):
                if n >= 2:
                    pe.wait_ge(S["cent"], 4 * k + n - 1)
                pe.matmul(pb[n % 2][:, :], mean_w, src[:, 512 * n:512 * n + 512], start=True, stop=True)\
                    .then_inc(S["mean_mm"], 1)
            for t in range(16):
                if t % 4 == 0:
                    pe.wait_ge(S["cent_sq"], 4 * k + t // 4 + 1)
                i = pe.matmul(ob[0][:, t:t + 1], bq[:, 128 * t:128 * t + 128], mean_w[:, 0:1], start=True, stop=True)
            i.then_inc(S["var_mm"], 1)
            pe.wait_ge(S["rstd_done"], k + 1)
            for n in range(4):
                if n >= 2:
                    pe.wait_ge(S["normed"], 4 * k + n - 1)
                else:
                    pe.wait_ge(S["cent"], 4 * k + 4)
                for t in range(4):
                    i = pe.matmul(pb[n % 2][:, 128 * t:128 * t + 128],
                                  brs[:, 4 * n + t:4 * n + t + 1].broadcast_to([128, 128]), ident,
                                  start=True, stop=True)
                i.then_inc(S["rstd_mm"], 1)

        def ln_dve(dve, k, src, bc, bsd, brs):
            for n in range(4):
                dve.wait_ge(S["mean_mm"], 4 * k + n + 1)
                c = slice(512 * n, 512 * n + 512)
                dve.tensor_tensor(bc[:, c], src[:, c], pb[n % 2][:, :], ALU.subtract).then_inc(S["cent"], 1)
            dve.wait_ge(S["sd_done"], k + 1)
            dve.reciprocal(brs, bsd).then_inc(S["rstd_done"], 1)
            for n in range(4):
                dve.wait_ge(S["rstd_mm"], 4 * k + n + 1)
                c = slice(512 * n, 512 * n + 512)
                dve.tensor_tensor(bc[:, c], bc[:, c], pb[n % 2][:, :], ALU.mult).then_inc(S["normed"], 1)

        def ln_act(act, k, bc, bq, bsd, dst, scale, bias):
            for n in range(4):
                act.wait_ge(S["cent"], 4 * k + n + 1)
                c = slice(512 * n, 512 * n + 512)
                nc.scalar.activation(bq[:, c], bc[:, c], ACT.Square).then_inc(S["cent_sq"], 1)
            act.wait_ge(S["var_mm"], k + 1)
            nc.scalar.activation(bsd, ob[0][:, 0:16], ACT.Sqrt, bias=eps_col).then_inc(S["sd_done"], 1)
            for b in range(BATCH):
                act.wait_ge(S["normed"], 4 * k + b // 2 + 1)
                c = slice(TOKENS * b, TOKENS * b + TOKENS)
                nc.scalar.activation(dst[:, c], bc[:, c], ACT.Identity, scale=scale(b), bias=bias(b))\
                    .then_inc(S["affine"], 1)

        LN_BUFS = dict(bc=ln_c, bq=ln_q, bsd=ln_sd, brs=ln_rs)
        LN_F = dict(bc=f_c, bq=f_q, bsd=f_sd, brs=f_rs)

        @block.sync
        def _(sp):
            sp.dma_start(xo[:, :], xT).then_inc(S["in_x"], 16)
            sp.dma_start(consts[:, :], c_f32).then_inc(S["in_const"], 16)
            sp.dma_start(cb[:, :], c_bf16).then_inc(S["in_const"], 16)
            sp.dma_start(cs[:, 0:BATCH], cT).then_inc(S["in_mod"], 16)
            sp.dma_start(wm[:, :], wmod).then_inc(S["in_mod"], 16)
            sp.dma_start(arena[:, after_ln:after_ln + 2560], w_att1).then_inc(S["in_w1"], 16)
            sp.dma_start(vec1, v_att1).then_inc(S["in_w1"], 16)
            sp.dma_start(wa[:, :], w_att[0, :, :]).then_inc(S["wa_in"], 16)
            sp.dma_start(wf[:, :], w_ffn[0, :, :]).then_inc(S["wf_in"], 16)
            with sp.Fori(0, LAYERS - 1) as l:
                sp.wait_ge(S["y_mm"], 8 * l + 8)
                sp.dma_start(wa[:, :], w_att[ds(l + 1, 1), :, :].rearrange("a p n -> (a p) n")).then_inc(S["wa_in"], 16)
                sp.wait_ge(S["xf_done"], 4 * l + 4)
                sp.dma_start(wf[:, :], w_ffn[ds(l + 1, 1), :, :].rearrange("a p n -> (a p) n")).then_inc(S["wf_in"], 16)
            sp.wait_ge(S["b_x"], 2 * BATCH + BATCH)
            sp.dma_start(out, xo[:, :]).then_inc(S["stored"], 16)
            sp.wait_ge(S["stored"], 16)

        @block.tensor
        def _(pe):
            pe.wait_ge(S["in_mod"], 32)
            pe.wait_ge(S["silu_done"], 3)
            for j in range(6):
                i = pe.matmul(PS[7][:, BATCH * j:BATCH * j + BATCH], wm[:, DIM * j:DIM * j + DIM],
                              cs[:, 3 * BATCH:4 * BATCH], start=True, stop=True)
            i.then_inc(S["mod_mm"], 1)

            def ready0(pe):
                pe.wait_ge(S["in_x"], 16)
                pe.wait_ge(S["in_const"], 32)
                pe.wait_ge(S["mod_done"], 1)
            ln_pe(pe, 0, xo, ready0, ln_c, ln_q, ln_rs)
            pe.wait_ge(S["affine"], 8)
            pe.wait_ge(S["in_w1"], 32)

            def a_qk(U, cc, slot):
                pe.wait_ge(S["a_qksb"], 8 * U + 2 * cc)
                pe.wait_ge(S["a_vs"], 2 * U)
                for j in range(2):
                    i = pe.matmul(pb[0][:, TOKENS * j:TOKENS * j + TOKENS], w1a[:, j, 128 * cc:128 * cc + 128], hs1[slot],
                                  start=True, stop=True)
                i.then_inc(S["a_qk"], 1)

            def a_n2(U, cc):
                pe.wait_ge(S["a_sq"], 4 * U + cc + 1)
                if not isinstance(U, int) or 4 * U + cc > 0:
                    pe.wait_ge(S["a_qa"], 4 * U + cc)
                    pe.wait_ge(S["a_ka"], 4 * U + cc)
                for j, w in enumerate((q2_w, k2_w)):
                    i = pe.matmul(pb[1][:, TOKENS * j:TOKENS * j + TOKENS], w, sq1[cc % 2][:, j, :],
                                  start=True, stop=True)
                i.then_inc(S["a_n2"], 1)

            def a_scores(U, cc):
                pe.wait_ge(S["a_qa"], 4 * U + cc + 1)
                pe.wait_ge(S["a_km"], 16 * U + 4 * cc + 4)
                for t in range(TILES):
                    for p in range(2):
                        i = 4 * cc + 2 * t + p
                        if not isinstance(U, int) or 32 * U + 2 * i - 2 > 0:
                            pe.wait_ge(S["a_cl"], 32 * U + 2 * i - 2)
                        pe.matmul(sbk[i % 2][:, :], qa1[cc % 2][:, 128 * t:128 * t + 128],
                                  km1[cc % 2][:, 2 * p:2 * p + 2, :], start=True, stop=True).then_inc(S["a_sc"], 1)

            def a_v(U, t, slot):
                pe.wait_ge(S["a_qksb"], 8 * U + 8)
                if t:
                    pe.wait_ge(S["a_vs"], 2 * U + 1)
                pe.matmul(pb[0][:, :], hs1[slot][:, 128 * t:128 * t + 128], w1a[:, 2, :],
                          start=True, stop=True).then_inc(S["a_vmm"], 1)

            def b_t(U, cc, slot):
                for u in range(4):
                    h = 4 * cc + u
                    pe.wait_ge(S["b_exp"], 32 * U + 2 * h + 2)
                    q = S["b_pd"] if h % 2 == 0 else S["b_pa"]
                    if not isinstance(U, int) or 8 * U + h // 2 > 0:
                        pe.wait_ge(q, 8 * U + h // 2)
                    for jt in range(TILES):
                        for t in range(TILES):
                            a = 256 * jt + 128 * t
                            i = pe.transpose(tb[h % 2][:, a:a + 128], dist[slot][:, h, t, 128 * jt:128 * jt + 128],
                                             ident)
                    i.then_inc(S["b_t"], 1)

            def b_pv(U, cc, slot):
                pe.wait_ge(S["b_pd"], 8 * U + 2 * cc + 2)
                pe.wait_ge(S["b_pa"], 8 * U + 2 * cc + 2)
                pe.wait_ge(S["a_vs"], 2 * U + 2)
                if not isinstance(U, int) or 4 * U + cc > 0:
                    pe.wait_ge(S["b_o"], 4 * U + cc)
                for jt in range(TILES):
                    for u in range(4):
                        h = 4 * cc + u
                        i = pe.matmul(ob[0][32 * u:32 * u + 32, 0:TOKENS], v1[slot][:, jt, 32 * h:32 * h + 32],
                                      pt1[:, h % 8, jt, :], start=(jt == 0), stop=(jt == 1),
                                      skip_group_check=True)
                i.then_inc(S["b_pv"], 1)
                pe.wait_ge(S["b_rw"], 4 * U + cc + 1)
                if not isinstance(U, int) or 4 * U + cc > 0:
                    pe.wait_ge(S["b_on"], 4 * U + cc)
                    pe.wait_ge(S["b_tmp"], U)
                for t in range(TILES):
                    i = pe.matmul(ob[1][:, 128 * t:128 * t + 128], rinv_w[:, t, :], ident,
                                  start=True, stop=True)
                i.then_inc(S["b_r"], 1)

            def b_y(U):
                pe.wait_ge(S["b_on"], 4 * U + 4)
                for cc in range(4):
                    i = pe.matmul(ob[1][:, 0:TOKENS], wo1[:, cc, :], on1[:, cc, :], start=(cc == 0), stop=(cc == 3))
                i.then_inc(S["b_y"], 1)

            def dist_unit(UA, sa, UB, sb_):
                A, B = UA is not None, UB is not None
                if A:
                    pe.wait_ge(S["h_in"], UA + 1)
                    a_qk(UA, 0, sa)
                    a_qk(UA, 1, sa)
                    a_n2(UA, 0)
                for cc in range(4):
                    if B:
                        b_t(UB, cc, sb_)
                    if A:
                        a_scores(UA, cc)
                        if cc < 2:
                            a_qk(UA, cc + 2, sa)
                        if cc == 2:
                            a_v(UA, 0, sa)
                        if cc < 3:
                            a_n2(UA, cc + 1)
                    if B and cc:
                        b_pv(UB, cc - 1, sb_)
                if A:
                    a_v(UA, 1, sa)
                if B:
                    b_pv(UB, 3, sb_)
                    b_y(UB)

            dist_unit(0, 0, None, None)
            with pe.Fori(0, 3) as i2:
                dist_unit(2 * i2 + 1, 1, 2 * i2, 0)
                dist_unit(2 * i2 + 2, 0, 2 * i2 + 1, 1)
            dist_unit(7, 1, 6, 0)
            dist_unit(None, None, 7, 1)

            def ready1(pe):
                pe.wait_ge(S["b_x"], 2 * BATCH)
            ln_pe(pe, 1, xo, ready1, ln_c, ln_q, ln_rs)

            banks = [Bank() for _ in wb]

            def qk(U, j):
                w = ((wq, wq_r), (wk, wk_r))[j // 4]
                for r in range(2):
                    n = 2 * (j % 2) + r
                    banks[n].take(pe, *(("sq_done", 8 * U + j + 1), ("t_done", 16 * U + 2 * j + 2))[r])
                    for c in range(2):
                        i = pe.matmul(wb[n][:, TOKENS * c:TOKENS * c + TOKENS], w[r][:, 2 * (j % 4) + c, :],
                                      xs[cur["sa"]][:, WINDOW:PAD], start=True, stop=True)
                    i.then_inc(S["qk_mm"], 1)

            def values(U, w):
                r = VB[w]
                banks[r].take(pe, "v_done", 8 * U + w + 1)
                for v in range(2):
                    i = pe.matmul(wb[r][64 * v:64 * v + 64, :], xs[cur["sa"]][:, WINDOW * w:WINDOW * w + 64],
                                  wv[:, v, :], start=True, stop=True)
                i.then_inc(S["v_mm"], 1)

            def norms(U):
                pe.wait_ge(S["sq_done"], 8 * U + 8)
                banks[0].take(pe, "nrm_sd", U + 1)
                for c in range(4):
                    for g in range(4):
                        i = pe.matmul(pb[0][32 * g:32 * g + 32, 0:TOKENS], slide[:, 30 - 2 * c:62 - 2 * c],
                                      sq[:, 4 * g + c, :], start=(c == 0), stop=(c == 3), skip_group_check=True)
                i.then_inc(S["nrm_mm"], 1)

            def q_norms(U):
                pe.wait_ge(S["rinv_done"], U + 1)
                for t in range(TILES):
                    i = pe.transpose(tb[0][:, 128 * t:128 * t + 128], rinv[:, 128 * t:128 * t + 128], ident)
                i.then_inc(S["rq_mm"], 1)

            def k_norms(U, j):
                banks[j].take(pe, "k_done", 4 * U + j + 1)
                for c in range(2):
                    i = pe.matmul(wb[j][:, TOKENS * c:TOKENS * c + TOKENS], k_sel[:, 2 * j + c, :], rinv,
                                  start=True, stop=True)
                i.then_inc(S["kb_mm"], 1)

            def scores(U, t, slot):
                if t == 0:
                    pe.wait_ge(S["add_done"], 8 * U + 8)
                    pe.wait_ge(S["k_done"], 4 * U + 4)
                    pe.wait_ge(S["rq_done"], U + 1)
                    pe.wait_ge(S["v_done"], 8 * U + 8)
                if not isinstance(U, int) or 4 * U + 2 * t > 0:
                    pe.wait_ge(S["sc_done"], 4 * U + 2 * t)
                for v in range(2):
                    pe.matmul(sbk[v][:, :], ident_b, rep(mask_b[t], 1, PAIRS), start=True, stop=False,
                              skip_group_check=True)
                for c in range(PAIRS):
                    for w in range(4):
                        W = 4 * t + w
                        for v in range(2):
                            p = slice(64 * v, 64 * v + 64)
                            i = pe.matmul(sbk[v][32 * w:32 * w + 32, 64 * c:64 * c + 64],
                                          qr[slot][p, c, 32 * W:32 * W + 32], kr[slot][p, c, 32 * W:32 * W + 64],
                                          start=False, stop=(c == PAIRS - 1), skip_group_check=True)
                i.then_inc(S["s_mm"], 1)

            def transposes(U, t, step, src):
                for r in range(2):
                    if step:
                        pe.wait_ge(S["tr_out"], 8 * U + 2 * step + r - 1)
                    for c in range(4):
                        i = pe.transpose(tb[r][:, 128 * c:128 * c + 128], src[:, 4 * r + c, :], ident)
                    i.then_inc(S["tr_mm"], 1)

            def p_t(U, t):
                pe.wait_ge(S["exp_done"], 2 * U + t + 1)
                if t == 0:
                    pe.wait_ge(S["rq_done"], U + 1)
                transposes(U, t, (0, 1)[t], pr[t].rearrange("p (c v) j -> p c (v j)", v=2))

            def o_t(U, t):
                pe.wait_ge(S["o_done"], 4 * U + 2 * t + 2)
                transposes(U, t, (2, 3)[t], ow[t])

            def pv(U, t, slot):
                for c in range(PAIRS):
                    for w in range(4):
                        for v in range(2):
                            p = slice(64 * v, 64 * v + 64)
                            i = pe.matmul(sbk[v][32 * w:32 * w + 32, 64 * c:64 * c + 64],
                                          pt[t][p, c, 32 * w:32 * w + 32],
                                          vw[slot][p, 4 * t + w, 64 * c:64 * c + 64], start=True, stop=True,
                                          skip_group_check=True)
                i.then_inc(S["pv_mm"], 1)

            def out_proj(U):
                pe.wait_ge(S["tr_out"], 8 * U + 8)
                banks[3].take(pe, "x_done", U + 1)
                for c in range(PAIRS):
                    i = pe.matmul(wb[3][:, 0:TOKENS], wo[:, c, :], ot[:, c, :], start=(c == 0), stop=(c == PAIRS - 1))
                i.then_inc(S["y_mm"], 1)

            cur = {}

            def win_unit(UA, sa, UB, sb_):
                A, B = UA is not None, UB is not None
                cur["sa"] = sa
                ua = UA if A else UB + 1
                for n in range(4):
                    banks[n].enter(("k_done", 4 * ua - 3 + n) if B else None)
                if A:
                    pe.wait_ge(S["xs_in"], 2 * UA + 2)
                    values(UA, 0)
                    values(UA, 1)
                if B:
                    scores(UB, 0, sb_)
                if A:
                    values(UA, 2)
                    values(UA, 3)
                if B:
                    scores(UB, 1, sb_)
                if A:
                    qk(UA, 0)
                    qk(UA, 1)
                if B:
                    p_t(UB, 0)
                if A:
                    qk(UA, 2)
                    qk(UA, 3)
                if B:
                    p_t(UB, 1)
                    pv(UB, 0, sb_)
                if A:
                    qk(UA, 4)
                    qk(UA, 5)
                if B:
                    o_t(UB, 0)
                    pv(UB, 1, sb_)
                if A:
                    qk(UA, 6)
                    qk(UA, 7)
                if B:
                    o_t(UB, 1)
                if A:
                    norms(UA)
                    for w in range(4, 8):
                        values(UA, w)
                if B:
                    out_proj(UB)
                if A:
                    if B:
                        pe.wait_ge(S["tr_out"], 8 * UB + 8)
                    q_norms(UA)
                    for j in range(4):
                        k_norms(UA, j)

            with pe.Fori(0, LAYERS) as l:
                pe.wait_ge(S["wa_in"], 16 * l + 16)
                win_unit(8 * l, 0, None, None)
                with pe.Fori(0, 3) as i2:
                    U = 8 * l + 2 * i2
                    win_unit(U + 1, 1, U, 0)
                    win_unit(U + 2, 0, U + 1, 1)
                win_unit(8 * l + 7, 1, 8 * l + 6, 0)
                win_unit(None, None, 8 * l + 7, 1)

                def ready2(pe):
                    pe.wait_ge(S["fs_in"], 3 * l + 3)
                ln_pe(pe, l + 2, f_s, ready2, f_c, f_q, f_rs)
                hb = PS[2:8]
                pe.wait_ge(S["wf_in"], 16 * l + 16)

                def hidden(n):
                    pe.wait_ge(S["affine"], 8 * (l + 2) + 2 * n + 2)
                    for j in range(FFC):
                        m = FFP[j]
                        for g in range(2):
                            if n:
                                pe.wait_ge(S["hh_done"], 12 * l + 3 * (n - 1) + j + 1)
                            c = FF * g + 128 * j
                            pe.matmul(hb[2 * j + g][0:m, :], w1[:, c:c + m], f_q[:, 512 * n:512 * n + 512],
                                      start=True, stop=True).then_inc(S["h_mm"], 1)

                def down(n):
                    if n >= 2:
                        pe.wait_ge(S["xf_done"], 4 * l + n - 1)
                    for j in range(FFC):
                        m = FFP[j]
                        pe.wait_ge(S["hh_done"], 12 * l + 3 * n + j + 1)
                        i = pe.matmul(pb[n % 2][:, :], w2[0:m, j, :], hh[j][0:m, :], start=(j == 0), stop=(j == FFC - 1))
                    i.then_inc(S["y2_mm"], 1)

                hidden(0)
                for n in range(4):
                    down(n)
                    if n < 3:
                        hidden(n + 1)

        @block.vector
        def _(dve):
            chain = [0]

            def step(ins):
                chain[0] += 1
                ins.then_inc(S["mod_step"], 1)
                dve.wait_ge(S["mod_step"], chain[0])

            dve.wait_ge(S["silu_e"], 1)
            c = [cs[:, BATCH * j:BATCH * j + BATCH] for j in range(4)]
            dve.tensor_scalar(c[2], c[1], 1.0, None, ALU.add).then_inc(S["silu_done"], 1)
            dve.wait_ge(S["silu_done"], 1)
            dve.reciprocal(c[1], c[2]).then_inc(S["silu_done"], 1)
            dve.wait_ge(S["silu_done"], 2)
            dve.tensor_tensor(c[3], c[0], c[1], ALU.mult).then_inc(S["silu_done"], 1)
            dve.wait_ge(S["mod_mm"], 1)
            step(nc.vector.tensor_copy(mod[:, :, :], PS[7][:, 0:6 * BATCH].rearrange("p (j b) -> p j b", j=6)))
            for j in (1, 4):
                step(nc.vector.tensor_scalar(mod[:, j, :], mod[:, j, :], 1.0, None, ALU.add))
            for j in (2, 5):
                g = mod[:, j, :]
                step(nc.vector.tensor_scalar(mod_t[:, 0, :], g, 0.0, 2.0, ALU.is_ge, ALU.mult))
                step(nc.vector.tensor_scalar(mod_t[:, 1, :], g, -1.0, None, ALU.mult))
                step(nc.vector.tensor_tensor(mod_t[:, 2, :], mod_t[:, 1, :], g, ALU.max))
                step(nc.vector.tensor_scalar(mod_t[:, 1, :], mod_t[:, 2, :], 0.25, None, ALU.max))
                step(nc.vector.tensor_scalar(mod_t[:, 2, :], mod_t[:, 0, :], -1.0, None, ALU.add))
                step(nc.vector.tensor_tensor(g, mod_t[:, 1, :], mod_t[:, 2, :], ALU.mult))
            nc.vector.tensor_copy(mod_t[:, 0, :], mod[:, 2, :]).then_inc(S["mod_done"], 1)
            dve.wait_ge(S["in_x"], 16)
            ln_dve(dve, 0, xo, ln_c, ln_sd, ln_rs)
            dve.wait_ge(S["in_w1"], 32)
            dve.wait_ge(S["in_const"], 32)

            def a_qksb(U, cc):
                dve.wait_ge(S["a_qk"], 4 * U + cc + 1)
                if not isinstance(U, int) or 4 * U + cc >= 2:
                    dve.wait_ge(S["a_sq"], 4 * U + cc - 1)
                nc.vector.tensor_scalar(qk1[cc % 2][:, 0, :], pb[0][:, 0:TOKENS], vec1[:, cc:cc + 1], -2.0,
                                        ALU.add, ALU.mult).then_inc(S["a_qksb"], 1)
                nc.vector.tensor_scalar(qk1[cc % 2][:, 1, :], pb[0][:, TOKENS:2 * TOKENS], vec1[:, 4 + cc:5 + cc], None,
                                        ALU.add).then_inc(S["a_qksb"], 1)

            def a_aug(U, cc):
                n = 4 * U + cc
                dve.wait_ge(S["a_n2"], n + 1)
                dve.wait_ge(S["a_qksb"], 2 * n + 2)
                if not isinstance(U, int) or n >= 2:
                    dve.wait_ge(S["a_sc"], 4 * n - 4)
                nc.vector.scalar_tensor_tensor(out=qa1[cc % 2], in0=pb[1][:, 0:TOKENS], scalar=one9,
                                               in1=qk1[cc % 2][:, 0, :], op0=ALU.add, op1=ALU.add)\
                    .then_inc(S["a_qa"], 1)
                if not isinstance(U, int) or n > 0:
                    dve.wait_ge(S["a_km"], 4 * n)
                nc.vector.scalar_tensor_tensor(out=ka1, in0=pb[1][:, TOKENS:2 * TOKENS], scalar=one8,
                                               in1=qk1[cc % 2][:, 1, :], op0=ALU.add, op1=ALU.add)\
                    .then_inc(S["a_ka"], 1)
                dve.wait_ge(S["a_ka"], n + 1)
                for u in range(4):
                    nc.vector.tensor_scalar(km1[cc % 2][:, u, :], ka1, head_sel[:, u:u + 1], None, ALU.mult)\
                        .then_inc(S["a_km"], 1)

            def a_clamp(U, cc, slot):
                for t in range(TILES):
                    for p in range(2):
                        i = 4 * cc + 2 * t + p
                        dve.wait_ge(S["a_sc"], 16 * U + i + 1)
                        for q in range(2):
                            h = 4 * cc + 2 * p + q
                            k = 2 * h + t
                            nc.vector.tensor_scalar(dist[slot][:, h, t, :], sbk[i % 2][:, TOKENS * q:TOKENS * q + TOKENS],
                                                    1e-12, None, ALU.max, ALU.min,
                                                    accum_out=dmin[slot][:, k:k + 1]).then_inc(S["a_cl"], 1)

            def a_vs(U, t, slot):
                dve.wait_ge(S["a_vmm"], 2 * U + t + 1)
                nc.vector.tensor_tensor(v1[slot][:, t, :], pb[0][:, :], bv1, ALU.add).then_inc(S["a_vs"], 1)

            def b_pd(U, cc):
                for u in (0, 2):
                    h = 4 * cc + u
                    dve.wait_ge(S["b_t"], 16 * U + h + 1)
                    if u == 0 and cc >= 2:
                        dve.wait_ge(S["b_pv"], 4 * U + cc - 1)
                    nc.vector.tensor_copy(pt1[:, h % 8, :, :], tb[0][:, :].rearrange("p (a t) -> p a t", a=2))\
                        .then_inc(S["b_pd"], 1)

            def b_ri(U, cc):
                dve.wait_ge(S["b_exp"], 32 * U + 8 * cc + 8)
                nc.vector.reciprocal(rinv1[:, cc, :, :], rsum1[:, 8 * cc:8 * cc + 8].rearrange("p (u t) -> p u t", u=4))\
                    .then_inc(S["b_ri"], 1)

            def b_on(U, cc):
                dve.wait_ge(S["b_o"], 4 * U + cc + 1)
                dve.wait_ge(S["b_r"], 4 * U + cc + 1)
                dve.wait_ge(S["b_y"], U)
                nc.vector.tensor_tensor(on1[:, cc, :], osb1[cc % 2], ob[1][:, 0:TOKENS], ALU.mult).then_inc(S["b_on"], 1)

            def b_x(U):
                dve.wait_ge(S["b_y"], U + 1)
                dve.wait_ge(S["b_x"], 2 * U)
                nc.vector.tensor_scalar(tmp1, ob[1][:, 0:TOKENS], vec1[:, 8:9], None, ALU.add).then_inc(S["b_tmp"], 1)
                dve.wait_ge(S["b_tmp"], U + 1)
                nc.vector.tensor_tensor(tmp1, tmp1, mod[:, 2, ds(U, 1)].broadcast_to([128, TOKENS]), ALU.mult)\
                    .then_inc(S["b_x"], 1)
                dve.wait_ge(S["b_x"], 2 * U + 1)
                nc.vector.tensor_tensor(batch(xo, U), batch(xo, U), tmp1, ALU.add).then_inc(S["b_x"], 1)

            def dist_unit(UA, sa, UB, sb_):
                A, B = UA is not None, UB is not None
                if A:
                    if not isinstance(UA, int) or UA >= 2:
                        dve.wait_ge(S["b_t"], 16 * UA - 16)
                        dve.wait_ge(S["b_pv"], 4 * UA - 4)
                    a_qksb(UA, 0)
                    a_qksb(UA, 1)
                    a_aug(UA, 0)
                for cc in range(4):
                    if B:
                        b_pd(UB, cc)
                        b_ri(UB, cc)
                    if A:
                        a_clamp(UA, cc, sa)
                        if cc < 2:
                            a_qksb(UA, cc + 2)
                        if cc == 2:
                            a_vs(UA, 0, sa)
                        if cc < 3:
                            a_aug(UA, cc + 1)
                    if B and cc:
                        b_on(UB, cc - 1)
                if A:
                    a_vs(UA, 1, sa)
                if B:
                    b_on(UB, 3)
                    b_x(UB)

            dist_unit(0, 0, None, None)
            with dve.Fori(0, 3) as i2:
                dist_unit(2 * i2 + 1, 1, 2 * i2, 0)
                dist_unit(2 * i2 + 2, 0, 2 * i2 + 1, 1)
            dist_unit(7, 1, 6, 0)
            dist_unit(None, None, 7, 1)
            dve.wait_ge(S["b_x"], 2 * BATCH)
            ln_dve(dve, 1, xo, ln_c, ln_sd, ln_rs)

            def rotary(U, j, prologue):
                for r, dst in enumerate((t_cos, t_sin)):
                    dve.wait_ge(S["qk_mm"], 16 * U + 2 * j + r + 1)
                    if r == 0 and not (prologue and j < 2):
                        dve.wait_ge(S["add_done"], 8 * U + j - 1)
                    ins = nc.vector.tensor_tensor(dst[j % 2], wb[2 * (j % 2) + r][:, :].rearrange("p (c t) -> p c t", c=2),
                                                  rep(qk_tab[:, 2 * (j // 4) + r, :], 1, 2), ALU.mult)
                    ins.then_inc(S["t_done"], 1)

            def norm_inv(U):
                dve.wait_ge(S["nrm_sd"], U + 1)
                nc.vector.tensor_scalar(nrm_c, nrm, 1e-12, None, ALU.max).then_inc(S["nrm_max"], 1)
                dve.wait_ge(S["nrm_max"], U + 1)
                nc.vector.reciprocal(rinv, nrm_c).then_inc(S["rinv_done"], 1)

            def q_inv(U, slot):
                dve.wait_ge(S["rq_mm"], U + 1)
                nc.vector.tensor_scalar(rq[slot], tb[0][:, 0:256].rearrange("p (t g n) -> p t g n", t=2, g=4)[:, :, 0:2, 0:8],
                                        QK_SCALE, None, ALU.mult).then_inc(S["rq_done"], 1)

            def k_scale(U, j, slot):
                dve.wait_ge(S["kb_mm"], 4 * U + j + 1)
                dve.wait_ge(S["add_done"], 8 * U + 5 + j)
                nc.vector.tensor_tensor(kr[slot][:, 2 * j:2 * j + 2, WINDOW:PAD], k0[:, 2 * j:2 * j + 2, :],
                                        wb[j][:, :].rearrange("p (c t) -> p c t", c=2), ALU.mult)\
                    .then_inc(S["k_done"], 1)

            def scale_max(U, t, slot):
                dve.wait_ge(S["s_mm"], 2 * U + t + 1)
                p = pr[t].rearrange("p (c v) j -> p c v j", v=2)
                q = rq[slot].rearrange("p t g n -> p t (g n)")[:, t, :].rearrange("p (c v) -> p c v", v=2)
                for v in range(2):
                    nc.vector.tensor_tensor(p[:, :, v, :], sbk[v][:, :].rearrange("p (c j) -> p c j", c=PAIRS),
                                            rep(q[:, :, v], 2, 2 * WINDOW), ALU.mult).then_inc(S["sc_done"], 1)
                dve.wait_ge(S["sc_done"], 4 * U + 2 * t + 2)
                nc.vector.tensor_reduce(mx[t], pr[t], X, ALU.max).then_inc(S["mx_done"], 1)

            def row_sums(U, t):
                dve.wait_ge(S["exp_done"], 2 * U + t + 1)
                nc.vector.tensor_reduce(rs[t], pr[t], X, ALU.add).then_inc(S["rs_sum"], 1)
                dve.wait_ge(S["rs_sum"], 2 * U + t + 1)
                nc.vector.reciprocal(rsi[t], rs[t]).then_inc(S["rs_done"], 1)

            def o_norm(U, t):
                dve.wait_ge(S["pv_mm"], 2 * U + t + 1)
                dve.wait_ge(S["rs_done"], 2 * U + t + 1)
                o4 = ow[t].rearrange("p c (v n) -> p c v n", v=2)
                r3 = rsi[t].rearrange("p (c v) -> p c v", v=2)
                for v in range(2):
                    nc.vector.tensor_tensor(o4[:, :, v, :], sbk[v][:, :].rearrange("p (c n) -> p c n", c=PAIRS),
                                            rep(r3[:, :, v], 2, DH), ALU.mult).then_inc(S["o_done"], 1)

            def residual(U, b):
                dve.wait_ge(S["y_mm"], U + 1)
                nc.vector.tensor_tensor(batch(xi, b), wb[3][:, 0:TOKENS], batch(xi, b), ALU.add).then_inc(S["x_done"], 1)

            def win_unit(UA, sa, UB, sb_, b):
                A, B = UA is not None, UB is not None
                pro = not B
                if B:
                    scale_max(UB, 0, sb_)
                    scale_max(UB, 1, sb_)
                if A:
                    rotary(UA, 0, pro)
                    rotary(UA, 1, pro)
                if B:
                    row_sums(UB, 0)
                if A:
                    rotary(UA, 2, pro)
                    rotary(UA, 3, pro)
                if B:
                    row_sums(UB, 1)
                    o_norm(UB, 0)
                if A:
                    rotary(UA, 4, pro)
                    rotary(UA, 5, pro)
                if B:
                    o_norm(UB, 1)
                if A:
                    rotary(UA, 6, pro)
                    rotary(UA, 7, pro)
                    norm_inv(UA)
                if B:
                    residual(UB, b)
                if A:
                    q_inv(UA, sa)
                    if not pro:
                        dve.wait_ge(S["s_mm"], 2 * UA - 2)
                    for j in range(4):
                        k_scale(UA, j, sa)

            with dve.Fori(0, LAYERS) as l:
                dve.wait_ge(S["tab"], 4 * l + 4)
                win_unit(8 * l, 0, None, None, None)
                with dve.Fori(0, 3) as i2:
                    U = 8 * l + 2 * i2
                    win_unit(U + 1, 1, U, 0, 2 * i2)
                    win_unit(U + 2, 0, U + 1, 1, 2 * i2 + 1)
                win_unit(8 * l + 7, 1, 8 * l + 6, 0, 6)
                win_unit(None, None, 8 * l + 7, 1, 7)
                dve.wait_ge(S["fs_in"], 3 * l + 3)
                ln_dve(dve, l + 2, f_s, f_c, f_sd, f_rs)
                dve.wait_ge(S["wf_in"], 16 * l + 16)

                def gate(n):
                    for j in range(FFC):
                        m = FFP[j]
                        dve.wait_ge(S["gl_done"], 12 * l + 3 * n + j + 1)
                        dve.wait_ge(S["h_mm"], 24 * l + 6 * n + 2 * j + 1)
                        if n:
                            dve.wait_ge(S["y2_mm"], 4 * l + n)
                        nc.vector.scalar_tensor_tensor(out=hh[j][0:m, :], in0=PS[2 + 2 * j][0:m, :], scalar=b1a[0:m, j:j + 1],
                                                       in1=gl[j][0:m, :], op0=ALU.add, op1=ALU.mult)\
                            .then_inc(S["hh_done"], 1)

                for n in range(4):
                    gate(n)
                    dve.wait_ge(S["y2_mm"], 4 * l + n + 1)
                    c = slice(512 * n, 512 * n + 512)
                    nc.vector.scalar_tensor_tensor(out=xi[:, c], in0=pb[n % 2][:, :], scalar=b2, in1=xi[:, c],
                                                   op0=ALU.add, op1=ALU.add).then_inc(S["xf_done"], 1)
            dve.wait_ge(S["xf_done"], 4 * LAYERS)
            for b in range(BATCH):
                c = slice(TOKENS * b, TOKENS * b + TOKENS)
                nc.vector.scalar_tensor_tensor(out=xo[:, c], in0=xi[:, c], scalar=mod[:, 5, b:b + 1], in1=xo[:, c],
                                               op0=ALU.mult, op1=ALU.add).then_inc(S["b_x"], 1)

        @block.scalar
        def _(act):
            act.wait_ge(S["in_mod"], 32)
            nc.scalar.activation(cs[:, BATCH:2 * BATCH], cs[:, 0:BATCH], ACT.Exp, scale=-1.0).then_inc(S["silu_e"], 1)
            act.wait_ge(S["in_const"], 32)
            act.wait_ge(S["mod_done"], 1)
            ln_act(act, 0, ln_c, ln_q, ln_sd, h1, lambda b: mod[:, 1, b:b + 1], lambda b: mod[:, 0, b:b + 1])
            act.wait_ge(S["affine"], 8)

            def a_h(U, slot):
                if not isinstance(U, int) or U >= 2:
                    act.wait_ge(S["a_vmm"], 2 * U - 2)
                nc.scalar.activation(hs1[slot], batch(h1, U), ACT.Copy).then_inc(S["h_in"], 1)

            def a_sq(U, cc):
                n = 4 * U + cc
                act.wait_ge(S["a_qksb"], 2 * n + 2)
                if not isinstance(U, int) or n >= 2:
                    act.wait_ge(S["a_n2"], n - 1)
                nc.scalar.activation(sq1[cc % 2], qk1[cc % 2], ACT.Square).then_inc(S["a_sq"], 1)

            def a_sqrt(U, slot):
                for cc in range(4):
                    act.wait_ge(S["a_cl"], 32 * U + 8 * cc + 8)
                    d = dist[slot][:, 4 * cc:4 * cc + 4, :, :]
                    nc.scalar.activation(d, d, ACT.Sqrt).then_inc(S["a_sqrt"], 1)
                nc.scalar.activation(dmin_r[slot], dmin[slot], ACT.Sqrt).then_inc(S["a_sqrt"], 1)

            def b_exp(U, h, slot):
                if h == 0:
                    act.wait_ge(S["a_sqrt"], 5 * U + 5)
                for t in range(TILES):
                    k = 2 * h + t
                    d = dist[slot][:, h, t, :]
                    nc.scalar.activation(d, d, ACT.Exp, scale=-1.0, bias=dmin_r[slot][:, k:k + 1],
                                         accum_out=rsum1[:, k:k + 1]).then_inc(S["b_exp"], 1)

            def b_pa(U, h):
                    act.wait_ge(S["b_t"], 16 * U + h + 1)
                    if h % 4 == 1 and h >= 8:
                        act.wait_ge(S["b_pv"], 4 * U + h // 4 - 1)
                    nc.scalar.activation(pt1[:, h % 8, :, :], tb[1][:, :].rearrange("p (a t) -> p a t", a=2), ACT.Copy)\
                        .then_inc(S["b_pa"], 1)

            def b_o(U, cc):
                act.wait_ge(S["b_pv"], 4 * U + cc + 1)
                if cc >= 2:
                    act.wait_ge(S["b_on"], 4 * U + cc - 1)
                nc.scalar.activation(osb1[cc % 2], ob[0][:, 0:TOKENS], ACT.Copy).then_inc(S["b_o"], 1)

            def dist_unit(UA, sa, UB, sb_):
                A, B = UA is not None, UB is not None
                if A:
                    a_h(UA, sa)
                    a_sq(UA, 0)
                if B:
                    for h in range(4):
                        b_exp(UB, h, sb_)
                for cc in range(4):
                    if B:
                        for h in range(4 * cc, 4 * cc + 4):
                            if cc < 3:
                                b_exp(UB, h + 4, sb_)
                            if h % 2:
                                b_pa(UB, h)
                    if A and cc < 3:
                        a_sq(UA, cc + 1)
                    if B and cc:
                        b_o(UB, cc - 1)
                if B:
                    b_o(UB, 3)
                if A:
                    a_sqrt(UA, sa)

            dist_unit(0, 0, None, None)
            with act.Fori(0, 3) as i2:
                dist_unit(2 * i2 + 1, 1, 2 * i2, 0)
                dist_unit(2 * i2 + 2, 0, 2 * i2 + 1, 1)
            dist_unit(7, 1, 6, 0)
            dist_unit(None, None, 7, 1)
            ln_act(act, 1, ln_c, ln_q, ln_sd, xi, lambda b: mod[:, 4, b:b + 1], lambda b: mod[:, 3, b:b + 1])

            def shift_in(U, b, slot, prologue):
                if not prologue:
                    act.wait_ge(S["v_mm"], 8 * U - 8)
                nc.scalar.activation(xs[slot][0:64, WINDOW:PAD], xi[0:64, ds(b * TOKENS, TOKENS)], ACT.Copy)\
                    .then_inc(S["xs_in"], 1)
                nc.scalar.activation(xs[slot][64:128, WINDOW + 1:PAD], xi[64:128, ds(b * TOKENS, TOKENS - 1)], ACT.Copy)\
                    .then_inc(S["xs_in"], 1)

            def v_out(U, w, slot, prologue):
                act.wait_ge(S["v_mm"], 8 * U + w + 1)
                if w == 0 and not prologue:
                    act.wait_ge(S["pv_mm"], 2 * U - 2)
                nc.scalar.activation(vw[slot][:, w, :], wb[VB[w]][:, :], ACT.Copy).then_inc(S["v_done"], 1)

            def squares(U, j, prologue):
                act.wait_ge(S["t_done"], 16 * U + 2 * j + 1)
                if j == 0 and not prologue:
                    act.wait_ge(S["nrm_mm"], U)
                nc.scalar.activation(sq[:, 2 * j:2 * j + 2, :], wb[2 * (j % 2)][:, :].rearrange("p (c t) -> p c t", c=2), ACT.Square)\
                    .then_inc(S["sq_done"], 1)

            def norm_sqrt(U):
                act.wait_ge(S["nrm_mm"], U + 1)
                act.wait_ge(S["nrm_max"], U)
                nc.scalar.activation(nrm, pb[0][:, 0:TOKENS], ACT.Sqrt).then_inc(S["nrm_sd"], 1)

            def exps(U, t):
                act.wait_ge(S["sub_done"], 2 * U + t + 1)
                nc.scalar.activation(pr[t], pr[t], ACT.Exp).then_inc(S["exp_done"], 1)

            def tr_out(U, t, step, dst):
                for r in range(2):
                    act.wait_ge(S["tr_mm"], 8 * U + 2 * step + r + 1)
                    nc.scalar.activation(dst[:, 4 * r:4 * r + 4, :], tb[r][:, :].rearrange("p (c t) -> p c t", c=4),
                                         ACT.Copy).then_inc(S["tr_out"], 1)

            def p_out(U, t):
                tr_out(U, t, t, pt[t])

            def o_out(U, t):
                if t == 0:
                    act.wait_ge(S["y_mm"], U)
                tr_out(U, t, 2 + t, ot[:, :, 128 * t:128 * t + 128])

            def win_unit(UA, sa, UB, sb_, b):
                A, B = UA is not None, UB is not None
                pro = not B
                if A:
                    shift_in(UA, b, sa, pro)
                    for w in range(4):
                        v_out(UA, w, sa, pro)
                if B:
                    exps(UB, 0)
                if A:
                    squares(UA, 0, pro)
                    squares(UA, 1, pro)
                if B:
                    exps(UB, 1)
                    p_out(UB, 0)
                if A:
                    squares(UA, 2, pro)
                    squares(UA, 3, pro)
                if B:
                    p_out(UB, 1)
                if A:
                    squares(UA, 4, pro)
                    squares(UA, 5, pro)
                if B:
                    o_out(UB, 0)
                if A:
                    squares(UA, 6, pro)
                    squares(UA, 7, pro)
                if B:
                    o_out(UB, 1)
                if A:
                    norm_sqrt(UA)
                    v_out(UA, 4, sa, pro)
                    v_out(UA, 5, sa, pro)
                    v_out(UA, 6, sa, pro)
                    v_out(UA, 7, sa, pro)

            act.wait_ge(S["affine"], 16)
            act.wait_ge(S["pads"], 4)
            with act.Fori(0, LAYERS) as l:
                act.wait_ge(S["xf_done"], 4 * l)
                win_unit(8 * l, 0, None, None, 0)
                with act.Fori(0, 3) as i2:
                    U = 8 * l + 2 * i2
                    win_unit(U + 1, 1, U, 0, 2 * i2 + 1)
                    win_unit(U + 2, 0, U + 1, 1, 2 * i2 + 2)
                win_unit(8 * l + 7, 1, 8 * l + 6, 0, 7)
                win_unit(None, None, 8 * l + 7, 1, None)
                act.wait_ge(S["x_done"], 8 * l + 8)
                s3 = f_s.rearrange("p (b t) -> p b t", b=BATCH)
                x3 = xi[:, :].rearrange("p (b t) -> p b t", b=BATCH)
                nc.scalar.activation(s3[0:64, :, :], x3[0:64, :, :], ACT.Copy).then_inc(S["fs_in"], 1)
                nc.scalar.activation(s3[64:128, :, 1:TOKENS], x3[64:128, :, 0:TOKENS - 1], ACT.Copy).then_inc(S["fs_in"], 1)
                nc.scalar.activation(s3[64:128, :, 0:1], xs[0][64:128, 0:BATCH].unsqueeze(2), ACT.Copy).then_inc(S["fs_in"], 1)
                act.wait_ge(S["wf_in"], 16 * l + 16)
                ln_act(act, l + 2, f_c, f_q, f_sd, f_q, lambda b: ln_g, lambda b: ln_b)
                for n in range(4):
                    for j in range(FFC):
                        m = FFP[j]
                        act.wait_ge(S["h_mm"], 24 * l + 6 * n + 2 * j + 2)
                        if n:
                            act.wait_ge(S["hh_done"], 12 * l + 3 * (n - 1) + j + 1)
                        nc.scalar.activation(gl[j][0:m, :], PS[3 + 2 * j][0:m, :], ACT.Gelu, bias=b1g[0:m, j:j + 1])\
                            .then_inc(S["gl_done"], 1)

        @block.gpsimd
        def _(pool):
            def b_rw(U, cc):
                pool.wait_ge(S["b_ri"], 4 * U + cc + 1)
                pool.wait_ge(S["b_r"], 4 * U + cc)
                nc.gpsimd.tensor_tensor(rinv_w.rearrange("p t (u n) -> p t u n", u=4),
                                        rep(rinv1[:, cc, :, :].rearrange("p u t -> p t u"), 3, 32),
                                        ones_w.rearrange("p (t u n) -> p t u n", t=1, u=4).broadcast_to([128, TILES, 4, 32]),
                                        ALU.mult).then_inc(S["b_rw"], 1)

            with pool.Fori(0, BATCH) as U:
                for cc in range(4):
                    b_rw(U, cc)

            pool.wait_ge(S["affine"], 16)
            for s in range(2):
                nc.gpsimd.memset(xs[s][:, 0:WINDOW + 1], 0.0).then_inc(S["pads"], 1)
                nc.gpsimd.memset(kr[s][:, :, 0:WINDOW], 0.0).then_inc(S["pads"], 1)

            def add(U, j, slot, prologue):
                pool.wait_ge(S["t_done"], 16 * U + 2 * j + 2)
                if j == 0 and not prologue:
                    pool.wait_ge(S["s_mm"], 2 * U - 2)
                    pool.wait_ge(S["k_done"], 4 * U)
                dst = qr[slot][:, 2 * j:2 * j + 2, :] if j < 4 else k0[:, 2 * (j - 4):2 * (j - 4) + 2, :]
                nc.gpsimd.tensor_tensor(dst, t_cos[j % 2], t_sin[j % 2], ALU.add).then_inc(S["add_done"], 1)

            def sub(U, t):
                pool.wait_ge(S["mx_done"], 2 * U + t + 1)
                nc.gpsimd.tensor_tensor(pr[t], pr[t], rep(mx[t], 2, 2 * WINDOW), ALU.subtract)\
                    .then_inc(S["sub_done"], 1)

            def win_unit(UA, sa, UB):
                A, B = UA is not None, UB is not None
                if B:
                    sub(UB, 0)
                    sub(UB, 1)
                if A:
                    for j in range(8):
                        add(UA, j, sa, not B)

            with pool.Fori(0, LAYERS) as l:
                pool.wait_ge(S["wa_in"], 16 * l + 16)
                pool.wait_ge(S["affine"], 8 * l + 16)
                for j in range(4):
                    nc.gpsimd.tensor_tensor(qk_tab[:, j, :], rot[:, j, :], qk_vec[:, j:j + 1].broadcast_to([128, TOKENS]), ALU.mult)\
                        .then_inc(S["tab"], 1)
                win_unit(8 * l, 0, None)
                with pool.Fori(0, 3) as i2:
                    U = 8 * l + 2 * i2
                    win_unit(U + 1, 1, U)
                    win_unit(U + 2, 0, U + 1)
                win_unit(8 * l + 7, 1, 8 * l + 6)
                win_unit(None, None, 8 * l + 7)


def _constants(np):
    p = np.arange(128)
    f = np.float32
    ident = np.eye(128, dtype=f)
    mean_w = np.full((128, 128), 1.0 / 128, f)
    same = (p[:, None] // 32 == p[None, :] // 32) & (p[:, None] % 32 < 8)
    q2_w = np.where(same & (p[None, :] % 32 == 8), f(0.25), f(0))
    k2_w = np.where(same & (p[None, :] % 32 == 9), f(1), f(0))
    head_sel = (p[:, None] // 32 == np.arange(4)[None]).astype(f)
    one8 = (p % 32 == 8).astype(f)[:, None]
    one9 = (p % 32 == 9).astype(f)[:, None]
    eps = np.full((128, 1), LN_EPS, f)
    slide = np.zeros((128, 64), f)
    slide[p, 30 + p // 64] = 1
    k_sel = np.zeros((128, PAIRS, 128), f)
    for c in range(PAIRS):
        for v in range(2):
            k_sel[64 + 32 * (c // 4) + 2 * (c % 4) + v, c, 64 * v:64 * v + 64] = 1
    half = np.arange(0, DH, 2, dtype=f)
    inv_freq = (1.0 / 10000.0 ** (half / DH)).astype(f)
    t = np.arange(TOKENS, dtype=f)
    freqs = t[:, None] * inv_freq[None, :]
    base = (half + 0.4 * DH) / (1.4 * DH)
    power = (t - TOKENS // 2) / (WINDOW // 2)
    scale = (base[None, :].astype(np.float64) ** power[:, None]).astype(f)
    cos, sin = np.cos(freqs.astype(np.float64)), np.sin(freqs.astype(np.float64))
    sign = np.where(p % DH < DH // 2, -1.0, 1.0)[:, None]
    d = p % (DH // 2)
    rot = np.stack([(cos * scale).T[d], sign * (sin * scale).T[d], (cos / scale).T[d], sign * (sin / scale).T[d]], 1)
    c_f32 = np.concatenate([ident, mean_w, q2_w, k2_w, head_sel, one8, one9, eps, np.ones((128, 128), f), slide, k_sel.reshape(128, -1),
                            rot.astype(f).reshape(128, -1)], 1).astype(f)
    i, j = (p % WINDOW)[:, None], np.arange(2 * WINDOW)[None]
    seen = np.where(j < WINDOW, i <= j, j - WINDOW <= i)
    first = seen & ((j >= WINDOW) | (p[:, None] >= WINDOW))
    masks = [np.where(m, 0.0, -1e30) for m in (first, seen)]
    return c_f32, np.concatenate([ident] + masks, 1)


def kernel(**inputs):
    import numpy as np
    import concourse.bacc as bacc
    from concourse import mybir as _mybir
    from concourse.bass_utils import run_bass_kernel_spmd as run

    g = {k: np.asarray(v) for k, v in inputs.items()}
    f = np.float32
    cc = np.ascontiguousarray

    def pad_heads(w):
        w = w.reshape(w.shape[:-1] + (HEADS, 8))
        return np.pad(w, [(0, 0)] * (w.ndim - 1) + [(0, 24)]).reshape(w.shape[:-2] + (HEADS * 32,))

    def columns(v, n):
        return np.pad(v, (0, 128 * n - v.shape[0])).reshape(n, 128).T

    bv = np.broadcast_to(pad_heads(g["L0_attn_bv"])[None], (128, 512))
    wo1 = pad_heads(g["L0_attn_wo"]).reshape(128, 4, 128).transpose(2, 1, 0).reshape(128, 512)
    w_att1 = np.concatenate([pad_heads(g[f"L0_attn_w{n}"].T) for n in "qkv"] + [wo1, bv], 1)
    v_att1 = np.concatenate([columns(pad_heads(g["L0_attn_bq"]), 4), columns(pad_heads(g["L0_attn_bk"]), 4),
                             g["L0_attn_bo"][:, None]], 1)
    swap = (np.arange(DH) + DH // 2) % DH
    qkv = g["L0_ffn_Wqkv"].reshape(LAYERS, DIM, 3, HEADS, DH)
    q, k, v = qkv[:, :, 0], qkv[:, :, 1], qkv[:, :, 2]
    two = lambda s: np.concatenate([s, s], 1)[:, :, None]
    qs, ks = g["L0_ffn_q_scale"], g["L0_ffn_k_scale"]
    w_att = np.concatenate(
        [m.reshape(LAYERS, DIM, INNER) for m in (q, q[..., swap], k, k[..., swap])]
        + [v.reshape(LAYERS, DIM, PAIRS, 2, DH).transpose(0, 1, 3, 2, 4).reshape(LAYERS, DIM, INNER),
           g["L0_ffn_Wo"].reshape(LAYERS, PAIRS, 128, DIM).transpose(0, 2, 1, 3).reshape(LAYERS, 128, INNER),
           two(qs), two(qs[:, swap]), two(ks), two(ks[:, swap])], 2)
    w2 = np.pad(g["L0_ffn_W2"], ((0, 0), (0, 128 * FFC - FF), (0, 0)))
    b1 = g["L0_ffn_b1"]
    w_ffn = np.stack([np.concatenate(
        [g["L0_ffn_W1"][n], w2[n].reshape(FFC, 128, DIM).transpose(1, 0, 2).reshape(128, FFC * DIM),
         columns(b1[n, :FF], FFC), columns(b1[n, FF:], FFC), g["L0_ffn_b2"][n][:, None],
         g["L0_ffn_ln_g"][n][:, None], g["L0_ffn_ln_b"][n][:, None]], 1) for n in range(LAYERS)])
    c_f32, c_bf16 = _constants(np)
    arrays = {
        "xT": g["L0_attn_x"].reshape(COLS, DIM).T, "cT": g["L0_c"].T, "wmod": g["L0_wmod"],
        "w_att1": w_att1, "v_att1": v_att1, "w_att": w_att, "w_ffn": w_ffn, "c_f32": c_f32,
        "c_bf16": c_bf16.astype(_mybir.dt.np(_mybir.dt.bfloat16)),
    }
    arrays = {n: cc(a) for n, a in arrays.items()}
    nc = bacc.Bacc("TRN2", target_bir_lowering=False, num_devices=1)
    args = [nc.dram_tensor(n, a.shape, _mybir.dt.from_np(a.dtype), kind="ExternalInput").ap() for n, a in arrays.items()]
    out = nc.dram_tensor("out", (DIM, COLS), _mybir.dt.float32, kind="ExternalOutput").ap()
    adaln_kernel(nc, *args, out)
    r = run(nc, [arrays], core_ids=[0])
    return cc(r.results[0]["out"].T).reshape(BATCH, TOKENS, DIM).astype(f)
```

```python
import concourse.bass as bass
from concourse import mybir
from contextlib import ExitStack

BATCH, TOKENS, DIM = 8, 256, 128
COLS = BATCH * TOKENS
TILES = TOKENS // 128
HEADS = 16
LAYERS = 6
DH = 64
PAIRS = HEADS // 2
WINDOW = 32
WINDOWS = TOKENS // WINDOW
INNER = HEADS * DH
FF = int(DIM * 4 * 2 / 3)
FFC = 3
FFP = [128, 128, FF - 256]
WA = 4 * INNER + 4
WF = 2 * FF + FFC * DIM + 2 * FFC + 3
QK_SCALE = 8.0
LN_EPS = 1e-5


def adaln_kernel(nc, xT, cT, wmod, w_att1, v_att1, w_att, w_ffn, c_f32, c_bf16, out):
    f32 = mybir.dt.float32
    bf16 = mybir.dt.bfloat16
    ALU = mybir.AluOpType
    ACT = mybir.ActivationFunctionType
    X = mybir.AxisListType.X
    ds = bass.ds

    ctx = ExitStack()
    with ctx:
        def sb(name, shape, dt=f32):
            return ctx.enter_context(nc.sbuf_tensor(name, shape, dt))

        def sem(name):
            return ctx.enter_context(nc.semaphore(name))

        consts = sb("consts", [128, c_f32.shape[1]])
        at = [0]

        def const(n):
            at[0] += n
            return consts[:, at[0] - n:at[0]]

        ident = const(128)
        mean_w = const(128)
        q2_w = const(128)
        k2_w = const(128)
        head_sel = const(4)
        one8 = const(1)
        one9 = const(1)
        eps_col = const(1)
        ones_w = const(128)
        slide = const(64)
        k_sel = const(PAIRS * 128).rearrange("p (c n) -> p c n", c=PAIRS)
        rot = const(4 * TOKENS).rearrange("p (a t) -> p a t", a=4)
        cb = sb("cb", [128, 128 + 2 * 2 * WINDOW], bf16)
        ident_b = cb[:, 0:128]
        mask_b = [cb[:, 128 + 64 * t:192 + 64 * t] for t in range(TILES)]

        wa = sb("wa", [128, WA])
        wq, wk = [wa[:, INNER * j:INNER * (j + 1)].rearrange("p (c n) -> p c n", c=PAIRS) for j in range(2)]
        wv = wa[:, 2 * INNER:3 * INNER].rearrange("p (v n) -> p v n", v=2)
        wo = wa[:, 3 * INNER:4 * INNER].rearrange("p (c n) -> p c n", c=PAIRS)
        qk_vec = wa[:, 4 * INNER:WA]
        wf = sb("wf", [128, WF])
        w1 = wf[:, 0:2 * FF]
        w2 = wf[:, 2 * FF:2 * FF + FFC * DIM].rearrange("p (c n) -> p c n", c=FFC)
        o = 2 * FF + FFC * DIM
        b1a, b1g = wf[:, o:o + FFC], wf[:, o + FFC:o + 2 * FFC]
        b2, ln_g, ln_b = [wf[:, o + 2 * FFC + j:o + 2 * FFC + j + 1] for j in range(3)]

        xo = sb("xo", [128, COLS])
        xi = sb("xi", [128, COLS])

        cs = sb("cs", [128, 4 * BATCH])
        wm = sb("wm", [128, 6 * DIM])
        mod = sb("mod", [128, 6, BATCH])
        mod_t = sb("mod_t", [128, 3, BATCH])

        arena_cols = 37000
        arena = sb("arena", [128, arena_cols])

        class Carve:
            def __init__(self):
                self.at = 0

            def __call__(self, *shape):
                n = 1
                for k in shape:
                    n *= k
                v = arena[:, self.at:self.at + n]
                self.at += n
                assert self.at <= arena_cols, self.at
                names = "abcd"[:len(shape)]
                if len(shape) > 1:
                    v = v.rearrange("p (" + " ".join(names) + ") -> p " + " ".join(names),
                                    **dict(zip(names[1:], shape[1:])))
                return v

        c0 = Carve()
        ln_c = c0(COLS)
        ln_q = c0(COLS)
        ln_s = c0(COLS)
        ln_sd, ln_rs = c0(16), c0(16)
        after_ln = c0.at

        c1 = Carve()
        pt1 = c1(8, TILES, TOKENS)
        c1.at = after_ln
        h1 = ln_s
        w1a = c1(3, 512)
        wo1 = c1(4, 128)
        bv1 = c1(512)
        vec1 = c1(9)
        dist = [c1(HEADS, TILES, TOKENS) for _ in range(2)]
        dmin = [c1(HEADS * TILES) for _ in range(2)]
        dmin_r = [c1(HEADS * TILES) for _ in range(2)]
        rsum1 = c1(HEADS * TILES)
        rinv1 = c1(4, 4, TILES)
        rinv_w = c1(TILES, 128)
        qk1 = [c1(2, TOKENS) for _ in range(2)]
        sq1 = [c1(2, TOKENS) for _ in range(2)]
        qa1 = [c1(TOKENS) for _ in range(2)]
        ka1 = c1(TOKENS)
        km1 = [c1(4, TOKENS) for _ in range(2)]
        v1 = [c1(TILES, 512) for _ in range(2)]
        hs1 = [c1(TOKENS) for _ in range(2)]
        osb1 = [c1(TOKENS) for _ in range(2)]
        on1 = c1(4, TOKENS)
        tmp1 = c1(TOKENS)

        c2 = Carve()
        c2.at = 0
        qk_tab = c2(4, TOKENS)
        PAD = WINDOW + TOKENS
        xs = [c2(PAD) for _ in range(2)]
        ln_at = c2.at
        raw = c2(2 * PAIRS, TOKENS)
        k0 = c2(PAIRS, TOKENS)
        nrm, nrm_c, rinv = c2(TOKENS), c2(TOKENS), c2(TOKENS)
        rq = [c2(TILES, 2, PAIRS) for _ in range(2)]
        qr = [c2(PAIRS, TOKENS) for _ in range(2)]
        kr = [c2(PAIRS, PAD) for _ in range(2)]
        swp = [c2(4, TOKENS) for _ in range(2)]
        vraw = c2(TILES, 2, 512)
        vw_at = c2.at
        vw = [c2(WINDOWS, 512) for _ in range(2)]
        pr = [c2(HEADS, 2 * WINDOW) for _ in range(TILES)]
        mx, rs, rsi = [[c2(HEADS) for _ in range(TILES)] for _ in range(3)]
        pt = [c2(PAIRS, 128) for _ in range(TILES)]
        ow = [p.rearrange("p (c v) j -> p c (v j)", v=2) for p in pr]
        ot = c2(PAIRS, TOKENS)
        c3 = Carve()
        c3.at = vw_at + 512
        gl = [c3(512) for _ in range(FFC)]
        hh = [c3(512) for _ in range(FFC)]

        c4 = Carve()
        c4.at = ln_at
        f_c, f_q, f_s = c4(COLS), c4(COLS), c4(COLS)
        f_sd, f_rs = c4(16), c4(16)

        PS = [ctx.enter_context(nc.psum_tensor(f"ps{i}", [128, 512], f32)) for i in range(8)]
        pb, sbk, tb, ob = PS[0:2], PS[2:4], PS[4:6], PS[6:8]
        wb = PS[0:2] + PS[6:8]

        S = {}

        def sems(*names):
            for n in names:
                S[n] = sem(n)

        sems("in_x", "in_mod", "in_const", "in_w1", "wa_in", "wf_in", "stored")
        sems("silu_e", "silu_done", "mod_mm", "mod_step", "mod_done")
        sems("mean_mm", "cent", "cent_sq", "var_mm", "sd_done", "rstd_done", "rstd_mm", "normed", "affine", "h_in")
        sems("a_qk", "a_qksb", "a_sq", "a_n2", "a_qa", "a_ka", "a_km", "a_sc", "a_cl", "a_sqrt", "a_vmm", "a_vs",
             "b_exp", "b_ri", "b_rw", "b_t", "b_pd", "b_pa", "b_pv", "b_r", "b_o", "b_on", "b_y", "b_tmp", "b_x")
        sems("pads", "tab", "xs_in", "qk_mm", "raw_done", "cos_done", "swp_in0", "swp_in1", "sin_done", "sq_done",
             "add_done", "nrm_mm", "nrm_sd", "nrm_max", "rinv_done", "rq_mm", "rq_done", "kb_mm", "k_done",
             "v_mm", "v_raw", "v_in0", "v_in1",
             "s_mm", "sc_done", "mx_done", "sub_done", "exp_done", "rs_sum", "rs_done", "tr_mm", "tr_out",
             "pv_mm", "o_done", "y_mm", "x_done")
        sems("fs_in", "h_mm", "gl_done", "hh_done", "y2_mm", "xf_done")

        block = ctx.enter_context(nc.Block())

        def batch(t, b):
            return t[:, ds(b * TOKENS, TOKENS)]

        def rep(ap, dim, n):
            ap = ap.unsqueeze(dim)
            shape = list(ap.shape)
            shape[dim] = n
            return ap.broadcast_to(shape)

        class Bank:

            def enter(self, last):
                self.last = last

            def take(self, pe, name, value):
                if self.last:
                    pe.wait_ge(S[self.last[0]], self.last[1])
                self.last = (name, value)

        def ln_pe(pe, k, src, ready, bc, bq, brs):
            ready(pe)
            for n in range(4):
                if n >= 2:
                    pe.wait_ge(S["cent"], 4 * k + n - 1)
                pe.matmul(pb[n % 2][:, :], mean_w, src[:, 512 * n:512 * n + 512], start=True, stop=True)\
                    .then_inc(S["mean_mm"], 1)
            for t in range(16):
                if t % 4 == 0:
                    pe.wait_ge(S["cent_sq"], 4 * k + t // 4 + 1)
                i = pe.matmul(ob[0][:, t:t + 1], bq[:, 128 * t:128 * t + 128], mean_w[:, 0:1], start=True, stop=True)
            i.then_inc(S["var_mm"], 1)
            pe.wait_ge(S["rstd_done"], k + 1)
            for n in range(4):
                if n >= 2:
                    pe.wait_ge(S["normed"], 4 * k + n - 1)
                else:
                    pe.wait_ge(S["cent"], 4 * k + 4)
                for t in range(4):
                    i = pe.matmul(pb[n % 2][:, 128 * t:128 * t + 128],
                                  brs[:, 4 * n + t:4 * n + t + 1].broadcast_to([128, 128]), ident,
                                  start=True, stop=True)
                i.then_inc(S["rstd_mm"], 1)

        def ln_dve(dve, k, src, bc, bsd, brs):
            for n in range(4):
                dve.wait_ge(S["mean_mm"], 4 * k + n + 1)
                c = slice(512 * n, 512 * n + 512)
                dve.tensor_tensor(bc[:, c], src[:, c], pb[n % 2][:, :], ALU.subtract).then_inc(S["cent"], 1)
            dve.wait_ge(S["sd_done"], k + 1)
            dve.reciprocal(brs, bsd).then_inc(S["rstd_done"], 1)
            for n in range(4):
                dve.wait_ge(S["rstd_mm"], 4 * k + n + 1)
                c = slice(512 * n, 512 * n + 512)
                dve.tensor_tensor(bc[:, c], bc[:, c], pb[n % 2][:, :], ALU.mult).then_inc(S["normed"], 1)

        def ln_act(act, k, bc, bq, bsd, dst, scale, bias):
            for n in range(4):
                act.wait_ge(S["cent"], 4 * k + n + 1)
                c = slice(512 * n, 512 * n + 512)
                nc.scalar.activation(bq[:, c], bc[:, c], ACT.Square).then_inc(S["cent_sq"], 1)
            act.wait_ge(S["var_mm"], k + 1)
            nc.scalar.activation(bsd, ob[0][:, 0:16], ACT.Sqrt, bias=eps_col).then_inc(S["sd_done"], 1)
            for b in range(BATCH):
                act.wait_ge(S["normed"], 4 * k + b // 2 + 1)
                c = slice(TOKENS * b, TOKENS * b + TOKENS)
                nc.scalar.activation(dst[:, c], bc[:, c], ACT.Identity, scale=scale(b), bias=bias(b))\
                    .then_inc(S["affine"], 1)

        LN_BUFS = dict(bc=ln_c, bq=ln_q, bsd=ln_sd, brs=ln_rs)
        LN_F = dict(bc=f_c, bq=f_q, bsd=f_sd, brs=f_rs)

        @block.sync
        def _(sp):
            sp.dma_start(xo[:, :], xT).then_inc(S["in_x"], 16)
            sp.dma_start(consts[:, :], c_f32).then_inc(S["in_const"], 16)
            sp.dma_start(cb[:, :], c_bf16).then_inc(S["in_const"], 16)
            sp.dma_start(cs[:, 0:BATCH], cT).then_inc(S["in_mod"], 16)
            sp.dma_start(wm[:, :], wmod).then_inc(S["in_mod"], 16)
            sp.dma_start(arena[:, after_ln:after_ln + 2560], w_att1).then_inc(S["in_w1"], 16)
            sp.dma_start(vec1, v_att1).then_inc(S["in_w1"], 16)
            sp.dma_start(wa[:, :], w_att[0, :, :]).then_inc(S["wa_in"], 16)
            sp.dma_start(wf[:, :], w_ffn[0, :, :]).then_inc(S["wf_in"], 16)

            def waits(*pairs):
                pairs = [(name, sp.to_reg(v)) for name, v in (p for p in pairs if p is not True)]
                for name, v in pairs:
                    sp.wait_ge(S[name], v)

            def move_unit(H, slot, first, first_two):
                U = 2 * H + slot
                for g in range(4):
                    waits(("raw_done", 8 * U + 2 * g + 2),
                          (first and g < 2) or ("add_done", 4 * U + g - 1))
                    for a in range(4):
                        b = 32 * a
                        e = b + 32 if a % 2 == 0 else b - 32
                        sp.dma_start(swp[g % 2][b:b + 32, :, :], raw[e:e + 32, 4 * g:4 * g + 4, :])\
                            .then_inc(S[f"swp_in{g % 2}"], 16)
                waits(("v_raw", 4 * U + 4),
                      first_two or ("pv_mm", 2 * U - 2))
                for v in range(2):
                    for n in range(4):
                        for role in range(2):
                            m = 1 if n + role == 4 else 2
                            a = 64 * v + 32 - 32 * role
                            dst = vw[slot][a:a + 32, n + role:n + role + 4 * m - 3:4, :]
                            sp.dma_start(dst, vraw[32 * n:32 * n + 32, 0:m, v, :]).then_inc(S[f"v_in{slot}"], 16)

            def move_layer(l):
                move_unit(4 * l, 0, True, True)
                move_unit(4 * l, 1, False, True)
                with sp.Fori(1, 4) as h:
                    move_unit(4 * l + h, 0, False, False)
                    move_unit(4 * l + h, 1, False, False)

            with sp.Fori(0, LAYERS - 1) as l:
                move_layer(l)
                sp.wait_ge(S["y_mm"], 8 * l + 8)
                sp.dma_start(wa[:, :], w_att[ds(l + 1, 1), :, :].rearrange("a p n -> (a p) n")).then_inc(S["wa_in"], 16)
                sp.wait_ge(S["xf_done"], 4 * l + 4)
                sp.dma_start(wf[:, :], w_ffn[ds(l + 1, 1), :, :].rearrange("a p n -> (a p) n")).then_inc(S["wf_in"], 16)
            move_layer(LAYERS - 1)
            sp.wait_ge(S["b_x"], 2 * BATCH + BATCH)
            sp.dma_start(out, xo[:, :]).then_inc(S["stored"], 16)
            sp.wait_ge(S["stored"], 16)

        @block.tensor
        def _(pe):
            pe.wait_ge(S["in_mod"], 32)
            pe.wait_ge(S["silu_done"], 3)
            for j in range(6):
                i = pe.matmul(PS[7][:, BATCH * j:BATCH * j + BATCH], wm[:, DIM * j:DIM * j + DIM],
                              cs[:, 3 * BATCH:4 * BATCH], start=True, stop=True)
            i.then_inc(S["mod_mm"], 1)

            def ready0(pe):
                pe.wait_ge(S["in_x"], 16)
                pe.wait_ge(S["in_const"], 32)
                pe.wait_ge(S["mod_done"], 1)
            ln_pe(pe, 0, xo, ready0, ln_c, ln_q, ln_rs)
            pe.wait_ge(S["affine"], 8)
            pe.wait_ge(S["in_w1"], 32)

            def a_qk(U, cc, slot):
                pe.wait_ge(S["a_qksb"], 8 * U + 2 * cc)
                pe.wait_ge(S["a_vs"], 2 * U)
                for j in range(2):
                    i = pe.matmul(pb[0][:, TOKENS * j:TOKENS * j + TOKENS], w1a[:, j, 128 * cc:128 * cc + 128], hs1[slot],
                                  start=True, stop=True)
                i.then_inc(S["a_qk"], 1)

            def a_n2(U, cc):
                pe.wait_ge(S["a_sq"], 4 * U + cc + 1)
                if not isinstance(U, int) or 4 * U + cc > 0:
                    pe.wait_ge(S["a_qa"], 4 * U + cc)
                    pe.wait_ge(S["a_ka"], 4 * U + cc)
                for j, w in enumerate((q2_w, k2_w)):
                    i = pe.matmul(pb[1][:, TOKENS * j:TOKENS * j + TOKENS], w, sq1[cc % 2][:, j, :],
                                  start=True, stop=True)
                i.then_inc(S["a_n2"], 1)

            def a_scores(U, cc, t):
                if t == 0:
                    pe.wait_ge(S["a_qa"], 4 * U + cc + 1)
                    pe.wait_ge(S["a_km"], 16 * U + 4 * cc + 4)
                for p in range(2):
                    i = 4 * cc + 2 * t + p
                    if not isinstance(U, int) or 32 * U + 2 * i - 2 > 0:
                        pe.wait_ge(S["a_cl"], 32 * U + 2 * i - 2)
                    pe.matmul(sbk[i % 2][:, :], qa1[cc % 2][:, 128 * t:128 * t + 128],
                              km1[cc % 2][:, 2 * p:2 * p + 2, :], start=True, stop=True).then_inc(S["a_sc"], 1)

            def a_v(U, t, slot):
                pe.wait_ge(S["a_qksb"], 8 * U + 8)
                if t:
                    pe.wait_ge(S["a_vs"], 2 * U + 1)
                pe.matmul(pb[0][:, :], hs1[slot][:, 128 * t:128 * t + 128], w1a[:, 2, :],
                          start=True, stop=True).then_inc(S["a_vmm"], 1)

            def b_t(U, cc, half, slot):
                for u in (2 * half, 2 * half + 1):
                    h = 4 * cc + u
                    pe.wait_ge(S["b_exp"], 32 * U + 2 * h + 2)
                    q = S["b_pd"] if h % 2 == 0 else S["b_pa"]
                    if not isinstance(U, int) or 8 * U + h // 2 > 0:
                        pe.wait_ge(q, 8 * U + h // 2)
                    for jt in range(TILES):
                        for t in range(TILES):
                            a = 256 * jt + 128 * t
                            i = pe.transpose(tb[h % 2][:, a:a + 128], dist[slot][:, h, t, 128 * jt:128 * jt + 128],
                                             ident)
                    i.then_inc(S["b_t"], 1)

            def b_pv(U, cc, slot):
                pe.wait_ge(S["b_pd"], 8 * U + 2 * cc + 2)
                pe.wait_ge(S["b_pa"], 8 * U + 2 * cc + 2)
                pe.wait_ge(S["a_vs"], 2 * U + 2)
                if not isinstance(U, int) or 4 * U + cc > 0:
                    pe.wait_ge(S["b_o"], 4 * U + cc)
                for jt in range(TILES):
                    for u in range(4):
                        h = 4 * cc + u
                        i = pe.matmul(ob[0][32 * u:32 * u + 32, 0:TOKENS], v1[slot][:, jt, 32 * h:32 * h + 32],
                                      pt1[:, h % 8, jt, :], start=(jt == 0), stop=(jt == 1),
                                      skip_group_check=True)
                i.then_inc(S["b_pv"], 1)
                pe.wait_ge(S["b_rw"], 4 * U + cc + 1)
                if not isinstance(U, int) or 4 * U + cc > 0:
                    pe.wait_ge(S["b_on"], 4 * U + cc)
                    pe.wait_ge(S["b_tmp"], U)
                for t in range(TILES):
                    i = pe.matmul(ob[1][:, 128 * t:128 * t + 128], rinv_w[:, t, :], ident,
                                  start=True, stop=True)
                i.then_inc(S["b_r"], 1)

            def b_y(U):
                pe.wait_ge(S["b_on"], 4 * U + 4)
                for cc in range(4):
                    i = pe.matmul(ob[1][:, 0:TOKENS], wo1[:, cc, :], on1[:, cc, :], start=(cc == 0), stop=(cc == 3))
                i.then_inc(S["b_y"], 1)

            def dist_step(A, B, C, sa):
                def some(part, U, *args):
                    if U is not None:
                        part(U, *args)

                if A is not None:
                    pe.wait_ge(S["h_in"], A + 1)
                some(a_qk, A, 0, sa)
                some(b_t, C, 2, 0, sa)
                some(a_qk, A, 1, sa)
                some(a_n2, A, 0)
                some(b_t, C, 2, 1, sa)
                some(b_pv, C, 1, sa)
                some(a_qk, A, 2, sa)
                some(a_n2, A, 1)
                some(a_scores, A, 0, 0)
                some(b_t, C, 3, 0, sa)
                some(a_qk, A, 3, sa)
                some(a_scores, A, 0, 1)
                some(a_n2, A, 2)
                some(b_t, C, 3, 1, sa)
                some(a_scores, A, 1, 0)
                some(b_pv, C, 2, sa)
                some(a_n2, A, 3)
                some(a_scores, A, 1, 1)
                some(b_t, B, 0, 0, 1 - sa)
                some(a_scores, A, 2, 0)
                some(b_t, B, 0, 1, 1 - sa)
                some(b_pv, C, 3, sa)
                some(a_scores, A, 2, 1)
                some(b_y, C)
                some(a_v, A, 0, sa)
                some(b_t, B, 1, 0, 1 - sa)
                some(a_scores, A, 3, 0)
                some(b_t, B, 1, 1, 1 - sa)
                some(a_v, A, 1, sa)
                some(a_scores, A, 3, 1)
                some(b_pv, B, 0, 1 - sa)

            dist_step(0, None, None, 0)
            dist_step(1, 0, None, 1)
            with pe.Fori(0, 3) as i2:
                dist_step(2 * i2 + 2, 2 * i2 + 1, 2 * i2, 0)
                dist_step(2 * i2 + 3, 2 * i2 + 2, 2 * i2 + 1, 1)
            dist_step(None, 7, 6, 0)
            dist_step(None, None, 7, 1)

            def ready1(pe):
                pe.wait_ge(S["b_x"], 2 * BATCH)
            ln_pe(pe, 1, xo, ready1, ln_c, ln_q, ln_rs)

            banks = [Bank() for _ in wb]

            def qk(U, j):
                w = (wq, wk)[j // 4]
                n = j % 4
                banks[n].take(pe, "raw_done", 8 * U + j + 1)
                for c in range(2):
                    i = pe.matmul(wb[n][:, TOKENS * c:TOKENS * c + TOKENS], w[:, 2 * n + c, :],
                                  xs[cur["sa"]][:, WINDOW:PAD], start=True, stop=True)
                i.then_inc(S["qk_mm"], 1)

            def values(U, n):
                banks[n].take(pe, "v_raw", 4 * U + n + 1)
                a = WINDOW + 128 * (n // 2)
                pe.matmul(wb[n][:, :], xs[cur["sa"]][:, a:a + 128], wv[:, n % 2, :], start=True, stop=True)\
                    .then_inc(S["v_mm"], 1)

            def norms(U, c):
                if c == 0:
                    pe.wait_ge(S["sq_done"], 4 * U + 4)
                    banks[0].take(pe, "nrm_sd", U + 1)
                for g in range(4):
                    i = pe.matmul(pb[0][32 * g:32 * g + 32, 0:TOKENS], slide[:, 30 - 2 * c:62 - 2 * c],
                                  raw[:, 4 * g + c, :], start=(c == 0), stop=(c == 3), skip_group_check=True)
                if c == 3:
                    i.then_inc(S["nrm_mm"], 1)

            def q_norms(U):
                pe.wait_ge(S["rinv_done"], U + 1)
                for t in range(TILES):
                    i = pe.transpose(tb[0][:, 128 * t:128 * t + 128], rinv[:, 128 * t:128 * t + 128], ident)
                i.then_inc(S["rq_mm"], 1)

            def k_norms(U, j):
                banks[j].take(pe, "k_done", 4 * U + j + 1)
                for c in range(2):
                    i = pe.matmul(wb[j][:, TOKENS * c:TOKENS * c + TOKENS], k_sel[:, 2 * j + c, :], rinv,
                                  start=True, stop=True)
                i.then_inc(S["kb_mm"], 1)

            def scores(U, t, slot, quarter):
                if quarter == 0:
                    if t == 0:
                        pe.wait_ge(S["add_done"], 4 * U + 4)
                        pe.wait_ge(S["k_done"], 4 * U + 4)
                        pe.wait_ge(S["rq_done"], U + 1)
                        pe.wait_ge(S[f"v_in{slot}"], 256 * cur["HB"] + 256)
                    if not isinstance(U, int) or 4 * U + 2 * t > 0:
                        pe.wait_ge(S["sc_done"], 4 * U + 2 * t)
                    for v in range(2):
                        pe.matmul(sbk[v][:, :], ident_b, rep(mask_b[t], 1, PAIRS), start=True, stop=False,
                                  skip_group_check=True)
                for c in (2 * quarter, 2 * quarter + 1):
                    for w in range(4):
                        W = 4 * t + w
                        for v in range(2):
                            p = slice(64 * v, 64 * v + 64)
                            i = pe.matmul(sbk[v][32 * w:32 * w + 32, 64 * c:64 * c + 64],
                                          qr[slot][p, c, 32 * W:32 * W + 32], kr[slot][p, c, 32 * W:32 * W + 64],
                                          start=False, stop=(c == PAIRS - 1), skip_group_check=True)
                if quarter == 3:
                    i.then_inc(S["s_mm"], 1)

            def transposes(U, t, step, src):
                for r in range(2):
                    if step:
                        pe.wait_ge(S["tr_out"], 8 * U + 2 * step + r - 1)
                    for c in range(4):
                        i = pe.transpose(tb[r][:, 128 * c:128 * c + 128], src[:, 4 * r + c, :], ident)
                    i.then_inc(S["tr_mm"], 1)

            def p_t(U, t):
                pe.wait_ge(S["exp_done"], 2 * U + t + 1)
                if t == 0:
                    pe.wait_ge(S["rq_done"], U + 1)
                transposes(U, t, (0, 1)[t], pr[t].rearrange("p (c v) j -> p c (v j)", v=2))

            def o_t(U, t):
                pe.wait_ge(S["o_done"], 4 * U + 2 * t + 2)
                transposes(U, t, (2, 3)[t], ow[t])

            def pv(U, t, slot, quarter):
                for c in (2 * quarter, 2 * quarter + 1):
                    for w in range(4):
                        for v in range(2):
                            p = slice(64 * v, 64 * v + 64)
                            i = pe.matmul(sbk[v][32 * w:32 * w + 32, 64 * c:64 * c + 64],
                                          pt[t][p, c, 32 * w:32 * w + 32],
                                          vw[slot][p, 4 * t + w, 64 * c:64 * c + 64], start=True, stop=True,
                                          skip_group_check=True)
                if quarter == 3:
                    i.then_inc(S["pv_mm"], 1)

            def out_proj(U):
                pe.wait_ge(S["tr_out"], 8 * U + 8)
                banks[3].take(pe, "x_done", U + 1)
                for c in range(PAIRS):
                    i = pe.matmul(wb[3][:, 0:TOKENS], wo[:, c, :], ot[:, c, :], start=(c == 0), stop=(c == PAIRS - 1))
                i.then_inc(S["y_mm"], 1)

            cur = {}

            def win_unit(HA, sa, HB, sb_):
                A, B = HA is not None, HB is not None
                UA, UB = 2 * HA + sa if A else None, 2 * HB + sb_ if B else None
                cur["sa"], cur["HB"] = sa, HB
                ua = UA if A else UB + 1
                for n in range(4):
                    banks[n].enter(("k_done", 4 * ua - 3 + n) if B else None)
                if A:
                    pe.wait_ge(S["xs_in"], 2 * UA + 2)
                def some(part, U, *steps):
                    if U is not None:
                        for n in steps:
                            part(U, n)

                def sc(t, *quarters):
                    if B:
                        for n in quarters:
                            scores(UB, t, sb_, n)

                def out(t, *quarters):
                    if B:
                        for n in quarters:
                            pv(UB, t, sb_, n)

                some(values, UA, 0)
                sc(0, 0, 1)
                some(qk, UA, 0)
                sc(0, 2, 3)
                some(qk, UA, 1)
                sc(1, 0, 1)
                some(qk, UA, 2)
                sc(1, 2, 3)
                some(qk, UA, 3, 4, 5, 6)
                some(p_t, UB, 0)
                some(qk, UA, 7)
                some(p_t, UB, 1)
                some(values, UA, 1)
                out(0, 0, 1)
                some(values, UA, 2)
                out(0, 2, 3)
                some(values, UA, 3)
                some(o_t, UB, 0)
                out(1, 0, 1)
                some(norms, UA, 0, 1)
                out(1, 2, 3)
                some(norms, UA, 2, 3)
                if B:
                    o_t(UB, 1)
                    out_proj(UB)
                if A:
                    if B:
                        pe.wait_ge(S["tr_out"], 8 * UB + 8)
                    q_norms(UA)
                    for j in range(4):
                        k_norms(UA, j)

            with pe.Fori(0, LAYERS) as l:
                pe.wait_ge(S["wa_in"], 16 * l + 16)
                win_unit(4 * l, 0, None, None)
                with pe.Fori(0, 3) as h:
                    H = 4 * l + h
                    win_unit(H, 1, H, 0)
                    win_unit(H + 1, 0, H, 1)
                win_unit(4 * l + 3, 1, 4 * l + 3, 0)
                win_unit(None, None, 4 * l + 3, 1)

                def ready2(pe):
                    pe.wait_ge(S["fs_in"], 3 * l + 3)
                ln_pe(pe, l + 2, f_s, ready2, f_c, f_q, f_rs)
                hb = PS[2:8]
                pe.wait_ge(S["wf_in"], 16 * l + 16)

                def hidden(n):
                    pe.wait_ge(S["affine"], 8 * (l + 2) + 2 * n + 2)
                    for j in range(FFC):
                        m = FFP[j]
                        for g in range(2):
                            if n:
                                pe.wait_ge(S["hh_done"], 12 * l + 3 * (n - 1) + j + 1)
                            c = FF * g + 128 * j
                            pe.matmul(hb[2 * j + g][0:m, :], w1[:, c:c + m], f_q[:, 512 * n:512 * n + 512],
                                      start=True, stop=True).then_inc(S["h_mm"], 1)

                def down(n):
                    if n >= 2:
                        pe.wait_ge(S["xf_done"], 4 * l + n - 1)
                    for j in range(FFC):
                        m = FFP[j]
                        pe.wait_ge(S["hh_done"], 12 * l + 3 * n + j + 1)
                        i = pe.matmul(pb[n % 2][:, :], w2[0:m, j, :], hh[j][0:m, :], start=(j == 0), stop=(j == FFC - 1))
                    i.then_inc(S["y2_mm"], 1)

                hidden(0)
                for n in range(4):
                    down(n)
                    if n < 3:
                        hidden(n + 1)

        @block.vector
        def _(dve):
            chain = [0]

            def step(ins):
                chain[0] += 1
                ins.then_inc(S["mod_step"], 1)
                dve.wait_ge(S["mod_step"], chain[0])

            dve.wait_ge(S["silu_e"], 1)
            c = [cs[:, BATCH * j:BATCH * j + BATCH] for j in range(4)]
            dve.tensor_scalar(c[2], c[1], 1.0, None, ALU.add).then_inc(S["silu_done"], 1)
            dve.wait_ge(S["silu_done"], 1)
            dve.reciprocal(c[1], c[2]).then_inc(S["silu_done"], 1)
            dve.wait_ge(S["silu_done"], 2)
            dve.tensor_tensor(c[3], c[0], c[1], ALU.mult).then_inc(S["silu_done"], 1)
            dve.wait_ge(S["mod_mm"], 1)
            step(nc.vector.tensor_copy(mod[:, :, :], PS[7][:, 0:6 * BATCH].rearrange("p (j b) -> p j b", j=6)))
            for j in (1, 4):
                step(nc.vector.tensor_scalar(mod[:, j, :], mod[:, j, :], 1.0, None, ALU.add))
            for j in (2, 5):
                g = mod[:, j, :]
                step(nc.vector.tensor_scalar(mod_t[:, 0, :], g, 0.0, 2.0, ALU.is_ge, ALU.mult))
                step(nc.vector.tensor_scalar(mod_t[:, 1, :], g, -1.0, None, ALU.mult))
                step(nc.vector.tensor_tensor(mod_t[:, 2, :], mod_t[:, 1, :], g, ALU.max))
                step(nc.vector.tensor_scalar(mod_t[:, 1, :], mod_t[:, 2, :], 0.25, None, ALU.max))
                step(nc.vector.tensor_scalar(mod_t[:, 2, :], mod_t[:, 0, :], -1.0, None, ALU.add))
                step(nc.vector.tensor_tensor(g, mod_t[:, 1, :], mod_t[:, 2, :], ALU.mult))
            nc.vector.tensor_copy(mod_t[:, 0, :], mod[:, 2, :]).then_inc(S["mod_done"], 1)
            dve.wait_ge(S["in_x"], 16)
            ln_dve(dve, 0, xo, ln_c, ln_sd, ln_rs)
            dve.wait_ge(S["in_w1"], 32)
            dve.wait_ge(S["in_const"], 32)

            def a_qksb(U, cc):
                dve.wait_ge(S["a_qk"], 4 * U + cc + 1)
                if not isinstance(U, int) or 4 * U + cc >= 2:
                    dve.wait_ge(S["a_sq"], 4 * U + cc - 1)
                nc.vector.tensor_scalar(qk1[cc % 2][:, 0, :], pb[0][:, 0:TOKENS], vec1[:, cc:cc + 1], -2.0,
                                        ALU.add, ALU.mult).then_inc(S["a_qksb"], 1)
                nc.vector.tensor_scalar(qk1[cc % 2][:, 1, :], pb[0][:, TOKENS:2 * TOKENS], vec1[:, 4 + cc:5 + cc], None,
                                        ALU.add).then_inc(S["a_qksb"], 1)

            def a_aug(U, cc):
                n = 4 * U + cc
                dve.wait_ge(S["a_n2"], n + 1)
                dve.wait_ge(S["a_qksb"], 2 * n + 2)
                if not isinstance(U, int) or n >= 2:
                    dve.wait_ge(S["a_sc"], 4 * n - 4)
                nc.vector.scalar_tensor_tensor(out=qa1[cc % 2], in0=pb[1][:, 0:TOKENS], scalar=one9,
                                               in1=qk1[cc % 2][:, 0, :], op0=ALU.add, op1=ALU.add)\
                    .then_inc(S["a_qa"], 1)
                if not isinstance(U, int) or n > 0:
                    dve.wait_ge(S["a_km"], 4 * n)
                nc.vector.scalar_tensor_tensor(out=ka1, in0=pb[1][:, TOKENS:2 * TOKENS], scalar=one8,
                                               in1=qk1[cc % 2][:, 1, :], op0=ALU.add, op1=ALU.add)\
                    .then_inc(S["a_ka"], 1)
                dve.wait_ge(S["a_ka"], n + 1)
                for u in range(4):
                    nc.vector.tensor_scalar(km1[cc % 2][:, u, :], ka1, head_sel[:, u:u + 1], None, ALU.mult)\
                        .then_inc(S["a_km"], 1)

            def a_clamp(U, cc, t, slot):
                if t == 0 and (not isinstance(U, int) or U >= 2):
                    dve.wait_ge(S["b_t"], 16 * U + 4 * cc - 28)
                for p in range(2):
                    i = 4 * cc + 2 * t + p
                    dve.wait_ge(S["a_sc"], 16 * U + i + 1)
                    for q in range(2):
                        h = 4 * cc + 2 * p + q
                        k = 2 * h + t
                        nc.vector.tensor_scalar(dist[slot][:, h, t, :], sbk[i % 2][:, TOKENS * q:TOKENS * q + TOKENS],
                                                1e-12, None, ALU.max, ALU.min,
                                                accum_out=dmin[slot][:, k:k + 1]).then_inc(S["a_cl"], 1)

            def a_vs(U, t, slot):
                dve.wait_ge(S["a_vmm"], 2 * U + t + 1)
                if not isinstance(U, int) or U >= 2:
                    dve.wait_ge(S["b_pv"], 4 * U - 4)
                nc.vector.tensor_tensor(v1[slot][:, t, :], pb[0][:, :], bv1, ALU.add).then_inc(S["a_vs"], 1)

            def b_pd(U, cc, half):
                for u in (2 * half,):
                    h = 4 * cc + u
                    dve.wait_ge(S["b_t"], 16 * U + h + 1)
                    if u == 0 and (not isinstance(U, int) or 4 * U + cc >= 2):
                        dve.wait_ge(S["b_pv"], 4 * U + cc - 1)
                    nc.vector.tensor_copy(pt1[:, h % 8, :, :], tb[0][:, :].rearrange("p (a t) -> p a t", a=2))\
                        .then_inc(S["b_pd"], 1)

            def b_ri(U, cc):
                dve.wait_ge(S["b_exp"], 32 * U + 8 * cc + 8)
                nc.vector.reciprocal(rinv1[:, cc, :, :], rsum1[:, 8 * cc:8 * cc + 8].rearrange("p (u t) -> p u t", u=4))\
                    .then_inc(S["b_ri"], 1)

            def b_on(U, cc):
                dve.wait_ge(S["b_o"], 4 * U + cc + 1)
                dve.wait_ge(S["b_r"], 4 * U + cc + 1)
                dve.wait_ge(S["b_y"], U)
                nc.vector.tensor_tensor(on1[:, cc, :], osb1[cc % 2], ob[1][:, 0:TOKENS], ALU.mult).then_inc(S["b_on"], 1)

            def b_x(U):
                dve.wait_ge(S["b_y"], U + 1)
                dve.wait_ge(S["b_x"], 2 * U)
                nc.vector.tensor_scalar(tmp1, ob[1][:, 0:TOKENS], vec1[:, 8:9], None, ALU.add).then_inc(S["b_tmp"], 1)
                dve.wait_ge(S["b_tmp"], U + 1)
                nc.vector.tensor_tensor(tmp1, tmp1, mod[:, 2, ds(U, 1)].broadcast_to([128, TOKENS]), ALU.mult)\
                    .then_inc(S["b_x"], 1)
                dve.wait_ge(S["b_x"], 2 * U + 1)
                nc.vector.tensor_tensor(batch(xo, U), batch(xo, U), tmp1, ALU.add).then_inc(S["b_x"], 1)

            def dist_step(A, B, C, sa):
                def some(part, U, *args):
                    if U is not None:
                        part(U, *args)

                some(a_qksb, A, 0)
                some(b_ri, C, 2)
                some(b_pd, C, 2, 0)
                some(a_qksb, A, 1)
                some(a_aug, A, 0)
                some(b_pd, C, 2, 1)
                some(b_ri, C, 3)
                some(a_qksb, A, 2)
                some(a_aug, A, 1)
                some(b_on, C, 1)
                some(a_clamp, A, 0, 0, sa)
                some(b_pd, C, 3, 0)
                some(a_qksb, A, 3)
                some(a_clamp, A, 0, 1, sa)
                some(a_aug, A, 2)
                some(b_pd, C, 3, 1)
                some(a_clamp, A, 1, 0, sa)
                some(b_on, C, 2)
                some(a_clamp, A, 1, 1, sa)
                some(a_aug, A, 3)
                some(b_ri, B, 0)
                some(b_pd, B, 0, 0)
                some(a_clamp, A, 2, 0, sa)
                some(b_pd, B, 0, 1)
                some(b_on, C, 3)
                some(a_clamp, A, 2, 1, sa)
                some(b_x, C)
                some(a_vs, A, 0, sa)
                some(b_ri, B, 1)
                some(b_pd, B, 1, 0)
                some(a_clamp, A, 3, 0, sa)
                some(b_pd, B, 1, 1)
                some(a_vs, A, 1, sa)
                some(a_clamp, A, 3, 1, sa)
                some(b_on, B, 0)

            dist_step(0, None, None, 0)
            dist_step(1, 0, None, 1)
            with dve.Fori(0, 3) as i2:
                dist_step(2 * i2 + 2, 2 * i2 + 1, 2 * i2, 0)
                dist_step(2 * i2 + 3, 2 * i2 + 2, 2 * i2 + 1, 1)
            dist_step(None, 7, 6, 0)
            dist_step(None, None, 7, 1)
            dve.wait_ge(S["b_x"], 2 * BATCH)
            ln_dve(dve, 1, xo, ln_c, ln_sd, ln_rs)

            dve.wait_ge(S["affine"], 16)
            for s in range(2):
                for v in range(2):
                    nc.vector.memset(vw[s][64 * v:64 * v + 32, 0, :], 0.0).then_inc(S["pads"], 1)

            def rot_dst(slot, g):
                return qr[slot][:, 4 * g:4 * g + 4, :] if g < 2 else k0[:, 4 * g - 8:4 * g - 4, :]

            def cos_part(U, g, slot, prologue):
                dve.wait_ge(S["raw_done"], 8 * U + 2 * g + 2)
                if g == 0 and not prologue:
                    dve.wait_ge(S["s_mm"], 2 * U - 2)
                if g == 2 and not prologue:
                    dve.wait_ge(S["k_done"], 4 * U)
                nc.vector.tensor_tensor(rot_dst(slot, g), raw[:, 4 * g:4 * g + 4, :],
                                        rep(qk_tab[:, 2 * (g // 2), :], 1, 4), ALU.mult).then_inc(S["cos_done"], 1)

            def sin_part(H, slot, g):
                dve.wait_ge(S[f"swp_in{g % 2}"], 256 * H + 128 * slot + 64 * (g // 2) + 64)
                s = swp[g % 2]
                nc.vector.tensor_tensor(s, s, rep(qk_tab[:, 2 * (g // 2) + 1, :], 1, 4), ALU.mult)\
                    .then_inc(S["sin_done"], 1)

            def norm_inv(U):
                dve.wait_ge(S["nrm_sd"], U + 1)
                nc.vector.tensor_scalar(nrm_c, nrm, 1e-12, None, ALU.max).then_inc(S["nrm_max"], 1)
                dve.wait_ge(S["nrm_max"], U + 1)
                nc.vector.reciprocal(rinv, nrm_c).then_inc(S["rinv_done"], 1)

            def q_inv(U, slot):
                dve.wait_ge(S["rq_mm"], U + 1)
                nc.vector.tensor_scalar(rq[slot], tb[0][:, 0:256].rearrange("p (t g n) -> p t g n", t=2, g=4)[:, :, 0:2, 0:8],
                                        QK_SCALE, None, ALU.mult).then_inc(S["rq_done"], 1)

            def k_scale(U, j, slot):
                dve.wait_ge(S["kb_mm"], 4 * U + j + 1)
                dve.wait_ge(S["add_done"], 4 * U + 3 + j // 2)
                nc.vector.tensor_tensor(kr[slot][:, 2 * j:2 * j + 2, WINDOW:PAD], k0[:, 2 * j:2 * j + 2, :],
                                        wb[j][:, :].rearrange("p (c t) -> p c t", c=2), ALU.mult)\
                    .then_inc(S["k_done"], 1)

            def scale_max(U, t, slot):
                dve.wait_ge(S["s_mm"], 2 * U + t + 1)
                p = pr[t].rearrange("p (c v) j -> p c v j", v=2)
                q = rq[slot].rearrange("p t g n -> p t (g n)")[:, t, :].rearrange("p (c v) -> p c v", v=2)
                for v in range(2):
                    nc.vector.tensor_tensor(p[:, :, v, :], sbk[v][:, :].rearrange("p (c j) -> p c j", c=PAIRS),
                                            rep(q[:, :, v], 2, 2 * WINDOW), ALU.mult).then_inc(S["sc_done"], 1)
                dve.wait_ge(S["sc_done"], 4 * U + 2 * t + 2)
                nc.vector.tensor_reduce(mx[t], pr[t], X, ALU.max).then_inc(S["mx_done"], 1)

            def row_sums(U, t):
                dve.wait_ge(S["exp_done"], 2 * U + t + 1)
                nc.vector.tensor_reduce(rs[t], pr[t], X, ALU.add).then_inc(S["rs_sum"], 1)
                dve.wait_ge(S["rs_sum"], 2 * U + t + 1)
                nc.vector.reciprocal(rsi[t], rs[t]).then_inc(S["rs_done"], 1)

            def o_norm(U, t):
                dve.wait_ge(S["pv_mm"], 2 * U + t + 1)
                dve.wait_ge(S["rs_done"], 2 * U + t + 1)
                o4 = ow[t].rearrange("p c (v n) -> p c v n", v=2)
                r3 = rsi[t].rearrange("p (c v) -> p c v", v=2)
                for v in range(2):
                    nc.vector.tensor_tensor(o4[:, :, v, :], sbk[v][:, :].rearrange("p (c n) -> p c n", c=PAIRS),
                                            rep(r3[:, :, v], 2, DH), ALU.mult).then_inc(S["o_done"], 1)

            def residual(U, b):
                dve.wait_ge(S["y_mm"], U + 1)
                nc.vector.tensor_tensor(batch(xi, b), wb[3][:, 0:TOKENS], batch(xi, b), ALU.add).then_inc(S["x_done"], 1)

            def win_unit(HA, sa, HB, sb_, b):
                A, B = HA is not None, HB is not None
                UA, UB = 2 * HA + sa if A else None, 2 * HB + sb_ if B else None
                pro = not B
                if B:
                    scale_max(UB, 0, sb_)
                    scale_max(UB, 1, sb_)
                if A:
                    cos_part(UA, 0, sa, pro)
                    cos_part(UA, 1, sa, pro)
                if B:
                    row_sums(UB, 0)
                if A:
                    sin_part(HA, sa, 0)
                if B:
                    row_sums(UB, 1)
                if A:
                    sin_part(HA, sa, 1)
                    cos_part(UA, 2, sa, pro)
                if B:
                    o_norm(UB, 0)
                if A:
                    cos_part(UA, 3, sa, pro)
                    sin_part(HA, sa, 2)
                if B:
                    o_norm(UB, 1)
                if A:
                    sin_part(HA, sa, 3)
                    norm_inv(UA)
                if B:
                    residual(UB, b)
                if A:
                    q_inv(UA, sa)
                    if not pro:
                        dve.wait_ge(S["s_mm"], 2 * UA - 2)
                    for j in range(4):
                        k_scale(UA, j, sa)

            with dve.Fori(0, LAYERS) as l:
                dve.wait_ge(S["tab"], 4 * l + 4)
                win_unit(4 * l, 0, None, None, None)
                with dve.Fori(0, 3) as h:
                    H = 4 * l + h
                    win_unit(H, 1, H, 0, 2 * h)
                    win_unit(H + 1, 0, H, 1, 2 * h + 1)
                win_unit(4 * l + 3, 1, 4 * l + 3, 0, 6)
                win_unit(None, None, 4 * l + 3, 1, 7)
                dve.wait_ge(S["fs_in"], 3 * l + 3)
                ln_dve(dve, l + 2, f_s, f_c, f_sd, f_rs)
                dve.wait_ge(S["wf_in"], 16 * l + 16)

                def gate(n):
                    for j in range(FFC):
                        m = FFP[j]
                        dve.wait_ge(S["gl_done"], 12 * l + 3 * n + j + 1)
                        dve.wait_ge(S["h_mm"], 24 * l + 6 * n + 2 * j + 1)
                        if n:
                            dve.wait_ge(S["y2_mm"], 4 * l + n)
                        nc.vector.scalar_tensor_tensor(out=hh[j][0:m, :], in0=PS[2 + 2 * j][0:m, :], scalar=b1a[0:m, j:j + 1],
                                                       in1=gl[j][0:m, :], op0=ALU.add, op1=ALU.mult)\
                            .then_inc(S["hh_done"], 1)

                for n in range(4):
                    gate(n)
                    dve.wait_ge(S["y2_mm"], 4 * l + n + 1)
                    c = slice(512 * n, 512 * n + 512)
                    nc.vector.scalar_tensor_tensor(out=xi[:, c], in0=pb[n % 2][:, :], scalar=b2, in1=xi[:, c],
                                                   op0=ALU.add, op1=ALU.add).then_inc(S["xf_done"], 1)
            dve.wait_ge(S["xf_done"], 4 * LAYERS)
            for b in range(BATCH):
                c = slice(TOKENS * b, TOKENS * b + TOKENS)
                nc.vector.scalar_tensor_tensor(out=xo[:, c], in0=xi[:, c], scalar=mod[:, 5, b:b + 1], in1=xo[:, c],
                                               op0=ALU.mult, op1=ALU.add).then_inc(S["b_x"], 1)

        @block.scalar
        def _(act):
            act.wait_ge(S["in_mod"], 32)
            nc.scalar.activation(cs[:, BATCH:2 * BATCH], cs[:, 0:BATCH], ACT.Exp, scale=-1.0).then_inc(S["silu_e"], 1)
            act.wait_ge(S["in_const"], 32)
            act.wait_ge(S["mod_done"], 1)
            ln_act(act, 0, ln_c, ln_q, ln_sd, h1, lambda b: mod[:, 1, b:b + 1], lambda b: mod[:, 0, b:b + 1])
            act.wait_ge(S["affine"], 8)

            def a_h(U, slot):
                if not isinstance(U, int) or U >= 2:
                    act.wait_ge(S["a_vmm"], 2 * U - 2)
                nc.scalar.activation(hs1[slot], batch(h1, U), ACT.Copy).then_inc(S["h_in"], 1)

            def a_sq(U, cc):
                n = 4 * U + cc
                act.wait_ge(S["a_qksb"], 2 * n + 2)
                if not isinstance(U, int) or n >= 2:
                    act.wait_ge(S["a_n2"], n - 1)
                nc.scalar.activation(sq1[cc % 2], qk1[cc % 2], ACT.Square).then_inc(S["a_sq"], 1)

            def a_sqrt(U, slot, first, last):
                for cc in range(first, last):
                    act.wait_ge(S["a_cl"], 32 * U + 8 * cc + 8)
                    d = dist[slot][:, 4 * cc:4 * cc + 4, :, :]
                    nc.scalar.activation(d, d, ACT.Sqrt).then_inc(S["a_sqrt"], 1)
                if last == 4:
                    nc.scalar.activation(dmin_r[slot], dmin[slot], ACT.Sqrt).then_inc(S["a_sqrt"], 1)

            def b_exp(U, h, slot):
                if h == 0:
                    act.wait_ge(S["a_sqrt"], 5 * U + 5)
                    if not isinstance(U, int) or U > 0:
                        act.wait_ge(S["b_ri"], 4 * U)
                for t in range(TILES):
                    k = 2 * h + t
                    d = dist[slot][:, h, t, :]
                    nc.scalar.activation(d, d, ACT.Exp, scale=-1.0, bias=dmin_r[slot][:, k:k + 1],
                                         accum_out=rsum1[:, k:k + 1]).then_inc(S["b_exp"], 1)

            def b_pa(U, h):
                    act.wait_ge(S["b_t"], 16 * U + h + 1)
                    if h % 4 == 1 and (not isinstance(U, int) or 4 * U + h // 4 >= 2):
                        act.wait_ge(S["b_pv"], 4 * U + h // 4 - 1)
                    nc.scalar.activation(pt1[:, h % 8, :, :], tb[1][:, :].rearrange("p (a t) -> p a t", a=2), ACT.Copy)\
                        .then_inc(S["b_pa"], 1)

            def b_o(U, cc):
                act.wait_ge(S["b_pv"], 4 * U + cc + 1)
                if not isinstance(U, int) or 4 * U + cc >= 2:
                    act.wait_ge(S["b_on"], 4 * U + cc - 1)
                nc.scalar.activation(osb1[cc % 2], ob[0][:, 0:TOKENS], ACT.Copy).then_inc(S["b_o"], 1)

            def dist_step(A, B, C, sa):
                def some(part, U, *args):
                    if U is not None:
                        part(U, *args)

                def exp(*heads):
                    for h in heads:
                        some(b_exp, B, h, 1 - sa)

                def pa(U, *heads):
                    for h in heads:
                        some(b_pa, U, h)

                if sa == 0:
                    some(a_h, A, 0)
                some(a_sq, A, 0)
                pa(C, 9)
                some(a_sqrt, B, 1 - sa, 0, 1)
                some(a_sq, A, 1)
                pa(C, 11)
                some(a_sq, A, 2)
                some(b_o, C, 1)
                some(a_sqrt, B, 1 - sa, 1, 2)
                pa(C, 13)
                some(a_sq, A, 3)
                some(a_sqrt, B, 1 - sa, 2, 3)
                pa(C, 15)
                some(a_sqrt, B, 1 - sa, 3, 4)
                exp(0, 1)
                some(b_o, C, 2)
                exp(2, 3, 4)
                pa(B, 1)
                exp(5, 6)
                pa(B, 3)
                some(b_o, C, 3)
                exp(7, 8, 9)
                pa(B, 5)
                exp(10, 11)
                pa(B, 7)
                exp(12, 13)
                some(b_o, B, 0)
                exp(14, 15)
                if sa == 0 and A is not None:
                    a_h(A + 1, 1)

            dist_step(0, None, None, 0)
            dist_step(1, 0, None, 1)
            with act.Fori(0, 3) as i2:
                dist_step(2 * i2 + 2, 2 * i2 + 1, 2 * i2, 0)
                dist_step(2 * i2 + 3, 2 * i2 + 2, 2 * i2 + 1, 1)
            dist_step(None, 7, 6, 0)
            dist_step(None, None, 7, 1)
            ln_act(act, 1, ln_c, ln_q, ln_sd, xi, lambda b: mod[:, 4, b:b + 1], lambda b: mod[:, 3, b:b + 1])

            def shift_in(U, b, slot, prologue):
                if not prologue:
                    act.wait_ge(S["qk_mm"], 8 * U - 8)
                nc.scalar.activation(xs[slot][0:64, WINDOW:PAD], xi[0:64, ds(b * TOKENS, TOKENS)], ACT.Copy)\
                    .then_inc(S["xs_in"], 1)
                nc.scalar.activation(xs[slot][64:128, WINDOW + 1:PAD], xi[64:128, ds(b * TOKENS, TOKENS - 1)], ACT.Copy)\
                    .then_inc(S["xs_in"], 1)

            def v_out(H, n, slot, prologue):
                U = 2 * H + slot
                act.wait_ge(S["v_mm"], 4 * U + n + 1)
                if n == 0 and not prologue:
                    act.wait_ge(S[f"v_in{1 - slot}"], 256 * H + 256 * slot)
                nc.scalar.activation(vraw[:, n // 2, n % 2, :], wb[n][:, :], ACT.Copy).then_inc(S["v_raw"], 1)

            def raw_out(U, j, prologue):
                act.wait_ge(S["qk_mm"], 8 * U + j + 1)
                if j == 0 and not prologue:
                    act.wait_ge(S["nrm_mm"], U)
                nc.scalar.activation(raw[:, 2 * j:2 * j + 2, :], wb[j % 4][:, :].rearrange("p (c t) -> p c t", c=2),
                                     ACT.Copy).then_inc(S["raw_done"], 1)

            def squares(H, slot, g):
                act.wait_ge(S["cos_done"], 4 * (2 * H + slot) + g + 1)
                act.wait_ge(S[f"swp_in{g % 2}"], 256 * H + 128 * slot + 64 * (g // 2) + 64)
                r4 = raw[:, 4 * g:4 * g + 4, :]
                nc.scalar.activation(r4, r4, ACT.Square).then_inc(S["sq_done"], 1)

            def norm_sqrt(U):
                act.wait_ge(S["nrm_mm"], U + 1)
                act.wait_ge(S["nrm_max"], U)
                nc.scalar.activation(nrm, pb[0][:, 0:TOKENS], ACT.Sqrt).then_inc(S["nrm_sd"], 1)

            def exps(U, t):
                act.wait_ge(S["sub_done"], 2 * U + t + 1)
                nc.scalar.activation(pr[t], pr[t], ACT.Exp).then_inc(S["exp_done"], 1)

            def tr_out(U, t, step, dst):
                for r in range(2):
                    act.wait_ge(S["tr_mm"], 8 * U + 2 * step + r + 1)
                    nc.scalar.activation(dst[:, 4 * r:4 * r + 4, :], tb[r][:, :].rearrange("p (c t) -> p c t", c=4),
                                         ACT.Copy).then_inc(S["tr_out"], 1)

            def p_out(U, t):
                tr_out(U, t, t, pt[t])

            def o_out(U, t):
                if t == 0:
                    act.wait_ge(S["y_mm"], U)
                tr_out(U, t, 2 + t, ot[:, :, 128 * t:128 * t + 128])

            def win_unit(HA, sa, HB, sb_, b):
                A, B = HA is not None, HB is not None
                UA, UB = 2 * HA + sa if A else None, 2 * HB + sb_ if B else None
                pro = not B
                if A:
                    shift_in(UA, b, sa, pro)
                    v_out(HA, 0, sa, pro)
                    raw_out(UA, 0, pro)
                    raw_out(UA, 1, pro)
                    raw_out(UA, 2, pro)
                if B:
                    exps(UB, 0)
                if A:
                    raw_out(UA, 3, pro)
                    raw_out(UA, 4, pro)
                    raw_out(UA, 5, pro)
                    raw_out(UA, 6, pro)
                    squares(HA, sa, 0)
                    raw_out(UA, 7, pro)
                if B:
                    exps(UB, 1)
                    p_out(UB, 0)
                    p_out(UB, 1)
                if A:
                    v_out(HA, 1, sa, pro)
                    squares(HA, sa, 1)
                    v_out(HA, 2, sa, pro)
                    v_out(HA, 3, sa, pro)
                    squares(HA, sa, 2)
                if B:
                    o_out(UB, 0)
                if A:
                    squares(HA, sa, 3)
                    norm_sqrt(UA)
                if B:
                    o_out(UB, 1)

            act.wait_ge(S["affine"], 16)
            act.wait_ge(S["pads"], 8)
            with act.Fori(0, LAYERS) as l:
                act.wait_ge(S["xf_done"], 4 * l)
                win_unit(4 * l, 0, None, None, 0)
                with act.Fori(0, 3) as h:
                    H = 4 * l + h
                    win_unit(H, 1, H, 0, 2 * h + 1)
                    win_unit(H + 1, 0, H, 1, 2 * h + 2)
                win_unit(4 * l + 3, 1, 4 * l + 3, 0, 7)
                win_unit(None, None, 4 * l + 3, 1, None)
                act.wait_ge(S["x_done"], 8 * l + 8)
                s3 = f_s.rearrange("p (b t) -> p b t", b=BATCH)
                x3 = xi[:, :].rearrange("p (b t) -> p b t", b=BATCH)
                nc.scalar.activation(s3[0:64, :, :], x3[0:64, :, :], ACT.Copy).then_inc(S["fs_in"], 1)
                nc.scalar.activation(s3[64:128, :, 1:TOKENS], x3[64:128, :, 0:TOKENS - 1], ACT.Copy).then_inc(S["fs_in"], 1)
                nc.scalar.activation(s3[64:128, :, 0:1], xs[0][64:128, 0:BATCH].unsqueeze(2), ACT.Copy).then_inc(S["fs_in"], 1)
                act.wait_ge(S["wf_in"], 16 * l + 16)
                ln_act(act, l + 2, f_c, f_q, f_sd, f_q, lambda b: ln_g, lambda b: ln_b)
                for n in range(4):
                    for j in range(FFC):
                        m = FFP[j]
                        act.wait_ge(S["h_mm"], 24 * l + 6 * n + 2 * j + 2)
                        if n:
                            act.wait_ge(S["hh_done"], 12 * l + 3 * (n - 1) + j + 1)
                        nc.scalar.activation(gl[j][0:m, :], PS[3 + 2 * j][0:m, :], ACT.Gelu, bias=b1g[0:m, j:j + 1])\
                            .then_inc(S["gl_done"], 1)

        @block.gpsimd
        def _(pool):
            def b_rw(U, cc):
                pool.wait_ge(S["b_ri"], 4 * U + cc + 1)
                pool.wait_ge(S["b_r"], 4 * U + cc)
                nc.gpsimd.tensor_tensor(rinv_w.rearrange("p t (u n) -> p t u n", u=4),
                                        rep(rinv1[:, cc, :, :].rearrange("p u t -> p t u"), 3, 32),
                                        ones_w.rearrange("p (t u n) -> p t u n", t=1, u=4).broadcast_to([128, TILES, 4, 32]),
                                        ALU.mult).then_inc(S["b_rw"], 1)

            with pool.Fori(0, BATCH) as U:
                for cc in range(4):
                    b_rw(U, cc)

            pool.wait_ge(S["affine"], 16)
            for s in range(2):
                nc.gpsimd.memset(xs[s][:, 0:WINDOW + 1], 0.0).then_inc(S["pads"], 1)
                nc.gpsimd.memset(kr[s][:, :, 0:WINDOW], 0.0).then_inc(S["pads"], 1)

            def add(U, g, slot):
                pool.wait_ge(S["cos_done"], 4 * U + g + 1)
                pool.wait_ge(S["sin_done"], 4 * U + g + 1)
                dst = qr[slot][:, 4 * g:4 * g + 4, :] if g < 2 else k0[:, 4 * g - 8:4 * g - 4, :]
                nc.gpsimd.tensor_tensor(dst, dst, swp[g % 2], ALU.add).then_inc(S["add_done"], 1)

            def sub(U, t):
                pool.wait_ge(S["mx_done"], 2 * U + t + 1)
                nc.gpsimd.tensor_tensor(pr[t], pr[t], rep(mx[t], 2, 2 * WINDOW), ALU.subtract)\
                    .then_inc(S["sub_done"], 1)

            def win_unit(UA, sa, UB):
                A, B = UA is not None, UB is not None
                if B:
                    sub(UB, 0)
                    sub(UB, 1)
                if A:
                    for g in range(4):
                        add(UA, g, sa)

            with pool.Fori(0, LAYERS) as l:
                pool.wait_ge(S["wa_in"], 16 * l + 16)
                pool.wait_ge(S["affine"], 8 * l + 16)
                for j in range(4):
                    nc.gpsimd.tensor_tensor(qk_tab[:, j, :], rot[:, j, :], qk_vec[:, j:j + 1].broadcast_to([128, TOKENS]), ALU.mult)\
                        .then_inc(S["tab"], 1)
                win_unit(8 * l, 0, None)
                with pool.Fori(0, 3) as i2:
                    U = 8 * l + 2 * i2
                    win_unit(U + 1, 1, U)
                    win_unit(U + 2, 0, U + 1)
                win_unit(8 * l + 7, 1, 8 * l + 6)
                win_unit(None, None, 8 * l + 7)


def _constants(np):
    p = np.arange(128)
    f = np.float32
    ident = np.eye(128, dtype=f)
    mean_w = np.full((128, 128), 1.0 / 128, f)
    same = (p[:, None] // 32 == p[None, :] // 32) & (p[:, None] % 32 < 8)
    q2_w = np.where(same & (p[None, :] % 32 == 8), f(0.25), f(0))
    k2_w = np.where(same & (p[None, :] % 32 == 9), f(1), f(0))
    head_sel = (p[:, None] // 32 == np.arange(4)[None]).astype(f)
    one8 = (p % 32 == 8).astype(f)[:, None]
    one9 = (p % 32 == 9).astype(f)[:, None]
    eps = np.full((128, 1), LN_EPS, f)
    slide = np.zeros((128, 64), f)
    slide[p, 30 + p // 64] = 1
    k_sel = np.zeros((128, PAIRS, 128), f)
    for c in range(PAIRS):
        for v in range(2):
            k_sel[64 + 32 * (c // 4) + 2 * (c % 4) + v, c, 64 * v:64 * v + 64] = 1
    half = np.arange(0, DH, 2, dtype=f)
    inv_freq = (1.0 / 10000.0 ** (half / DH)).astype(f)
    t = np.arange(TOKENS, dtype=f)
    freqs = t[:, None] * inv_freq[None, :]
    base = (half + 0.4 * DH) / (1.4 * DH)
    power = (t - TOKENS // 2) / (WINDOW // 2)
    scale = (base[None, :].astype(np.float64) ** power[:, None]).astype(f)
    cos, sin = np.cos(freqs.astype(np.float64)), np.sin(freqs.astype(np.float64))
    sign = np.where(p % DH < DH // 2, -1.0, 1.0)[:, None]
    d = p % (DH // 2)
    rot = np.stack([(cos * scale).T[d], sign * (sin * scale).T[d], (cos / scale).T[d], sign * (sin / scale).T[d]], 1)
    c_f32 = np.concatenate([ident, mean_w, q2_w, k2_w, head_sel, one8, one9, eps, np.ones((128, 128), f), slide, k_sel.reshape(128, -1),
                            rot.astype(f).reshape(128, -1)], 1).astype(f)
    i, j = (p % WINDOW)[:, None], np.arange(2 * WINDOW)[None]
    seen = np.where(j < WINDOW, i <= j, j - WINDOW <= i)
    first = seen & ((j >= WINDOW) | (p[:, None] >= WINDOW))
    masks = [np.where(m, 0.0, -1e30) for m in (first, seen)]
    return c_f32, np.concatenate([ident] + masks, 1)


def kernel(**inputs):
    import numpy as np
    import concourse.bacc as bacc
    from concourse import mybir as _mybir
    from concourse.bass_utils import run_bass_kernel_spmd as run

    g = {k: np.asarray(v) for k, v in inputs.items()}
    f = np.float32
    cc = np.ascontiguousarray

    def pad_heads(w):
        w = w.reshape(w.shape[:-1] + (HEADS, 8))
        return np.pad(w, [(0, 0)] * (w.ndim - 1) + [(0, 24)]).reshape(w.shape[:-2] + (HEADS * 32,))

    def columns(v, n):
        return np.pad(v, (0, 128 * n - v.shape[0])).reshape(n, 128).T

    bv = np.broadcast_to(pad_heads(g["L0_attn_bv"])[None], (128, 512))
    wo1 = pad_heads(g["L0_attn_wo"]).reshape(128, 4, 128).transpose(2, 1, 0).reshape(128, 512)
    w_att1 = np.concatenate([pad_heads(g[f"L0_attn_w{n}"].T) for n in "qkv"] + [wo1, bv], 1)
    v_att1 = np.concatenate([columns(pad_heads(g["L0_attn_bq"]), 4), columns(pad_heads(g["L0_attn_bk"]), 4),
                             g["L0_attn_bo"][:, None]], 1)
    swap = (np.arange(DH) + DH // 2) % DH
    qkv = g["L0_ffn_Wqkv"].reshape(LAYERS, DIM, 3, HEADS, DH)
    q, k, v = qkv[:, :, 0], qkv[:, :, 1], qkv[:, :, 2]
    two = lambda s: np.concatenate([s, s], 1)[:, :, None]
    qs, ks = g["L0_ffn_q_scale"], g["L0_ffn_k_scale"]
    w_att = np.concatenate(
        [m.reshape(LAYERS, DIM, INNER) for m in (q, k)]
        + [v.reshape(LAYERS, DIM, PAIRS, 2, DH).transpose(0, 1, 3, 2, 4).reshape(LAYERS, DIM, INNER),
           g["L0_ffn_Wo"].reshape(LAYERS, PAIRS, 128, DIM).transpose(0, 2, 1, 3).reshape(LAYERS, 128, INNER),
           two(qs), two(qs[:, swap]), two(ks), two(ks[:, swap])], 2)
    w2 = np.pad(g["L0_ffn_W2"], ((0, 0), (0, 128 * FFC - FF), (0, 0)))
    b1 = g["L0_ffn_b1"]
    w_ffn = np.stack([np.concatenate(
        [g["L0_ffn_W1"][n], w2[n].reshape(FFC, 128, DIM).transpose(1, 0, 2).reshape(128, FFC * DIM),
         columns(b1[n, :FF], FFC), columns(b1[n, FF:], FFC), g["L0_ffn_b2"][n][:, None],
         g["L0_ffn_ln_g"][n][:, None], g["L0_ffn_ln_b"][n][:, None]], 1) for n in range(LAYERS)])
    c_f32, c_bf16 = _constants(np)
    arrays = {
        "xT": g["L0_attn_x"].reshape(COLS, DIM).T, "cT": g["L0_c"].T, "wmod": g["L0_wmod"],
        "w_att1": w_att1, "v_att1": v_att1, "w_att": w_att, "w_ffn": w_ffn, "c_f32": c_f32,
        "c_bf16": c_bf16.astype(_mybir.dt.np(_mybir.dt.bfloat16)),
    }
    arrays = {n: cc(a) for n, a in arrays.items()}
    nc = bacc.Bacc("TRN2", target_bir_lowering=False, num_devices=1)
    args = [nc.dram_tensor(n, a.shape, _mybir.dt.from_np(a.dtype), kind="ExternalInput").ap() for n, a in arrays.items()]
    out = nc.dram_tensor("out", (DIM, COLS), _mybir.dt.float32, kind="ExternalOutput").ap()
    adaln_kernel(nc, *args, out)
    r = run(nc, [arrays], core_ids=[0])
    return cc(r.results[0]["out"].T).reshape(BATCH, TOKENS, DIM).astype(f)
```

```python
import concourse.bass as bass
from concourse import mybir
from contextlib import ExitStack

BATCH, TOKENS, DIM = 8, 256, 128
COLS = BATCH * TOKENS
TILES = TOKENS // 128
HEADS = 16
LAYERS = 6
DH = 64
PAIRS = HEADS // 2
WINDOW = 32
WINDOWS = TOKENS // WINDOW
INNER = HEADS * DH
FF = int(DIM * 4 * 2 / 3)
FFC = 3
FFP = [128, 128, FF - 256]
WA = 2 * INNER + 4
WF = 2 * FF + FFC * DIM + 2 * FFC + 3
QK_SCALE = 8.0
LN_EPS = 1e-5


def adaln_kernel(nc, xT, cT, wmod, w_att1, v_att1, w_qk, w_att, w_ffn, c_f32, k_sel, c_bf16, out):
    f32 = mybir.dt.float32
    bf16 = mybir.dt.bfloat16
    f32r = mybir.dt.float32r
    ALU = mybir.AluOpType
    ACT = mybir.ActivationFunctionType
    X = mybir.AxisListType.X
    ds = bass.ds

    ctx = ExitStack()
    with ctx:
        def sb(name, shape, dt=f32):
            return ctx.enter_context(nc.sbuf_tensor(name, shape, dt))

        def sem(name):
            return ctx.enter_context(nc.semaphore(name))

        consts = sb("consts", [128, c_f32.shape[1]])
        at = [0]

        def const(n):
            at[0] += n
            return consts[:, at[0] - n:at[0]]

        ident = const(128)
        mean_w = const(128)
        q2_w = const(128)
        k2_w = const(128)
        head_sel = const(4)
        one8 = const(1)
        one9 = const(1)
        eps_col = const(1)
        ones_w = const(128)
        slide = const(64)
        rot = const(4 * TOKENS).rearrange("p (a t) -> p a t", a=4)
        cb = sb("cb", [128, 128 + 2 * 2 * WINDOW], bf16)
        ident_b = cb[:, 0:128]
        mask_b = [cb[:, 128 + 64 * t:192 + 64 * t] for t in range(TILES)]

        wa = sb("wa", [128, WA])
        wv = wa[:, 0:INNER].rearrange("p (v n) -> p v n", v=2)
        wo = wa[:, INNER:2 * INNER].rearrange("p (c n) -> p c n", c=PAIRS)
        qk_vec = wa[:, 2 * INNER:WA]
        wf = sb("wf", [128, WF])
        w1 = wf[:, 0:2 * FF]
        w2 = wf[:, 2 * FF:2 * FF + FFC * DIM].rearrange("p (c n) -> p c n", c=FFC)
        o = 2 * FF + FFC * DIM
        b1a, b1g = wf[:, o:o + FFC], wf[:, o + FFC:o + 2 * FFC]
        b2, ln_g, ln_b = [wf[:, o + 2 * FFC + j:o + 2 * FFC + j + 1] for j in range(3)]

        k_sel_r = sb("k_sel_r", [128, PAIRS * 128], f32r)
        rinv_hi = sb("rinv_hi", [128, TOKENS], f32r)
        rinv_lo = sb("rinv_lo", [128, TOKENS], f32r)

        w_hi, w_lo = [sb(n, [128, 2 * PAIRS, 128], f32r) for n in ("w_hi", "w_lo")]
        x_hi, x_lo = [sb(n, [128, TOKENS], f32r)[:, :] for n in ("x_hi", "x_lo")]

        xo = sb("xo", [128, COLS])
        xi = sb("xi", [128, COLS])

        cs = sb("cs", [128, 4 * BATCH])
        mod = sb("mod", [128, 6, BATCH])
        mod_t = sb("mod_t", [128, 3, BATCH])

        arena_cols = 37600
        arena = sb("arena", [128, arena_cols])

        class Carve:
            def __init__(self):
                self.at = 0

            def __call__(self, *shape):
                n = 1
                for k in shape:
                    n *= k
                v = arena[:, self.at:self.at + n]
                self.at += n
                assert self.at <= arena_cols, self.at
                names = "abcd"[:len(shape)]
                if len(shape) > 1:
                    v = v.rearrange("p (" + " ".join(names) + ") -> p " + " ".join(names),
                                    **dict(zip(names[1:], shape[1:])))
                return v

        c0 = Carve()
        ln_c = c0(COLS)
        ln_q = c0(COLS)
        ln_s = c0(COLS)
        ln_sd, ln_rs = c0(16), c0(16)
        after_ln = c0.at

        c1 = Carve()
        pt1 = c1(8, TILES, TOKENS)
        c1.at = after_ln
        h1 = ln_s
        w1a = c1(3, 512)
        wo1 = c1(4, 128)
        bv1 = c1(512)
        vec1 = c1(9)
        dist = [c1(HEADS, TILES, TOKENS) for _ in range(2)]
        wm = dist[1].rearrange("p h t n -> p (h t n)")[:, 0:6 * DIM]
        dmin = [c1(HEADS * TILES) for _ in range(2)]
        dmin_r = [c1(HEADS * TILES) for _ in range(2)]
        rsum1 = c1(HEADS * TILES)
        rinv1 = c1(4, 4, TILES)
        rinv_w = c1(TILES, 128)
        qk1 = [c1(2, TOKENS) for _ in range(2)]
        sq1 = [c1(2, TOKENS) for _ in range(2)]
        qa1 = [c1(TOKENS) for _ in range(2)]
        ka1 = c1(TOKENS)
        km1 = [c1(4, TOKENS) for _ in range(2)]
        v1 = [c1(TILES, 512) for _ in range(2)]
        hs1 = [c1(TOKENS) for _ in range(2)]
        osb1 = [c1(TOKENS) for _ in range(2)]
        on1 = c1(4, TOKENS)
        tmp1 = c1(TOKENS)

        c2 = Carve()
        c2.at = 0
        qk_tab = c2(4, TOKENS)
        PAD = WINDOW + TOKENS
        xs = [c2(PAD) for _ in range(2)]
        ln_at = c2.at
        raw = c2(2 * PAIRS, TOKENS)
        k0 = c2(PAIRS, TOKENS)
        nrm, rinv = c2(TOKENS), c2(TOKENS)
        rq = [c2(TILES, 2, PAIRS) for _ in range(2)]
        qr = [c2(PAIRS, TOKENS) for _ in range(2)]
        kr = [c2(PAIRS, PAD) for _ in range(2)]
        swp_at = c2.at
        swp = [c2(4, TOKENS) for _ in range(4)]
        w_stage = arena[:, swp_at + 8 * TOKENS:swp_at + 16 * TOKENS]
        vraw = c2(TILES, 2, 512)
        vw_at = c2.at
        vw = [c2(WINDOWS, 512) for _ in range(2)]
        pr = [c2(HEADS, 2 * WINDOW) for _ in range(TILES)]
        mx, rs, rsi = [[c2(HEADS) for _ in range(TILES)] for _ in range(3)]
        pt_at = c2.at
        pt = [c2(PAIRS, 128) for _ in range(TILES)]
        ow = [p.rearrange("p (c v) j -> p c (v j)", v=2) for p in pr]
        ot = c2(PAIRS, TOKENS)
        c3 = Carve()
        c3.at = vw_at + (WINDOWS + 1) * 512
        gl = [c3(512) for _ in range(FFC)]
        c3.at = pt_at
        hh = [[c3(512) for _ in range(FFC)] for _ in range(2)]

        c4 = Carve()
        c4.at = ln_at
        f_c, f_q = c4(COLS), c4(COLS)
        c4.at += PAIRS * TOKENS
        f_sd, f_rs = c4(16), c4(16)
        c4.at = swp_at
        f_s = c4(COLS)

        PS = [ctx.enter_context(nc.psum_tensor(f"ps{i}", [128, 512], f32)) for i in range(8)]
        pb, sbk, tb, ob = PS[0:2], PS[2:4], PS[4:6], PS[6:8]
        wb = PS[0:2] + PS[6:8]

        S = {}

        def sems(*names):
            for n in names:
                S[n] = sem(n)

        sems("in_x", "in_mod", "in_const", "in_sel", "sel_done", "in_w1", "wqk_in", "wv_in", "wo_in", "wf_in", "stored")
        sems("silu_e", "silu_done", "mod_mm", "mod_step", "mod_done")
        sems("mean_mm", "cent", "cent_sq", "var_mm", "sd_done", "rstd_done", "rstd_mm", "normed", "affine", "h_in")
        sems("a_qk", "a_qksb", "a_sq", "a_n2", "a_qa", "a_ka", "a_km", "a_sc", "a_cl", "a_sqrt", "a_vmm", "a_vs",
             "b_exp", "b_ri", "b_rw", "b_t", "b_pd", "b_pa", "b_pv", "b_r", "b_o", "b_on", "b_y", "b_tmp", "b_x")
        sems("w_round", "w_split", "x_round", "x_split")
        sems("pads", "tab", "xs_in", "qk_mm", "raw_done", "cos_q", "cos_k", "swp_in0", "swp_in1", "swp_in2", "swp_in3", "sin_done", "sq_done",
             "add_done", "nrm_mm", "nrm_sd", "nrm_max", "rinv_done", "rinv_split", "rq_mm", "rq_done", "kb_mm", "k_done",
             "v_mm", "v_raw", "v_in0", "v_in1",
             "s_mm", "sc_done", "mx_done", "sub_done", "exp_done", "rs_sum", "rs_done", "tr_mm", "tr_out",
             "pv_mm", "o_done", "y_mm", "x_done")
        sems("f_mean", "f_cent", "f_sq", "f_var", "f_sd", "f_rstd", "f_spread", "f_normed", "f_affine")
        sems("fs_in", "h_mm", "gl_done", "hh_done", "y2_mm", "xf_done")

        block = ctx.enter_context(nc.Block())

        def batch(t, b):
            return t[:, ds(b * TOKENS, TOKENS)]

        def rep(ap, dim, n):
            ap = ap.unsqueeze(dim)
            shape = list(ap.shape)
            shape[dim] = n
            return ap.broadcast_to(shape)

        class Bank:

            def enter(self, last):
                self.last = last

            def take(self, pe, name, value):
                if self.last:
                    pe.wait_ge(S[self.last[0]], self.last[1])
                self.last = (name, value)

        def ln_pe(pe, k, src, ready, bc, bq, brs):
            ready(pe)
            for n in range(4):
                if n >= 2:
                    pe.wait_ge(S["cent"], 4 * k + n - 1)
                pe.matmul(pb[n % 2][:, :], mean_w, src[:, 512 * n:512 * n + 512], start=True, stop=True)\
                    .then_inc(S["mean_mm"], 1)
            for t in range(16):
                if t % 4 == 0:
                    pe.wait_ge(S["cent_sq"], 4 * k + t // 4 + 1)
                i = pe.matmul(ob[0][:, t:t + 1], bq[:, 128 * t:128 * t + 128], mean_w[:, 0:1], start=True, stop=True)
            i.then_inc(S["var_mm"], 1)
            pe.wait_ge(S["rstd_done"], k + 1)
            for n in range(4):
                if n >= 2:
                    pe.wait_ge(S["normed"], 4 * k + n - 1)
                else:
                    pe.wait_ge(S["cent"], 4 * k + 4)
                for t in range(4):
                    i = pe.matmul(pb[n % 2][:, 128 * t:128 * t + 128],
                                  brs[:, 4 * n + t:4 * n + t + 1].broadcast_to([128, 128]), ident,
                                  start=True, stop=True)
                i.then_inc(S["rstd_mm"], 1)

        def ln_dve(dve, k, src, bc, bsd, brs):
            for n in range(4):
                dve.wait_ge(S["mean_mm"], 4 * k + n + 1)
                c = slice(512 * n, 512 * n + 512)
                dve.tensor_tensor(bc[:, c], src[:, c], pb[n % 2][:, :], ALU.subtract).then_inc(S["cent"], 1)
            dve.wait_ge(S["sd_done"], k + 1)
            dve.reciprocal(brs, bsd).then_inc(S["rstd_done"], 1)
            for n in range(4):
                dve.wait_ge(S["rstd_mm"], 4 * k + n + 1)
                c = slice(512 * n, 512 * n + 512)
                dve.tensor_tensor(bc[:, c], bc[:, c], pb[n % 2][:, :], ALU.mult).then_inc(S["normed"], 1)

        def ln_act(act, k, bc, bq, bsd, dst, scale, bias):
            for n in range(4):
                act.wait_ge(S["cent"], 4 * k + n + 1)
                c = slice(512 * n, 512 * n + 512)
                nc.scalar.activation(bq[:, c], bc[:, c], ACT.Square).then_inc(S["cent_sq"], 1)
            act.wait_ge(S["var_mm"], k + 1)
            nc.scalar.activation(bsd, ob[0][:, 0:16], ACT.Sqrt, bias=eps_col).then_inc(S["sd_done"], 1)
            for b in range(BATCH):
                act.wait_ge(S["normed"], 4 * k + b // 2 + 1)
                c = slice(TOKENS * b, TOKENS * b + TOKENS)
                nc.scalar.activation(dst[:, c], bc[:, c], ACT.Identity, scale=scale(b), bias=bias(b))\
                    .then_inc(S["affine"], 1)

        def blk(t, n):
            return t[:, 512 * n:512 * n + 512]

        @block.sync
        def _(sp):
            sp.dma_start(xo[:, :], xT).then_inc(S["in_x"], 16)
            sp.dma_start(consts[:, :], c_f32).then_inc(S["in_const"], 16)
            sp.dma_start(cb[:, :], c_bf16).then_inc(S["in_const"], 16)
            sp.dma_start(arena[:, arena_cols - PAIRS * 128:arena_cols], k_sel).then_inc(S["in_sel"], 16)
            sp.dma_start(cs[:, 0:BATCH], cT).then_inc(S["in_mod"], 16)
            sp.dma_start(wm, wmod).then_inc(S["in_mod"], 16)
            sp.dma_start(arena[:, after_ln:after_ln + 2560], w_att1).then_inc(S["in_w1"], 16)
            sp.dma_start(vec1, v_att1).then_inc(S["in_w1"], 16)
            sp.dma_start(xi[:, :], w_qk[0, :, :]).then_inc(S["wqk_in"], 16)
            sp.dma_start(wa[:, 0:INNER], w_att[0, :, 0:INNER]).then_inc(S["wv_in"], 16)
            sp.dma_start(wa[:, INNER:WA], w_att[0, :, INNER:WA]).then_inc(S["wo_in"], 16)
            sp.dma_start(wf[:, :], w_ffn[0, :, :]).then_inc(S["wf_in"], 16)

            def waits(*pairs):
                pairs = [(name, sp.to_reg(v)) for name, v in (p for p in pairs if p is not True)]
                for name, v in pairs:
                    sp.wait_ge(S[name], v)

            def move_unit(H, slot, first, first_two):
                U = 2 * H + slot
                for g in range(4):
                    waits(("raw_done", 8 * U + 2 * g + 2),
                          first or ("add_done", 4 * U + g - 3))
                    for a in range(4):
                        b = 32 * a
                        e = b + 32 if a % 2 == 0 else b - 32
                        sp.dma_start(swp[g][b:b + 32, :, :], raw[e:e + 32, 4 * g:4 * g + 4, :])\
                            .then_inc(S[f"swp_in{g}"], 16)
                waits(("v_raw", 4 * U + 4),
                      first_two or ("pv_mm", 2 * U - 2))
                for v in range(2):
                    for n in range(4):
                        for role in range(2):
                            m = 1 if n + role == 4 else 2
                            a = 64 * v + 32 - 32 * role
                            dst = vw[slot][a:a + 32, n + role:n + role + 4 * m - 3:4, :]
                            sp.dma_start(dst, vraw[32 * n:32 * n + 32, 0:m, v, :]).then_inc(S[f"v_in{slot}"], 16)

            def move_layer(l, more):
                move_unit(4 * l, 1, False, True)
                with sp.Fori(1, 4) as h:
                    move_unit(4 * l + h, 0, False, False)
                    move_unit(4 * l + h, 1, False, False)
                if more:
                    sp.dma_start(wa[:, 0:INNER], w_att[ds(l + 1, 1), :, 0:INNER].rearrange("a p n -> (a p) n"))\
                        .then_inc(S["wv_in"], 16)
                    sp.wait_ge(S["add_done"], 32 * l + 32)
                    sp.dma_start(w_stage, w_qk[ds(l + 1, 1), :, :].rearrange("a p n -> (a p) n")).then_inc(S["wqk_in"], 16)
                    sp.wait_ge(S["y_mm"], 8 * l + 8)
                    sp.dma_start(wa[:, INNER:WA], w_att[ds(l + 1, 1), :, INNER:WA].rearrange("a p n -> (a p) n"))\
                        .then_inc(S["wo_in"], 16)
                    sp.wait_ge(S["w_split"], 4 * l + 8)
                    move_unit(4 * l + 4, 0, True, True)
                    sp.wait_ge(S["xf_done"], 4 * l + 4)
                    sp.dma_start(wf[:, :], w_ffn[ds(l + 1, 1), :, :].rearrange("a p n -> (a p) n")).then_inc(S["wf_in"], 16)

            move_unit(0, 0, True, True)
            with sp.Fori(0, LAYERS - 1) as l:
                move_layer(l, True)
            move_layer(LAYERS - 1, False)
            sp.wait_ge(S["b_x"], 2 * BATCH + BATCH)
            sp.dma_start(out, xo[:, :]).then_inc(S["stored"], 16)
            sp.wait_ge(S["stored"], 16)

        @block.tensor
        def _(pe):
            pe.wait_ge(S["in_mod"], 32)
            pe.wait_ge(S["silu_done"], 3)
            for j in range(6):
                i = pe.matmul(PS[7][:, BATCH * j:BATCH * j + BATCH], wm[:, DIM * j:DIM * j + DIM],
                              cs[:, 3 * BATCH:4 * BATCH], start=True, stop=True)
            i.then_inc(S["mod_mm"], 1)

            def ready0(pe):
                pe.wait_ge(S["in_x"], 16)
                pe.wait_ge(S["in_const"], 32)
                pe.wait_ge(S["mod_done"], 1)
            ln_pe(pe, 0, xo, ready0, ln_c, ln_q, ln_rs)
            pe.wait_ge(S["affine"], 8)
            pe.wait_ge(S["in_w1"], 32)

            def a_qk(U, cc, slot):
                pe.wait_ge(S["a_qksb"], 8 * U + 2 * cc)
                pe.wait_ge(S["a_vs"], 2 * U)
                for j in range(2):
                    i = pe.matmul(pb[0][:, TOKENS * j:TOKENS * j + TOKENS], w1a[:, j, 128 * cc:128 * cc + 128], hs1[slot],
                                  start=True, stop=True)
                i.then_inc(S["a_qk"], 1)

            def a_n2(U, cc):
                pe.wait_ge(S["a_sq"], 4 * U + cc + 1)
                if not isinstance(U, int) or 4 * U + cc > 0:
                    pe.wait_ge(S["a_qa"], 4 * U + cc)
                    pe.wait_ge(S["a_ka"], 4 * U + cc)
                for j, w in enumerate((q2_w, k2_w)):
                    i = pe.matmul(pb[1][:, TOKENS * j:TOKENS * j + TOKENS], w, sq1[cc % 2][:, j, :],
                                  start=True, stop=True)
                i.then_inc(S["a_n2"], 1)

            def a_scores(U, cc, t):
                if t == 0:
                    pe.wait_ge(S["a_qa"], 4 * U + cc + 1)
                    pe.wait_ge(S["a_km"], 16 * U + 4 * cc + 4)
                for p in range(2):
                    i = 4 * cc + 2 * t + p
                    if not isinstance(U, int) or 32 * U + 2 * i - 2 > 0:
                        pe.wait_ge(S["a_cl"], 32 * U + 2 * i - 2)
                    pe.matmul(sbk[i % 2][:, :], qa1[cc % 2][:, 128 * t:128 * t + 128],
                              km1[cc % 2][:, 2 * p:2 * p + 2, :], start=True, stop=True).then_inc(S["a_sc"], 1)

            def a_v(U, t, slot):
                pe.wait_ge(S["a_qksb"], 8 * U + 8)
                if t:
                    pe.wait_ge(S["a_vs"], 2 * U + 1)
                pe.matmul(pb[0][:, :], hs1[slot][:, 128 * t:128 * t + 128], w1a[:, 2, :],
                          start=True, stop=True).then_inc(S["a_vmm"], 1)

            def b_t(U, cc, half, slot):
                for u in (2 * half, 2 * half + 1):
                    h = 4 * cc + u
                    pe.wait_ge(S["b_exp"], 32 * U + 2 * h + 2)
                    q = S["b_pd"] if h % 2 == 0 else S["b_pa"]
                    if not isinstance(U, int) or 8 * U + h // 2 > 0:
                        pe.wait_ge(q, 8 * U + h // 2)
                    for jt in range(TILES):
                        for t in range(TILES):
                            a = 256 * jt + 128 * t
                            i = pe.transpose(tb[h % 2][:, a:a + 128], dist[slot][:, h, t, 128 * jt:128 * jt + 128],
                                             ident)
                    i.then_inc(S["b_t"], 1)

            def b_pv(U, cc, slot):
                pe.wait_ge(S["b_pd"], 8 * U + 2 * cc + 2)
                pe.wait_ge(S["b_pa"], 8 * U + 2 * cc + 2)
                pe.wait_ge(S["a_vs"], 2 * U + 2)
                if not isinstance(U, int) or 4 * U + cc > 0:
                    pe.wait_ge(S["b_o"], 4 * U + cc)
                for jt in range(TILES):
                    for u in range(4):
                        h = 4 * cc + u
                        i = pe.matmul(ob[0][32 * u:32 * u + 32, 0:TOKENS], v1[slot][:, jt, 32 * h:32 * h + 32],
                                      pt1[:, h % 8, jt, :], start=(jt == 0), stop=(jt == 1),
                                      skip_group_check=True)
                i.then_inc(S["b_pv"], 1)
                pe.wait_ge(S["b_rw"], 4 * U + cc + 1)
                if not isinstance(U, int) or 4 * U + cc > 0:
                    pe.wait_ge(S["b_on"], 4 * U + cc)
                    if cc == 0:
                        pe.wait_ge(S["b_tmp"], U)
                for t in range(TILES):
                    i = pe.matmul(ob[1][:, 128 * t:128 * t + 128], rinv_w[:, t, :], ident,
                                  start=True, stop=True)
                i.then_inc(S["b_r"], 1)

            def b_y(U):
                pe.wait_ge(S["b_on"], 4 * U + 4)
                for cc in range(4):
                    i = pe.matmul(ob[1][:, 0:TOKENS], wo1[:, cc, :], on1[:, cc, :], start=(cc == 0), stop=(cc == 3))
                i.then_inc(S["b_y"], 1)

            def dist_step(A, B, C, sa):
                def some(part, U, *args):
                    if U is not None:
                        part(U, *args)

                if A is not None:
                    pe.wait_ge(S["h_in"], A + 1)
                some(a_qk, A, 0, sa)
                some(b_t, C, 2, 0, sa)
                some(a_qk, A, 1, sa)
                some(a_n2, A, 0)
                some(b_t, C, 2, 1, sa)
                some(b_pv, C, 1, sa)
                some(a_qk, A, 2, sa)
                some(a_n2, A, 1)
                some(a_scores, A, 0, 0)
                some(b_t, C, 3, 0, sa)
                some(a_qk, A, 3, sa)
                some(a_scores, A, 0, 1)
                some(a_n2, A, 2)
                some(b_t, C, 3, 1, sa)
                some(a_scores, A, 1, 0)
                some(b_pv, C, 2, sa)
                some(a_n2, A, 3)
                some(a_scores, A, 1, 1)
                some(b_t, B, 0, 0, 1 - sa)
                some(a_scores, A, 2, 0)
                some(b_t, B, 0, 1, 1 - sa)
                some(b_pv, C, 3, sa)
                some(a_scores, A, 2, 1)
                some(b_y, C)
                some(a_v, A, 0, sa)
                some(b_t, B, 1, 0, 1 - sa)
                some(a_scores, A, 3, 0)
                some(b_t, B, 1, 1, 1 - sa)
                some(a_v, A, 1, sa)
                some(a_scores, A, 3, 1)
                some(b_pv, B, 0, 1 - sa)

            dist_step(0, None, None, 0)
            dist_step(1, 0, None, 1)
            with pe.Fori(0, 3) as i2:
                dist_step(2 * i2 + 2, 2 * i2 + 1, 2 * i2, 0)
                dist_step(2 * i2 + 3, 2 * i2 + 2, 2 * i2 + 1, 1)
            dist_step(None, 7, 6, 0)
            dist_step(None, None, 7, 1)

            def ready1(pe):
                pe.wait_ge(S["b_x"], 2 * BATCH)
            ln_pe(pe, 1, xo, ready1, ln_c, ln_q, ln_rs)

            banks = [Bank() for _ in wb]

            def qk(U, j):
                n = cur["banks"][j % 4]
                banks[n].take(pe, "raw_done", 8 * U + j + 1)
                for c in range(2):
                    o = wb[n][:, TOKENS * c:TOKENS * c + TOKENS]
                    pe.matmul(o, w_hi[:, 2 * j + c, :], x_hi, start=True, stop=False)
                    pe.matmul(o, w_hi[:, 2 * j + c, :], x_lo, start=False, stop=False)
                    i = pe.matmul(o, w_lo[:, 2 * j + c, :], x_hi, start=False, stop=True)
                i.then_inc(S["qk_mm"], 1)

            def values(U, n):
                b = cur["banks"][n]
                banks[b].take(pe, "v_raw", 4 * U + n + 1)
                a = WINDOW + 128 * (n // 2)
                pe.matmul(wb[b][:, :], xs[cur["sa"]][:, a:a + 128], wv[:, n % 2, :], start=True, stop=True)\
                    .then_inc(S["v_mm"], 1)

            def norms(U, c):
                if c == 0:
                    pe.wait_ge(S["sq_done"], 4 * U + 4)
                    banks[0].take(pe, "nrm_sd", U + 1)
                for g in range(4):
                    i = pe.matmul(pb[0][32 * g:32 * g + 32, 0:TOKENS], slide[:, 30 - 2 * c:62 - 2 * c],
                                  raw[:, 4 * g + c, :], start=(c == 0), stop=(c == 3), skip_group_check=True)
                if c == 3:
                    i.then_inc(S["nrm_mm"], 1)

            def q_norms(U):
                pe.wait_ge(S["rinv_done"], U + 1)
                for t in range(TILES):
                    i = pe.transpose(tb[0][:, 128 * t:128 * t + 128], rinv[:, 128 * t:128 * t + 128], ident)
                i.then_inc(S["rq_mm"], 1)

            def k_norms(U, j):
                if j == 0:
                    pe.wait_ge(S["rinv_split"], 2 * U + 2)
                banks[j].take(pe, "k_done", 4 * U + j + 1)
                for c in range(2):
                    sel = k_sel_r[:, 128 * (2 * j + c):128 * (2 * j + c + 1)]
                    o = wb[j][:, TOKENS * c:TOKENS * c + TOKENS]
                    pe.matmul(o, sel, rinv_hi[:, :], start=True, stop=False)
                    i = pe.matmul(o, sel, rinv_lo[:, :], start=False, stop=True)
                i.then_inc(S["kb_mm"], 1)

            def scores(U, t, slot, quarter):
                if quarter == 0:
                    if t == 0:
                        pe.wait_ge(S["add_done"], 4 * U + 4)
                        pe.wait_ge(S["k_done"], 4 * U + 4)
                        pe.wait_ge(S["rq_done"], U + 1)
                        pe.wait_ge(S[f"v_in{slot}"], 256 * cur["HB"] + 256)
                    if t:
                        pe.wait_ge(S["sc_done"], 4 * U + 2)
                    for v in range(2):
                        pe.matmul(sbk[v][:, :], ident_b, rep(mask_b[t], 1, PAIRS), start=True, stop=False,
                                  skip_group_check=True)
                for c in (2 * quarter, 2 * quarter + 1):
                    for w in range(4):
                        W = 4 * t + w
                        for v in range(2):
                            p = slice(64 * v, 64 * v + 64)
                            i = pe.matmul(sbk[v][32 * w:32 * w + 32, 64 * c:64 * c + 64],
                                          qr[slot][p, c, 32 * W:32 * W + 32], kr[slot][p, c, 32 * W:32 * W + 64],
                                          start=False, stop=(c == PAIRS - 1), skip_group_check=True)
                if quarter == 3:
                    i.then_inc(S["s_mm"], 1)

            def transposes(U, t, step, src):
                for r in range(2):
                    if step:
                        pe.wait_ge(S["tr_out"], 8 * U + 2 * step + r - 1)
                    for c in range(4):
                        i = pe.transpose(tb[r][:, 128 * c:128 * c + 128], src[:, 4 * r + c, :], ident)
                    i.then_inc(S["tr_mm"], 1)

            def p_t(U, t):
                pe.wait_ge(S["exp_done"], 2 * U + t + 1)
                if t == 0:
                    pe.wait_ge(S["rq_done"], U + 1)
                transposes(U, t, (0, 1)[t], pr[t].rearrange("p (c v) j -> p c (v j)", v=2))

            def o_t(U, t):
                pe.wait_ge(S["o_done"], 4 * U + 2 * t + 2)
                transposes(U, t, (2, 3)[t], ow[t])

            def pv(U, t, slot, quarter):
                for c in (2 * quarter, 2 * quarter + 1):
                    for w in range(4):
                        for v in range(2):
                            p = slice(64 * v, 64 * v + 64)
                            i = pe.matmul(sbk[v][32 * w:32 * w + 32, 64 * c:64 * c + 64],
                                          pt[t][p, c, 32 * w:32 * w + 32],
                                          vw[slot][p, 4 * t + w, 64 * c:64 * c + 64], start=True, stop=True,
                                          skip_group_check=True)
                if quarter == 3:
                    i.then_inc(S["pv_mm"], 1)

            def out_proj(U):
                banks[3].take(pe, "x_done", U + 1)
                for t in range(TILES):
                    pe.wait_ge(S["tr_out"], 8 * U + 6 + 2 * t)
                    for c in range(PAIRS):
                        i = pe.matmul(wb[3][:, 128 * t:128 * t + 128], wo[:, c, :], ot[:, c, 128 * t:128 * t + 128],
                                      start=(c == 0), stop=(c == PAIRS - 1))
                i.then_inc(S["y_mm"], 1)

            cur = {"banks": (0, 1, 2, 3)}

            def win_unit(HA, sa, HB, sb_):
                A, B = HA is not None, HB is not None
                UA, UB = 2 * HA + sa if A else None, 2 * HB + sb_ if B else None
                cur["sa"], cur["HB"] = sa, HB
                ua = UA if A else UB + 1
                for n in range(4):
                    banks[n].enter(("k_done", 4 * ua - 3 + n) if B else None)
                if A:
                    pe.wait_ge(S["xs_in"], 2 * UA + 2)
                    pe.wait_ge(S["x_split"], UA + 1)
                def some(part, U, *steps):
                    if U is not None:
                        for n in steps:
                            part(U, n)

                def sc(t, *quarters):
                    if B:
                        for n in quarters:
                            scores(UB, t, sb_, n)

                def out(t, *quarters):
                    if B:
                        for n in quarters:
                            pv(UB, t, sb_, n)

                some(values, UA, 0)
                some(qk, UA, 0, 1)
                sc(0, 0, 1)
                some(qk, UA, 2)
                sc(0, 2, 3)
                some(qk, UA, 3)
                sc(1, 0, 1)
                some(qk, UA, 4)
                sc(1, 2, 3)
                some(qk, UA, 5, 6)
                some(p_t, UB, 0)
                some(qk, UA, 7)
                if B:
                    pe.wait_ge(S["tr_out"], 8 * UB + 2)
                    pe.wait_ge(S["sc_done"], 4 * UB + 4)
                some(values, UA, 1)
                out(0, 0, 1)
                some(values, UA, 2)
                out(0, 2, 3)
                some(p_t, UB, 1)
                some(values, UA, 3)
                some(o_t, UB, 0)
                out(1, 0, 1)
                some(norms, UA, 0)
                out(1, 2, 3)
                some(norms, UA, 1, 2, 3)
                if B:
                    o_t(UB, 1)
                    out_proj(UB)
                if A:
                    if B:
                        pe.wait_ge(S["tr_out"], 8 * UB + 8)
                    q_norms(UA)
                    for j in range(4):
                        k_norms(UA, j)

            def layer(l, more):
                with pe.Fori(0, 3) as h:
                    H = 4 * l + h
                    win_unit(H, 1, H, 0)
                    win_unit(H + 1, 0, H, 1)
                win_unit(4 * l + 3, 1, 4 * l + 3, 0)

                def f_mean(n):
                    pe.wait_ge(S["fs_in"], 12 * l + 3 * n + 3)
                    if n >= 2:
                        pe.wait_ge(S["f_normed"], 4 * l + n - 1)
                    else:
                        pe.wait_ge(S["k_done"], 32 * l + 32)
                    pe.matmul(PS[n % 2][:, :], mean_w, blk(f_s, n), start=True, stop=True).then_inc(S["f_mean"], 1)

                def f_var(n):
                    pe.wait_ge(S["f_sq"], 4 * l + n + 1)
                    if n:
                        pe.wait_ge(S["f_sd"], 4 * l + n)
                    for t in range(4):
                        i = pe.matmul(PS[6][:, 4 * n + t:4 * n + t + 1], f_q[:, 512 * n + 128 * t:512 * n + 128 * t + 128],
                                      mean_w[:, 0:1], start=True, stop=True)
                    i.then_inc(S["f_var"], 1)

                def f_spread(n):
                    pe.wait_ge(S["f_rstd"], 4 * l + n + 1)
                    for t in range(4):
                        i = pe.matmul(PS[n % 2][:, 128 * t:128 * t + 128],
                                      f_rs[:, 4 * n + t:4 * n + t + 1].broadcast_to([128, 128]), ident,
                                      start=True, stop=True)
                    i.then_inc(S["f_spread"], 1)

                U = 8 * l + 7
                cur["HB"] = 4 * l + 3
                banks[3].enter(("k_done", 4 * U + 4))
                f_mean(0)
                f_mean(1)
                for n in range(4):
                    scores(U, 0, 1, n)
                    if n == 1:
                        f_var(0)
                f_var(1)
                for n in range(4):
                    scores(U, 1, 1, n)
                    if n == 1:
                        f_spread(0)
                f_spread(1)
                f_mean(2)
                p_t(U, 0)
                p_t(U, 1)
                for n in range(4):
                    pv(U, 0, 1, n)
                f_var(2)
                o_t(U, 0)
                for n in range(4):
                    pv(U, 1, 1, n)
                f_spread(2)
                o_t(U, 1)
                out_proj(U)

                pe.wait_ge(S["wf_in"], 16 * l + 16)

                def hidden(n):
                    pe.wait_ge(S["f_affine"], 4 * l + n + 1)
                    for j in range(FFC):
                        m = FFP[j]
                        k = 3 * n + j
                        if k >= 2:
                            pe.wait_ge(S["hh_done"], 12 * l + k - 1)
                        for g in range(2):
                            c = FF * g + 128 * j
                            pe.matmul(PS[2 + 2 * (k % 2) + g][0:m, :], w1[:, c:c + m], blk(f_q, n),
                                      start=True, stop=True).then_inc(S["h_mm"], 1)

                def down(n):
                    if n >= 2:
                        pe.wait_ge(S["xf_done"], 4 * l + n - 1)
                    if n == 0:
                        pe.wait_ge(S["f_normed"], 4 * l + 3)
                    for j in range(FFC):
                        m = FFP[j]
                        pe.wait_ge(S["hh_done"], 12 * l + 3 * n + j + 1)
                        i = pe.matmul(PS[7 * (n % 2)][:, :], w2[0:m, j, :], hh[n % 2][j][0:m, :],
                                      start=(j == 0), stop=(j == FFC - 1))
                    i.then_inc(S["y2_mm"], 1)

                def project(*js):
                    if more:
                        for j in js:
                            qk(8 * l + 8, j)

                hidden(0)
                f_mean(3)
                hidden(1)
                f_var(3)
                down(0)
                f_spread(3)
                hidden(2)
                if more:
                    cur["sa"], cur["banks"] = 0, (1, 2, 1, 2)
                    banks[0].enter(("xf_done", 4 * l + 3))
                    banks[1].enter(("f_normed", 4 * l + 4))
                    banks[2].enter(("f_sd", 4 * l + 4))
                    banks[3].enter(("xf_done", 4 * l + 4))
                down(1)
                if more:
                    pe.wait_ge(S["wv_in"], 16 * l + 32)
                    pe.wait_ge(S["w_split"], 4 * l + 8)
                    pe.wait_ge(S["xs_in"], 16 * l + 18)
                    pe.wait_ge(S["x_split"], 8 * l + 9)
                project(0, 1)
                project(2, 3)
                hidden(3)
                project(4, 5)
                down(2)
                project(6, 7)
                down(3)
                if more:
                    for n in range(4):
                        values(8 * l + 8, n)
                    for n in range(4):
                        norms(8 * l + 8, n)
                    q_norms(8 * l + 8)
                    for j in range(4):
                        k_norms(8 * l + 8, j)
                    pe.wait_ge(S["wo_in"], 16 * l + 32)
                    cur["banks"] = (0, 1, 2, 3)

            pe.wait_ge(S["wv_in"], 16)
            pe.wait_ge(S["w_split"], 4)
            pe.wait_ge(S["wo_in"], 16)
            pe.wait_ge(S["sel_done"], 1)
            win_unit(0, 0, None, None)
            with pe.Fori(0, LAYERS - 1) as l:
                layer(l, True)
            layer(LAYERS - 1, False)

        @block.vector
        def _(dve):
            chain = [0]

            def step(ins):
                chain[0] += 1
                ins.then_inc(S["mod_step"], 1)
                dve.wait_ge(S["mod_step"], chain[0])

            dve.wait_ge(S["silu_e"], 1)
            c = [cs[:, BATCH * j:BATCH * j + BATCH] for j in range(4)]
            dve.tensor_scalar(c[2], c[1], 1.0, None, ALU.add).then_inc(S["silu_done"], 1)
            dve.wait_ge(S["silu_done"], 1)
            dve.reciprocal(c[1], c[2]).then_inc(S["silu_done"], 1)
            dve.wait_ge(S["silu_done"], 2)
            dve.tensor_tensor(c[3], c[0], c[1], ALU.mult).then_inc(S["silu_done"], 1)
            dve.wait_ge(S["mod_mm"], 1)
            step(nc.vector.tensor_copy(mod[:, :, :], PS[7][:, 0:6 * BATCH].rearrange("p (j b) -> p j b", j=6)))
            for j in (1, 4):
                step(nc.vector.tensor_scalar(mod[:, j, :], mod[:, j, :], 1.0, None, ALU.add))
            for j in (2, 5):
                g = mod[:, j, :]
                step(nc.vector.tensor_scalar(mod_t[:, 0, :], g, 0.0, 2.0, ALU.is_ge, ALU.mult))
                step(nc.vector.tensor_scalar(mod_t[:, 1, :], g, -1.0, None, ALU.mult))
                step(nc.vector.tensor_tensor(mod_t[:, 2, :], mod_t[:, 1, :], g, ALU.max))
                step(nc.vector.tensor_scalar(mod_t[:, 1, :], mod_t[:, 2, :], 0.25, None, ALU.max))
                step(nc.vector.tensor_scalar(mod_t[:, 2, :], mod_t[:, 0, :], -1.0, None, ALU.add))
                step(nc.vector.tensor_tensor(g, mod_t[:, 1, :], mod_t[:, 2, :], ALU.mult))
            nc.vector.tensor_copy(mod_t[:, 0, :], mod[:, 2, :]).then_inc(S["mod_done"], 1)
            dve.wait_ge(S["in_x"], 16)
            ln_dve(dve, 0, xo, ln_c, ln_sd, ln_rs)
            dve.wait_ge(S["in_w1"], 32)
            dve.wait_ge(S["in_const"], 32)

            def a_qksb(U, cc):
                dve.wait_ge(S["a_qk"], 4 * U + cc + 1)
                if not isinstance(U, int) or 4 * U + cc >= 2:
                    dve.wait_ge(S["a_sq"], 4 * U + cc - 1)
                nc.vector.tensor_scalar(qk1[cc % 2][:, 0, :], pb[0][:, 0:TOKENS], vec1[:, cc:cc + 1], -2.0,
                                        ALU.add, ALU.mult).then_inc(S["a_qksb"], 1)
                nc.vector.tensor_scalar(qk1[cc % 2][:, 1, :], pb[0][:, TOKENS:2 * TOKENS], vec1[:, 4 + cc:5 + cc], None,
                                        ALU.add).then_inc(S["a_qksb"], 1)

            def a_aug(U, cc):
                n = 4 * U + cc
                dve.wait_ge(S["a_n2"], n + 1)
                dve.wait_ge(S["a_qksb"], 2 * n + 2)
                if not isinstance(U, int) or n >= 2:
                    dve.wait_ge(S["a_sc"], 4 * n - 4)
                nc.vector.scalar_tensor_tensor(out=qa1[cc % 2], in0=pb[1][:, 0:TOKENS], scalar=one9,
                                               in1=qk1[cc % 2][:, 0, :], op0=ALU.add, op1=ALU.add)\
                    .then_inc(S["a_qa"], 1)
                if not isinstance(U, int) or n > 0:
                    dve.wait_ge(S["a_km"], 4 * n)
                nc.vector.scalar_tensor_tensor(out=ka1, in0=pb[1][:, TOKENS:2 * TOKENS], scalar=one8,
                                               in1=qk1[cc % 2][:, 1, :], op0=ALU.add, op1=ALU.add)\
                    .then_inc(S["a_ka"], 1)
                dve.wait_ge(S["a_ka"], n + 1)
                for u in range(4):
                    nc.vector.tensor_scalar(km1[cc % 2][:, u, :], ka1, head_sel[:, u:u + 1], None, ALU.mult)\
                        .then_inc(S["a_km"], 1)

            def a_clamp(U, cc, t, slot):
                if t == 0 and (not isinstance(U, int) or U >= 2):
                    dve.wait_ge(S["b_t"], 16 * U + 4 * cc - 28)
                for p in range(2):
                    i = 4 * cc + 2 * t + p
                    dve.wait_ge(S["a_sc"], 16 * U + i + 1)
                    for q in range(2):
                        h = 4 * cc + 2 * p + q
                        k = 2 * h + t
                        nc.vector.tensor_scalar(dist[slot][:, h, t, :], sbk[i % 2][:, TOKENS * q:TOKENS * q + TOKENS],
                                                1e-12, None, ALU.max, ALU.min,
                                                accum_out=dmin[slot][:, k:k + 1]).then_inc(S["a_cl"], 1)

            def a_vs(U, t, slot):
                dve.wait_ge(S["a_vmm"], 2 * U + t + 1)
                if not isinstance(U, int) or U >= 2:
                    dve.wait_ge(S["b_pv"], 4 * U - 4)
                nc.vector.tensor_tensor(v1[slot][:, t, :], pb[0][:, :], bv1, ALU.add).then_inc(S["a_vs"], 1)

            def b_pd(U, cc, half):
                for u in (2 * half,):
                    h = 4 * cc + u
                    dve.wait_ge(S["b_t"], 16 * U + h + 1)
                    if u == 0 and (not isinstance(U, int) or 4 * U + cc >= 2):
                        dve.wait_ge(S["b_pv"], 4 * U + cc - 1)
                    nc.vector.tensor_copy(pt1[:, h % 8, :, :], tb[0][:, :].rearrange("p (a t) -> p a t", a=2))\
                        .then_inc(S["b_pd"], 1)

            def b_ri(U, cc):
                dve.wait_ge(S["b_exp"], 32 * U + 8 * cc + 8)
                nc.vector.reciprocal(rinv1[:, cc, :, :], rsum1[:, 8 * cc:8 * cc + 8].rearrange("p (u t) -> p u t", u=4))\
                    .then_inc(S["b_ri"], 1)

            def b_on(U, cc):
                dve.wait_ge(S["b_o"], 4 * U + cc + 1)
                dve.wait_ge(S["b_r"], 4 * U + cc + 1)
                if cc == 0 and not (isinstance(U, int) and U == 0):
                    dve.wait_ge(S["b_y"], U)
                    dve.wait_ge(S["b_x"], 2 * U)
                nc.vector.tensor_tensor(on1[:, cc, :], osb1[cc % 2], ob[1][:, 0:TOKENS], ALU.mult).then_inc(S["b_on"], 1)

            def b_x(U):
                dve.wait_ge(S["b_y"], U + 1)
                nc.vector.tensor_scalar(tmp1, ob[1][:, 0:TOKENS], vec1[:, 8:9], None, ALU.add).then_inc(S["b_tmp"], 1)
                dve.wait_ge(S["b_tmp"], U + 1)
                nc.vector.tensor_tensor(tmp1, tmp1, mod[:, 2, ds(U, 1)].broadcast_to([128, TOKENS]), ALU.mult)\
                    .then_inc(S["b_x"], 1)
                dve.wait_ge(S["b_x"], 2 * U + 1)
                nc.vector.tensor_tensor(batch(xo, U), batch(xo, U), tmp1, ALU.add).then_inc(S["b_x"], 1)

            def dist_step(A, B, C, sa):
                def some(part, U, *args):
                    if U is not None:
                        part(U, *args)

                some(a_qksb, A, 0)
                some(b_ri, C, 2)
                some(b_pd, C, 2, 0)
                some(a_qksb, A, 1)
                some(a_aug, A, 0)
                some(b_pd, C, 2, 1)
                some(b_ri, C, 3)
                some(a_qksb, A, 2)
                some(a_aug, A, 1)
                some(b_on, C, 1)
                some(a_clamp, A, 0, 0, sa)
                some(b_pd, C, 3, 0)
                some(a_qksb, A, 3)
                some(a_clamp, A, 0, 1, sa)
                some(a_aug, A, 2)
                some(b_pd, C, 3, 1)
                some(a_clamp, A, 1, 0, sa)
                some(b_on, C, 2)
                some(a_clamp, A, 1, 1, sa)
                some(a_aug, A, 3)
                some(b_ri, B, 0)
                some(b_pd, B, 0, 0)
                some(a_clamp, A, 2, 0, sa)
                some(b_pd, B, 0, 1)
                some(b_on, C, 3)
                some(a_clamp, A, 2, 1, sa)
                some(b_x, C)
                some(a_vs, A, 0, sa)
                some(b_ri, B, 1)
                some(b_pd, B, 1, 0)
                some(a_clamp, A, 3, 0, sa)
                some(b_pd, B, 1, 1)
                some(a_vs, A, 1, sa)
                some(a_clamp, A, 3, 1, sa)
                some(b_on, B, 0)

            dist_step(0, None, None, 0)
            dist_step(1, 0, None, 1)
            with dve.Fori(0, 3) as i2:
                dist_step(2 * i2 + 2, 2 * i2 + 1, 2 * i2, 0)
                dist_step(2 * i2 + 3, 2 * i2 + 2, 2 * i2 + 1, 1)
            dist_step(None, 7, 6, 0)
            dist_step(None, None, 7, 1)
            dve.wait_ge(S["b_x"], 2 * BATCH)
            ln_dve(dve, 1, xo, ln_c, ln_sd, ln_rs)

            dve.wait_ge(S["affine"], 16)
            for s in range(2):
                for v in range(2):
                    nc.vector.memset(vw[s][64 * v:64 * v + 32, 0, :], 0.0).then_inc(S["pads"], 1)

            def x_rest(U, slot):
                dve.wait_ge(S["x_round"], U + 1)
                nc.vector.tensor_tensor(x_lo, xs[slot][:, WINDOW:PAD], x_hi, ALU.subtract).then_inc(S["x_split"], 1)

            def cos_k(U, g):
                dve.wait_ge(S["raw_done"], 8 * U + 2 * g + 2)
                if not (isinstance(U, int) and U == 0):
                    dve.wait_ge(S["k_done"], 4 * U)
                nc.vector.tensor_tensor(k0[:, 4 * g - 8:4 * g - 4, :], raw[:, 4 * g:4 * g + 4, :],
                                        rep(qk_tab[:, 2, :], 1, 4), ALU.mult).then_inc(S["cos_k"], 1)

            def sin_part(H, slot, g):
                dve.wait_ge(S[f"swp_in{g}"], 128 * H + 64 * slot + 64)
                s = swp[g]
                nc.vector.tensor_tensor(s, s, rep(qk_tab[:, 2 * (g // 2) + 1, :], 1, 4), ALU.mult)\
                    .then_inc(S["sin_done"], 1)

            def norm_inv(U):
                dve.wait_ge(S["nrm_sd"], U + 1)
                nc.vector.tensor_scalar(rinv, nrm, 1e-12, None, ALU.max).then_inc(S["nrm_max"], 1)
                dve.wait_ge(S["nrm_max"], U + 1)
                nc.vector.reciprocal(rinv, rinv).then_inc(S["rinv_done"], 1)
                dve.wait_ge(S["rinv_done"], U + 1)
                nc.vector.tensor_copy(rinv_hi[:, :], rinv).then_inc(S["rinv_split"], 1)
                dve.wait_ge(S["rinv_split"], 2 * U + 1)
                nc.vector.tensor_tensor(rinv_lo[:, :], rinv, rinv_hi[:, :], ALU.subtract).then_inc(S["rinv_split"], 1)

            def q_inv(U, slot):
                dve.wait_ge(S["rq_mm"], U + 1)
                nc.vector.tensor_scalar(rq[slot], tb[0][:, 0:256].rearrange("p (t g n) -> p t g n", t=2, g=4)[:, :, 0:2, 0:8],
                                        QK_SCALE, None, ALU.mult).then_inc(S["rq_done"], 1)

            def k_scale(U, j, slot):
                dve.wait_ge(S["kb_mm"], 4 * U + j + 1)
                dve.wait_ge(S["add_done"], 4 * U + 3 + j // 2)
                nc.vector.tensor_tensor(kr[slot][:, 2 * j:2 * j + 2, WINDOW:PAD], k0[:, 2 * j:2 * j + 2, :],
                                        wb[j][:, :].rearrange("p (c t) -> p c t", c=2), ALU.mult)\
                    .then_inc(S["k_done"], 1)

            def scale_max(U, t, slot):
                dve.wait_ge(S["s_mm"], 2 * U + t + 1)
                p = pr[t].rearrange("p (c v) j -> p c v j", v=2)
                q = rq[slot].rearrange("p t g n -> p t (g n)")[:, t, :].rearrange("p (c v) -> p c v", v=2)
                for v in range(2):
                    nc.vector.tensor_tensor(p[:, :, v, :], sbk[v][:, :].rearrange("p (c j) -> p c j", c=PAIRS),
                                            rep(q[:, :, v], 2, 2 * WINDOW), ALU.mult).then_inc(S["sc_done"], 1)
                dve.wait_ge(S["sc_done"], 4 * U + 2 * t + 2)
                nc.vector.tensor_reduce(mx[t], pr[t], X, ALU.max).then_inc(S["mx_done"], 1)

            def row_sums(U, t):
                dve.wait_ge(S["exp_done"], 2 * U + t + 1)
                nc.vector.tensor_reduce(rs[t], pr[t], X, ALU.add).then_inc(S["rs_sum"], 1)
                dve.wait_ge(S["rs_sum"], 2 * U + t + 1)
                nc.vector.reciprocal(rsi[t], rs[t]).then_inc(S["rs_done"], 1)

            def o_norm(U, t):
                dve.wait_ge(S["pv_mm"], 2 * U + t + 1)
                dve.wait_ge(S["rs_done"], 2 * U + t + 1)
                o4 = ow[t].rearrange("p c (v n) -> p c v n", v=2)
                r3 = rsi[t].rearrange("p (c v) -> p c v", v=2)
                for v in range(2):
                    nc.vector.tensor_tensor(o4[:, :, v, :], sbk[v][:, :].rearrange("p (c n) -> p c n", c=PAIRS),
                                            rep(r3[:, :, v], 2, DH), ALU.mult).then_inc(S["o_done"], 1)

            def residual(U, b):
                dve.wait_ge(S["y_mm"], U + 1)
                nc.vector.tensor_tensor(batch(xi, b), wb[3][:, 0:TOKENS], batch(xi, b), ALU.add).then_inc(S["x_done"], 1)

            def win_unit(HA, sa, HB, sb_, b, more=True):
                A, B = HA is not None, HB is not None
                UA, UB = 2 * HA + sa if A else None, 2 * HB + sb_ if B else None
                pro = not B
                if B:
                    scale_max(UB, 0, sb_)
                    scale_max(UB, 1, sb_)
                if B:
                    row_sums(UB, 0)
                if A:
                    sin_part(HA, sa, 0)
                    cos_k(UA, 2)
                    sin_part(HA, sa, 1)
                if B:
                    row_sums(UB, 1)
                if A:
                    cos_k(UA, 3)
                if B:
                    o_norm(UB, 0)
                if A:
                    sin_part(HA, sa, 2)
                if B:
                    o_norm(UB, 1)
                if A:
                    sin_part(HA, sa, 3)
                    norm_inv(UA)
                if B:
                    residual(UB, b)
                if A:
                    q_inv(UA, sa)
                    if more:
                        x_rest(UA + 1, 1 - sa)
                    for j in range(4):
                        k_scale(UA, j, sa)

            def layer(l, more):
                with dve.Fori(0, 3) as h:
                    H = 4 * l + h
                    win_unit(H, 1, H, 0, 2 * h)
                    win_unit(H + 1, 0, H, 1, 2 * h + 1)
                win_unit(4 * l + 3, 1, 4 * l + 3, 0, 6, False)

                def f_center(n):
                    dve.wait_ge(S["f_mean"], 4 * l + n + 1)
                    nc.vector.tensor_tensor(blk(f_c, n), blk(f_s, n), PS[n % 2][:, :], ALU.subtract)\
                        .then_inc(S["f_cent"], 1)

                def f_recip(n):
                    dve.wait_ge(S["f_sd"], 4 * l + n + 1)
                    nc.vector.reciprocal(f_rs[:, 4 * n:4 * n + 4], f_sd[:, 4 * n:4 * n + 4]).then_inc(S["f_rstd"], 1)

                def f_norm(n):
                    dve.wait_ge(S["f_spread"], 4 * l + n + 1)
                    nc.vector.tensor_tensor(blk(f_c, n), blk(f_c, n), PS[n % 2][:, :], ALU.mult)\
                        .then_inc(S["f_normed"], 1)

                U = 8 * l + 7
                f_center(0)
                f_center(1)
                scale_max(U, 0, 1)
                f_recip(0)
                f_recip(1)
                scale_max(U, 1, 1)
                f_norm(0)
                f_norm(1)
                f_center(2)
                row_sums(U, 0)
                row_sums(U, 1)
                o_norm(U, 0)
                f_recip(2)
                o_norm(U, 1)
                f_norm(2)
                residual(U, 7)

                dve.wait_ge(S["wf_in"], 16 * l + 16)

                def gate(n):
                    for j in range(FFC):
                        m = FFP[j]
                        k = 3 * n + j
                        dve.wait_ge(S["gl_done"], 12 * l + k + 1)
                        dve.wait_ge(S["h_mm"], 24 * l + 2 * k + 1)
                        if n >= 2:
                            dve.wait_ge(S["y2_mm"], 4 * l + n - 1)
                        nc.vector.scalar_tensor_tensor(out=hh[n % 2][j][0:m, :], in0=PS[2 + 2 * (k % 2)][0:m, :],
                                                       scalar=b1a[0:m, j:j + 1], in1=gl[j][0:m, :],
                                                       op0=ALU.add, op1=ALU.mult).then_inc(S["hh_done"], 1)

                def add_down(n):
                    dve.wait_ge(S["y2_mm"], 4 * l + n + 1)
                    nc.vector.scalar_tensor_tensor(out=blk(xi, n), in0=PS[7 * (n % 2)][:, :], scalar=b2, in1=blk(xi, n),
                                                   op0=ALU.add, op1=ALU.add).then_inc(S["xf_done"], 1)

                gate(0)
                f_center(3)
                gate(1)
                f_recip(3)
                add_down(0)
                f_norm(3)
                gate(2)
                if more:
                    x_rest(8 * l + 8, 0)
                add_down(1)
                if more:
                    dve.wait_ge(S["tab"], 4 * l + 8)
                gate(3)
                if more:
                    sin_part(4 * l + 4, 0, 0)
                add_down(2)
                if more:
                    cos_k(8 * l + 8, 2)
                    sin_part(4 * l + 4, 0, 1)
                add_down(3)
                if more:
                    cos_k(8 * l + 8, 3)
                    sin_part(4 * l + 4, 0, 2)
                    sin_part(4 * l + 4, 0, 3)
                    norm_inv(8 * l + 8)
                    q_inv(8 * l + 8, 0)
                    x_rest(8 * l + 9, 1)
                    for j in range(4):
                        k_scale(8 * l + 8, j, 0)

            dve.wait_ge(S["tab"], 4)
            x_rest(0, 0)
            win_unit(0, 0, None, None, None)
            with dve.Fori(0, LAYERS - 1) as l:
                layer(l, True)
            layer(LAYERS - 1, False)
            dve.wait_ge(S["xf_done"], 4 * LAYERS)
            for b in range(BATCH):
                c = slice(TOKENS * b, TOKENS * b + TOKENS)
                nc.vector.scalar_tensor_tensor(out=xo[:, c], in0=xi[:, c], scalar=mod[:, 5, b:b + 1], in1=xo[:, c],
                                               op0=ALU.mult, op1=ALU.add).then_inc(S["b_x"], 1)

        @block.scalar
        def _(act):
            act.wait_ge(S["in_mod"], 32)
            nc.scalar.activation(cs[:, BATCH:2 * BATCH], cs[:, 0:BATCH], ACT.Exp, scale=-1.0).then_inc(S["silu_e"], 1)
            act.wait_ge(S["in_sel"], 16)
            nc.scalar.activation(k_sel_r[:, :], arena[:, arena_cols - PAIRS * 128:arena_cols], ACT.Copy)\
                .then_inc(S["sel_done"], 1)

            def round_weights(l, src):
                act.wait_ge(S["wqk_in"], 16 * l + 16)
                w = src.rearrange("p (c n) -> p c n", n=128)
                for j in range(4):
                    c = slice(4 * j, 4 * j + 4)
                    nc.scalar.activation(w_hi[:, c, :], w[:, c, :], ACT.Copy).then_inc(S["w_round"], 1)

            act.wait_ge(S["in_const"], 32)
            act.wait_ge(S["mod_done"], 1)
            ln_act(act, 0, ln_c, ln_q, ln_sd, h1, lambda b: mod[:, 1, b:b + 1], lambda b: mod[:, 0, b:b + 1])
            act.wait_ge(S["affine"], 8)

            def a_h(U, slot):
                if not isinstance(U, int) or U >= 2:
                    act.wait_ge(S["a_vmm"], 2 * U - 2)
                nc.scalar.activation(hs1[slot], batch(h1, U), ACT.Copy).then_inc(S["h_in"], 1)

            def a_sq(U, cc):
                n = 4 * U + cc
                act.wait_ge(S["a_qksb"], 2 * n + 2)
                if not isinstance(U, int) or n >= 2:
                    act.wait_ge(S["a_n2"], n - 1)
                nc.scalar.activation(sq1[cc % 2], qk1[cc % 2], ACT.Square).then_inc(S["a_sq"], 1)

            def a_sqrt(U, slot, first, last):
                for cc in range(first, last):
                    act.wait_ge(S["a_cl"], 32 * U + 8 * cc + 8)
                    d = dist[slot][:, 4 * cc:4 * cc + 4, :, :]
                    nc.scalar.activation(d, d, ACT.Sqrt).then_inc(S["a_sqrt"], 1)
                if last == 4:
                    nc.scalar.activation(dmin_r[slot], dmin[slot], ACT.Sqrt).then_inc(S["a_sqrt"], 1)

            def b_exp(U, h, slot):
                if h == 0:
                    act.wait_ge(S["a_sqrt"], 5 * U + 5)
                    if not isinstance(U, int) or U > 0:
                        act.wait_ge(S["b_ri"], 4 * U)
                for t in range(TILES):
                    k = 2 * h + t
                    d = dist[slot][:, h, t, :]
                    nc.scalar.activation(d, d, ACT.Exp, scale=-1.0, bias=dmin_r[slot][:, k:k + 1],
                                         accum_out=rsum1[:, k:k + 1]).then_inc(S["b_exp"], 1)

            def b_pa(U, h):
                    act.wait_ge(S["b_t"], 16 * U + h + 1)
                    if h % 4 == 1 and (not isinstance(U, int) or 4 * U + h // 4 >= 2):
                        act.wait_ge(S["b_pv"], 4 * U + h // 4 - 1)
                    nc.scalar.activation(pt1[:, h % 8, :, :], tb[1][:, :].rearrange("p (a t) -> p a t", a=2), ACT.Copy)\
                        .then_inc(S["b_pa"], 1)

            def b_o(U, cc):
                act.wait_ge(S["b_pv"], 4 * U + cc + 1)
                nc.scalar.activation(osb1[cc % 2], ob[0][:, 0:TOKENS], ACT.Copy).then_inc(S["b_o"], 1)

            round_weights(0, xi[:, :])

            def dist_step(A, B, C, sa):
                def some(part, U, *args):
                    if U is not None:
                        part(U, *args)

                def exp(U, *heads):
                    for h in heads:
                        some(b_exp, U, h, sa if h >= 14 else 1 - sa)

                def pa(U, *heads):
                    for h in heads:
                        some(b_pa, U, h)

                if sa == 0:
                    some(a_h, A, 0)
                exp(C, 14, 15)
                some(a_sq, A, 0)
                pa(C, 9)
                some(a_sqrt, B, 1 - sa, 0, 1)
                some(a_sq, A, 1)
                some(a_sqrt, B, 1 - sa, 1, 2)
                pa(C, 11)
                some(a_sq, A, 2)
                some(b_o, C, 1)
                some(a_sqrt, B, 1 - sa, 2, 3)
                pa(C, 13)
                some(a_sq, A, 3)
                some(a_sqrt, B, 1 - sa, 3, 4)
                pa(C, 15)
                exp(B, 0, 1)
                some(b_o, C, 2)
                exp(B, 2, 3, 4)
                pa(B, 1)
                exp(B, 5, 6)
                pa(B, 3)
                some(b_o, C, 3)
                exp(B, 7, 8, 9)
                pa(B, 5)
                exp(B, 10, 11)
                pa(B, 7)
                if sa == 0 and A is not None:
                    a_h(A + 1, 1)
                exp(B, 12)
                some(b_o, B, 0)
                exp(B, 13)

            dist_step(0, None, None, 0)
            dist_step(1, 0, None, 1)
            with act.Fori(0, 3) as i2:
                dist_step(2 * i2 + 2, 2 * i2 + 1, 2 * i2, 0)
                dist_step(2 * i2 + 3, 2 * i2 + 2, 2 * i2 + 1, 1)
            dist_step(None, 7, 6, 0)
            dist_step(None, None, 7, 1)
            act.wait_ge(S["w_split"], 4)
            ln_act(act, 1, ln_c, ln_q, ln_sd, xi, lambda b: mod[:, 4, b:b + 1], lambda b: mod[:, 3, b:b + 1])

            cur = {"banks": (0, 1, 2, 3)}

            def shift_in(U, b, slot, prologue):
                nc.scalar.activation(xs[slot][0:64, WINDOW:PAD], xi[0:64, ds(b * TOKENS, TOKENS)], ACT.Copy)\
                    .then_inc(S["xs_in"], 1)
                nc.scalar.activation(xs[slot][64:128, WINDOW + 1:PAD], xi[64:128, ds(b * TOKENS, TOKENS - 1)], ACT.Copy)\
                    .then_inc(S["xs_in"], 1)

                act.wait_ge(S["xs_in"], 2 * U + 2)
                nc.scalar.activation(x_hi, xs[slot][:, WINDOW:PAD], ACT.Copy).then_inc(S["x_round"], 1)

            def v_out(H, n, slot, prologue):
                U = 2 * H + slot
                act.wait_ge(S["v_mm"], 4 * U + n + 1)
                if n == 0 and not prologue:
                    act.wait_ge(S[f"v_in{1 - slot}"], 256 * H + 256 * slot)
                nc.scalar.activation(vraw[:, n // 2, n % 2, :], wb[cur["banks"][n]][:, :], ACT.Copy).then_inc(S["v_raw"], 1)

            def raw_out(U, j, prologue):
                act.wait_ge(S["qk_mm"], 8 * U + j + 1)
                if j == 0 and not prologue:
                    act.wait_ge(S["nrm_mm"], U)
                nc.scalar.activation(raw[:, 2 * j:2 * j + 2, :],
                                     wb[cur["banks"][j % 4]][:, :].rearrange("p (c t) -> p c t", c=2), ACT.Copy).then_inc(S["raw_done"], 1)

            def squares(H, slot, g):
                act.wait_ge(S["cos_q" if g < 2 else "cos_k"], 2 * (2 * H + slot) + g % 2 + 1)
                act.wait_ge(S[f"swp_in{g}"], 128 * H + 64 * slot + 64)
                r4 = raw[:, 4 * g:4 * g + 4, :]
                nc.scalar.activation(r4, r4, ACT.Square).then_inc(S["sq_done"], 1)

            def norm_sqrt(U):
                act.wait_ge(S["nrm_mm"], U + 1)
                act.wait_ge(S["nrm_max"], U)
                nc.scalar.activation(nrm, pb[0][:, 0:TOKENS], ACT.Sqrt).then_inc(S["nrm_sd"], 1)

            def exps(U, t):
                act.wait_ge(S["sub_done"], 2 * U + t + 1)
                nc.scalar.activation(pr[t], pr[t], ACT.Exp).then_inc(S["exp_done"], 1)

            def tr_out(U, t, step, dst):
                for r in range(2):
                    act.wait_ge(S["tr_mm"], 8 * U + 2 * step + r + 1)
                    nc.scalar.activation(dst[:, 4 * r:4 * r + 4, :], tb[r][:, :].rearrange("p (c t) -> p c t", c=4),
                                         ACT.Copy).then_inc(S["tr_out"], 1)

            def p_out(U, t):
                tr_out(U, t, t, pt[t])

            def o_out(U, t):
                tr_out(U, t, 2 + t, ot[:, :, 128 * t:128 * t + 128])

            def win_unit(HA, sa, HB, sb_, b):
                A, B = HA is not None, HB is not None
                UA, UB = 2 * HA + sa if A else None, 2 * HB + sb_ if B else None
                pro = not B
                if A:
                    shift_in(UA, b, sa, pro)
                    v_out(HA, 0, sa, pro)
                    raw_out(UA, 0, pro)
                    raw_out(UA, 1, pro)
                    raw_out(UA, 2, pro)
                    raw_out(UA, 3, pro)
                    raw_out(UA, 4, pro)
                if B:
                    exps(UB, 0)
                if A:
                    raw_out(UA, 5, pro)
                    raw_out(UA, 6, pro)
                if B:
                    p_out(UB, 0)
                if A:
                    raw_out(UA, 7, pro)
                    v_out(HA, 1, sa, pro)
                if B:
                    exps(UB, 1)
                if A:
                    squares(HA, sa, 0)
                    squares(HA, sa, 1)
                    v_out(HA, 2, sa, pro)
                if B:
                    p_out(UB, 1)
                if A:
                    v_out(HA, 3, sa, pro)
                    squares(HA, sa, 2)
                if B:
                    o_out(UB, 0)
                if A:
                    squares(HA, sa, 3)
                    norm_sqrt(UA)
                if B:
                    o_out(UB, 1)

            act.wait_ge(S["affine"], 16)
            act.wait_ge(S["pads"], 8)
            def layer(l, more):
                with act.Fori(0, 3) as h:
                    H = 4 * l + h
                    win_unit(H, 1, H, 0, 2 * h + 1)
                    win_unit(H + 1, 0, H, 1, 2 * h + 2)
                win_unit(4 * l + 3, 1, 4 * l + 3, 0, 7)

                def f_shift(n):
                    act.wait_ge(S["x_done"], 8 * l + 2 * n + 2)
                    if n == 0:
                        act.wait_ge(S["add_done"], 32 * l + 30)
                    s3 = blk(f_s, n).rearrange("p (b t) -> p b t", b=2)
                    x3 = blk(xi, n).rearrange("p (b t) -> p b t", b=2)
                    nc.scalar.activation(s3[0:64, :, :], x3[0:64, :, :], ACT.Copy).then_inc(S["fs_in"], 1)
                    nc.scalar.activation(s3[64:128, :, 1:TOKENS], x3[64:128, :, 0:TOKENS - 1], ACT.Copy)\
                        .then_inc(S["fs_in"], 1)
                    nc.scalar.activation(s3[64:128, :, 0:1], xs[0][64:128, 0:2].unsqueeze(2), ACT.Copy)\
                        .then_inc(S["fs_in"], 1)

                def f_square(n):
                    act.wait_ge(S["f_cent"], 4 * l + n + 1)
                    nc.scalar.activation(blk(f_q, n), blk(f_c, n), ACT.Square).then_inc(S["f_sq"], 1)

                def f_sqrt(n):
                    act.wait_ge(S["f_var"], 4 * l + n + 1)
                    nc.scalar.activation(f_sd[:, 4 * n:4 * n + 4], PS[6][:, 4 * n:4 * n + 4], ACT.Sqrt, bias=eps_col)\
                        .then_inc(S["f_sd"], 1)

                def f_scale(n):
                    act.wait_ge(S["f_normed"], 4 * l + n + 1)
                    nc.scalar.activation(blk(f_q, n), blk(f_c, n), ACT.Identity, scale=ln_g, bias=ln_b)\
                        .then_inc(S["f_affine"], 1)

                def gelu(n):
                    for j in range(FFC):
                        m = FFP[j]
                        k = 3 * n + j
                        act.wait_ge(S["h_mm"], 24 * l + 2 * k + 2)
                        if n:
                            act.wait_ge(S["hh_done"], 12 * l + k - 2)
                        nc.scalar.activation(gl[j][0:m, :], PS[3 + 2 * (k % 2)][0:m, :], ACT.Gelu, bias=b1g[0:m, j:j + 1])\
                            .then_inc(S["gl_done"], 1)

                U = 8 * l + 7
                f_shift(0)
                f_shift(1)
                f_square(0)
                f_square(1)
                f_shift(2)
                f_sqrt(0)
                f_sqrt(1)
                exps(U, 0)
                exps(U, 1)
                f_square(2)
                p_out(U, 0)
                p_out(U, 1)
                if more:
                    round_weights(l + 1, w_stage)
                act.wait_ge(S["wf_in"], 16 * l + 16)
                f_scale(0)
                f_scale(1)
                f_sqrt(2)
                o_out(U, 0)
                f_scale(2)
                o_out(U, 1)
                f_shift(3)
                gelu(0)
                f_square(3)
                gelu(1)
                f_sqrt(3)
                f_scale(3)
                H = 4 * l + 4

                def raws(*js):
                    if more:
                        for j in js:
                            raw_out(2 * H, j, True)

                if more:
                    cur["banks"] = (1, 2, 1, 2)
                gelu(2)
                if more:
                    act.wait_ge(S["xf_done"], 4 * l + 1)
                    shift_in(2 * H, 0, 0, True)
                raws(0, 1, 2, 3)
                gelu(3)
                raws(4, 5, 6, 7)
                if more:
                    for n in range(4):
                        v_out(H, n, 0, True)
                        squares(H, 0, n)
                    norm_sqrt(2 * H)
                    cur["banks"] = (0, 1, 2, 3)
                    act.wait_ge(S["xf_done"], 4 * l + 4)

            win_unit(0, 0, None, None, 0)
            with act.Fori(0, LAYERS - 1) as l:
                layer(l, True)
            layer(LAYERS - 1, False)

        @block.gpsimd
        def _(pool):
            def split_weights(l, src):
                w = src.rearrange("p (c n) -> p c n", n=128)
                for j in range(4):
                    c = slice(4 * j, 4 * j + 4)
                    pool.wait_ge(S["w_round"], 4 * l + j + 1)
                    nc.gpsimd.tensor_tensor(w_lo[:, c, :], w[:, c, :], w_hi[:, c, :], ALU.subtract)\
                        .then_inc(S["w_split"], 1)

            def b_rw(U, cc):
                pool.wait_ge(S["b_ri"], 4 * U + cc + 1)
                if not isinstance(U, int) or cc:
                    pool.wait_ge(S["b_r"], 4 * U + cc)
                nc.gpsimd.tensor_tensor(rinv_w.rearrange("p t (u n) -> p t u n", u=4),
                                        rep(rinv1[:, cc, :, :].rearrange("p u t -> p t u"), 3, 32),
                                        ones_w.rearrange("p (t u n) -> p t u n", t=1, u=4).broadcast_to([128, TILES, 4, 32]),
                                        ALU.mult).then_inc(S["b_rw"], 1)

            split_weights(0, xi[:, :])
            for cc in range(4):
                b_rw(0, cc)
            with pool.Fori(1, BATCH) as U:
                for cc in range(4):
                    b_rw(U, cc)

            pool.wait_ge(S["affine"], 16)
            for s in range(2):
                nc.gpsimd.memset(xs[s][:, 0:WINDOW + 1], 0.0).then_inc(S["pads"], 1)
                nc.gpsimd.memset(kr[s][:, :, 0:WINDOW], 0.0).then_inc(S["pads"], 1)

            def rotated(g, slot):
                return qr[slot][:, 4 * g:4 * g + 4, :] if g < 2 else k0[:, 4 * g - 8:4 * g - 4, :]

            def cos_q(U, g, slot, prologue):
                pool.wait_ge(S["raw_done"], 8 * U + 2 * g + 2)
                nc.gpsimd.tensor_tensor(rotated(g, slot), raw[:, 4 * g:4 * g + 4, :], rep(qk_tab[:, 0, :], 1, 4),
                                        ALU.mult).then_inc(S["cos_q"], 1)

            def add(U, g, slot):
                pool.wait_ge(S["cos_q" if g < 2 else "cos_k"], 2 * U + g % 2 + 1)
                pool.wait_ge(S["sin_done"], 4 * U + g + 1)
                dst = rotated(g, slot)
                nc.gpsimd.tensor_tensor(dst, dst, swp[g], ALU.add).then_inc(S["add_done"], 1)

            def sub(U, t):
                pool.wait_ge(S["mx_done"], 2 * U + t + 1)
                nc.gpsimd.tensor_tensor(pr[t], pr[t], rep(mx[t], 2, 2 * WINDOW), ALU.subtract)\
                    .then_inc(S["sub_done"], 1)

            def win_unit(UA, sa, UB):
                A, B = UA is not None, UB is not None
                pro = not B
                if B:
                    sub(UB, 0)
                if A:
                    cos_q(UA, 0, sa, pro)
                if B:
                    sub(UB, 1)
                if A:
                    cos_q(UA, 1, sa, pro)
                    for g in range(4):
                        add(UA, g, sa)

            def tables(l):
                pool.wait_ge(S["wo_in"], 16 * l + 16)
                for j in range(4):
                    nc.gpsimd.tensor_tensor(qk_tab[:, j, :], rot[:, j, :], qk_vec[:, j:j + 1].broadcast_to([128, TOKENS]), ALU.mult)\
                        .then_inc(S["tab"], 1)
                pool.wait_ge(S["tab"], 4 * l + 4)

            def layer(l, more):
                with pool.Fori(0, 3) as i2:
                    U = 8 * l + 2 * i2
                    win_unit(U + 1, 1, U)
                    win_unit(U + 2, 0, U + 1)
                win_unit(8 * l + 7, 1, 8 * l + 6)
                win_unit(None, None, 8 * l + 7)
                if more:
                    split_weights(l + 1, w_stage)
                    tables(l + 1)
                    win_unit(8 * l + 8, 0, None)

            tables(0)
            win_unit(0, 0, None)
            with pool.Fori(0, LAYERS - 1) as l:
                layer(l, True)
            layer(LAYERS - 1, False)


def _constants(np):
    p = np.arange(128)
    f = np.float32
    ident = np.eye(128, dtype=f)
    mean_w = np.full((128, 128), 1.0 / 128, f)
    same = (p[:, None] // 32 == p[None, :] // 32) & (p[:, None] % 32 < 8)
    q2_w = np.where(same & (p[None, :] % 32 == 8), f(0.25), f(0))
    k2_w = np.where(same & (p[None, :] % 32 == 9), f(1), f(0))
    head_sel = (p[:, None] // 32 == np.arange(4)[None]).astype(f)
    one8 = (p % 32 == 8).astype(f)[:, None]
    one9 = (p % 32 == 9).astype(f)[:, None]
    eps = np.full((128, 1), LN_EPS, f)
    slide = np.zeros((128, 64), f)
    slide[p, 30 + p // 64] = 1
    k_sel = np.zeros((128, PAIRS, 128), f)
    for c in range(PAIRS):
        for v in range(2):
            k_sel[64 + 32 * (c // 4) + 2 * (c % 4) + v, c, 64 * v:64 * v + 64] = 1
    half = np.arange(0, DH, 2, dtype=f)
    inv_freq = (1.0 / 10000.0 ** (half / DH)).astype(f)
    t = np.arange(TOKENS, dtype=f)
    freqs = t[:, None] * inv_freq[None, :]
    base = (half + 0.4 * DH) / (1.4 * DH)
    power = (t - TOKENS // 2) / (WINDOW // 2)
    scale = (base[None, :].astype(np.float64) ** power[:, None]).astype(f)
    cos, sin = np.cos(freqs.astype(np.float64)), np.sin(freqs.astype(np.float64))
    sign = np.where(p % DH < DH // 2, -1.0, 1.0)[:, None]
    d = p % (DH // 2)
    rot = np.stack([(cos * scale).T[d], sign * (sin * scale).T[d], (cos / scale).T[d], sign * (sin / scale).T[d]], 1)
    c_f32 = np.concatenate([ident, mean_w, q2_w, k2_w, head_sel, one8, one9, eps, np.ones((128, 128), f), slide,
                            rot.astype(f).reshape(128, -1)], 1).astype(f)
    i, j = (p % WINDOW)[:, None], np.arange(2 * WINDOW)[None]
    seen = np.where(j < WINDOW, i <= j, j - WINDOW <= i)
    first = seen & ((j >= WINDOW) | (p[:, None] >= WINDOW))
    masks = [np.where(m, 0.0, -1e30) for m in (first, seen)]
    return c_f32, k_sel.reshape(128, -1), np.concatenate([ident] + masks, 1)


def kernel(**inputs):
    import numpy as np
    import concourse.bacc as bacc
    from concourse import mybir as _mybir
    from concourse.bass_utils import run_bass_kernel_spmd as run

    g = {k: np.asarray(v) for k, v in inputs.items()}
    f = np.float32
    cc = np.ascontiguousarray

    def pad_heads(w):
        w = w.reshape(w.shape[:-1] + (HEADS, 8))
        return np.pad(w, [(0, 0)] * (w.ndim - 1) + [(0, 24)]).reshape(w.shape[:-2] + (HEADS * 32,))

    def columns(v, n):
        return np.pad(v, (0, 128 * n - v.shape[0])).reshape(n, 128).T

    bv = np.broadcast_to(pad_heads(g["L0_attn_bv"])[None], (128, 512))
    wo1 = pad_heads(g["L0_attn_wo"]).reshape(128, 4, 128).transpose(2, 1, 0).reshape(128, 512)
    w_att1 = np.concatenate([pad_heads(g[f"L0_attn_w{n}"].T) for n in "qkv"] + [wo1, bv], 1)
    v_att1 = np.concatenate([columns(pad_heads(g["L0_attn_bq"]), 4), columns(pad_heads(g["L0_attn_bk"]), 4),
                             g["L0_attn_bo"][:, None]], 1)
    swap = (np.arange(DH) + DH // 2) % DH
    qkv = g["L0_ffn_Wqkv"].reshape(LAYERS, DIM, 3, HEADS, DH)
    q, k, v = qkv[:, :, 0], qkv[:, :, 1], qkv[:, :, 2]
    two = lambda s: np.concatenate([s, s], 1)[:, :, None]
    qs, ks = g["L0_ffn_q_scale"], g["L0_ffn_k_scale"]
    w_qk = np.concatenate([m.reshape(LAYERS, DIM, INNER) for m in (q, k)], 2)
    w_att = np.concatenate(
        [v.reshape(LAYERS, DIM, PAIRS, 2, DH).transpose(0, 1, 3, 2, 4).reshape(LAYERS, DIM, INNER),
           g["L0_ffn_Wo"].reshape(LAYERS, PAIRS, 128, DIM).transpose(0, 2, 1, 3).reshape(LAYERS, 128, INNER),
           two(qs), two(qs[:, swap]), two(ks), two(ks[:, swap])], 2)
    w2 = np.pad(g["L0_ffn_W2"], ((0, 0), (0, 128 * FFC - FF), (0, 0)))
    b1 = g["L0_ffn_b1"]
    w_ffn = np.stack([np.concatenate(
        [g["L0_ffn_W1"][n], w2[n].reshape(FFC, 128, DIM).transpose(1, 0, 2).reshape(128, FFC * DIM),
         columns(b1[n, :FF], FFC), columns(b1[n, FF:], FFC), g["L0_ffn_b2"][n][:, None],
         g["L0_ffn_ln_g"][n][:, None], g["L0_ffn_ln_b"][n][:, None]], 1) for n in range(LAYERS)])
    c_f32, k_sel, c_bf16 = _constants(np)
    arrays = {
        "xT": g["L0_attn_x"].reshape(COLS, DIM).T, "cT": g["L0_c"].T, "wmod": g["L0_wmod"],
        "w_att1": w_att1, "v_att1": v_att1, "w_qk": w_qk, "w_att": w_att, "w_ffn": w_ffn, "c_f32": c_f32,
        "k_sel": k_sel,
        "c_bf16": c_bf16.astype(_mybir.dt.np(_mybir.dt.bfloat16)),
    }
    arrays = {n: cc(a) for n, a in arrays.items()}
    nc = bacc.Bacc("TRN2", target_bir_lowering=False, num_devices=1)
    args = [nc.dram_tensor(n, a.shape, _mybir.dt.from_np(a.dtype), kind="ExternalInput").ap() for n, a in arrays.items()]
    out = nc.dram_tensor("out", (DIM, COLS), _mybir.dt.float32, kind="ExternalOutput").ap()
    adaln_kernel(nc, *args, out)
    r = run(nc, [arrays], core_ids=[0])
    return cc(r.results[0]["out"].T).reshape(BATCH, TOKENS, DIM).astype(f)
```
